# Optimizing a Trainium2 kernel written in Bass

```python
import numpy as np
import jax
import jax.numpy as jnp

def _softmax(x, axis=-1):
    return jax.nn.softmax(x, axis=axis)

def _gelu(x):
    return jax.nn.gelu(x, approximate=True)

def _silu(x):
    return jax.nn.silu(x)

def _sigmoid(x):
    return jax.nn.sigmoid(x)

def _layernorm(x, axis=-1, eps=1e-05):
    m = jnp.mean(x, axis=axis, keepdims=True)
    v = jnp.var(x, axis=axis, keepdims=True)
    return (x - m) / jnp.sqrt(v + eps)

def _scatter_add(tgt, idx, src, axis=0):
    return tgt.at[idx].add(src)

def _segment_sum(src, seg, n):
    return jax.ops.segment_sum(src, seg, n)
kernel_name = 'mk_gnn_preln_d2_gnn_r8_1e4cef'

def setup_inputs(seed: int=0):
    np.random.seed(seed)
    _w = jnp.asarray

    def _rec_inputs():
        import jax
        import jax.numpy as jnp
        _gk = jax.random.key(seed)
        x = -8.776e-05 + 1 * jax.random.normal(jax.random.fold_in(_gk, 1), (12500, 256), jnp.float32)
        _s = jax.random.randint(jax.random.fold_in(_gk, 2), (100000,), 0, 12500, jnp.int32)
        _d = jax.random.randint(jax.random.fold_in(_gk, 3), (100000,), 0, 12500, jnp.int32)
        _loop = jnp.arange(12500, dtype=jnp.int32)
        src = jnp.concatenate([_s, _d, _loop])
        dst = jnp.concatenate([_d, _s, _loop])
        _o = jnp.argsort(dst, stable=True)
        src = src[_o]
        dst = dst[_o]
        edge_type_16 = jax.random.randint(jax.random.fold_in(_gk, 12), (212500,), 0, 16, jnp.int32)
        edge_weight1 = jax.random.uniform(jax.random.fold_in(_gk, 13), (212500, 1), jnp.float32, 0.0, 1)
        return (x, src, dst, edge_type_16, edge_weight1)
    x, src, dst, edge_type_16, edge_weight1 = _rec_inputs()

    def _L0_gnn_setup():
        import jax, jax.numpy as jnp
        import numpy as np
        N = 2500
        E = 40000
        HID = 256
        HEADS = 8
        HD = HID // HEADS
        key = jax.random.key(seed)
        ks = jax.random.split(key, 12)
        scale = 1.0 / np.sqrt(HID).astype(np.float32)

        def lin_w(k):
            return jax.random.normal(k, (HID, HID), jnp.float32) * scale

        def lin_b(k):
            return jax.random.normal(k, (HID,), jnp.float32) * 0.01
        return {'h': jax.random.normal(ks[0], (N, HID), jnp.float32), 'Wq': lin_w(ks[1]), 'bq': lin_b(ks[2]), 'Wk': lin_w(ks[3]), 'bk': lin_b(ks[4]), 'Wv': lin_w(ks[5]), 'bv': lin_b(ks[6]), 'Wo': lin_w(ks[7]), 'bo': lin_b(ks[8]), 'rows': jax.random.randint(ks[9], (E,), 0, N), 'cols': jax.random.randint(ks[10], (E,), 0, N)}
    _L0_gnn_all = _L0_gnn_setup()
    _L0_gnn_in = {k: v for k, v in _L0_gnn_all.items() if k in ('Wq', 'bq', 'Wk', 'bk', 'Wv', 'bv', 'Wo', 'bo')}
    del _L0_gnn_all

    def _L1_gnn_setup():
        import jax, jax.numpy as jnp
        import numpy as np
        N_NODES = 6250
        N_EDGES = 100000
        NUM_RELS = 16
        FEAT = 256
        OUT = 256
        key = jax.random.key(seed)
        ks = jax.random.split(key, 7)
        h = jax.random.normal(ks[0], (N_NODES, FEAT), dtype=jnp.float32)
        norm = jax.random.uniform(ks[1], (N_EDGES, 1), dtype=jnp.float32)
        weight = jax.random.normal(ks[2], (NUM_RELS, FEAT, OUT), dtype=jnp.float32) * 0.05
        gate_weight = jax.random.normal(ks[3], (NUM_RELS, FEAT, 1), dtype=jnp.float32) * 0.05
        src = jax.random.randint(ks[4], (N_EDGES,), 0, N_NODES)
        dst = jax.random.randint(ks[5], (N_EDGES,), 0, N_NODES)
        rel_type = jax.random.randint(ks[6], (N_EDGES,), 0, NUM_RELS)
        return {'h': h, 'norm': norm, 'weight': weight, 'gate_weight': gate_weight, 'src': src, 'dst': dst, 'rel_type': rel_type}
    _L1_gnn_all = _L1_gnn_setup()
    _L1_gnn_in = {k: v for k, v in _L1_gnn_all.items() if k in ('weight', 'gate_weight')}
    del _L1_gnn_all
    return {'x': x, 'src': src, 'dst': dst, 'edge_type_16': edge_type_16, 'edge_weight1': edge_weight1, 'L0_gnn_Wq': _L0_gnn_in['Wq'], 'L0_gnn_bq': _L0_gnn_in['bq'], 'L0_gnn_Wk': _L0_gnn_in['Wk'], 'L0_gnn_bk': _L0_gnn_in['bk'], 'L0_gnn_Wv': _L0_gnn_in['Wv'], 'L0_gnn_bv': _L0_gnn_in['bv'], 'L0_gnn_Wo': _L0_gnn_in['Wo'], 'L0_gnn_bo': _L0_gnn_in['bo'], 'L1_gnn_weight': _L1_gnn_in['weight'], 'L1_gnn_gate_weight': _L1_gnn_in['gate_weight']}

def reference(x, src, dst, edge_type_16, edge_weight1, L0_gnn_Wq, L0_gnn_bq, L0_gnn_Wk, L0_gnn_bk, L0_gnn_Wv, L0_gnn_bv, L0_gnn_Wo, L0_gnn_bo, L1_gnn_weight, L1_gnn_gate_weight):
    import jax
    import jax.numpy as jnp

    def _L0_gnn_ref(h, Wq, bq, Wk, bk, Wv, bv, Wo, bo, rows, cols):
        import jax, jax.numpy as jnp
        import numpy as np
        N = 2500
        E = 40000
        HID = 256
        HEADS = 8
        HD = HID // HEADS
        n = h.shape[0]
        scaling = HD ** (-0.5)
        q = (h @ Wq + bq).reshape(n, HD, HEADS) * scaling
        k = (h @ Wk + bk).reshape(n, HD, HEADS)
        v = (h @ Wv + bv).reshape(n, HD, HEADS)
        s = jnp.einsum('edh,edh->eh', q[rows], k[cols])
        m = jax.ops.segment_max(s, rows, num_segments=n)
        e = jnp.exp(s - m[rows])
        z = jax.ops.segment_sum(e, rows, num_segments=n)
        attn = e / z[rows]
        out = jax.ops.segment_sum(attn[:, None, :] * v[cols], rows, num_segments=n)
        return out.reshape(n, -1) @ Wo + bo

    def _L1_gnn_ref(h, norm, weight, gate_weight, src, dst, rel_type):
        import jax, jax.numpy as jnp
        import numpy as np
        N_NODES = 6250
        N_EDGES = 100000
        NUM_RELS = 16
        FEAT = 256
        OUT = 256
        n_nodes = h.shape[0]
        all_msg = jnp.einsum('nf,rfo->rno', h, weight)
        msg = all_msg[rel_type, src] * norm
        all_gate = jnp.einsum('nf,rf->rn', h, gate_weight[..., 0])
        gate = jax.nn.sigmoid(all_gate[rel_type, src])[:, None]
        msg = msg * gate
        agg = jax.ops.segment_sum(msg, dst, num_segments=n_nodes)
        return jax.nn.relu(agg)
    h = jnp.maximum(_layernorm(x, axis=-1), 0.0)
    x = x + _L0_gnn_ref(h, L0_gnn_Wq, L0_gnn_bq, L0_gnn_Wk, L0_gnn_bk, L0_gnn_Wv, L0_gnn_bv, L0_gnn_Wo, L0_gnn_bo, src, dst)
    h = jnp.maximum(_layernorm(x, axis=-1), 0.0)
    x = x + _L1_gnn_ref(h, edge_weight1, L1_gnn_weight, L1_gnn_gate_weight, src, dst, edge_type_16)
    return x

_drawn_inputs = setup_inputs


def setup_inputs(seed=0):
    import zlib

    import numpy as np

    out = dict(_drawn_inputs(seed))
    spreads = {}
    factors = {'L0_gnn_bq': 64.0, 'L0_gnn_bk': 64.0, 'L0_gnn_bv': 5.826, 'L0_gnn_bo': 6.444}
    for name, (base, spread) in spreads.items():
        noise = np.random.default_rng([zlib.crc32(name.encode()), seed]).standard_normal(out[name].shape)
        drawn = base * np.exp(spread * noise) if base else spread * noise
        out[name] = jnp.asarray(drawn.astype(out[name].dtype))
    for name, factor in factors.items():
        out[name] = (out[name] * factor).astype(out[name].dtype)
    return out
```

```python
import concourse.bass as bass
from concourse import mybir
from contextlib import ExitStack

F32 = mybir.dt.float32
BF16 = mybir.dt.bfloat16
I32 = mybir.dt.int32
ALU = mybir.AluOpType
ACT = mybir.ActivationFunctionType
AX = mybir.AxisListType

P = 128
D = 256
C = D // P
H = 8
HD = D // H
R = 16
N = 12500
E = 212500
B = 14
PAIRS = B // 2
RING = 3
BLOCKS = -(-E // (P * B))
BLOCKS += -BLOCKS % RING
FULL = E // (P * B)
TAIL = E - FULL * P * B
TAIL_P, TAIL_B = TAIL // B, TAIL % B
TILES = -(-N // P)
PAD_NODE = 16384
ROW = 2 * D + H
AGG = D + H
EPS = 1e-5
NEG = -3e38
TINY = 1e-30
OHG = [4, 4, 4, 2]


def row0(i):
    return N - P if isinstance(i, int) and i == TILES - 1 else i * P


def wait(eng, sem, value):
    if not isinstance(value, int) or value > 0:
        eng.wait_ge(sem, value)


def step(j, u, by=0):
    k = u + by
    return RING * (j + k // RING) + k % RING, k % RING, j + k // RING


def rounds(eng, body, count, unroll):
    first = unroll - 1
    for j in range(first):
        for u in range(unroll):
            body(j, u)
    with eng.Fori(first, count // unroll - 1) as j:
        for u in range(unroll):
            body(j, u)
    for u in range(unroll):
        body(count // unroll - 1, u)


def build(nc, x, src, dst, etype, eweight, wq, bq, wk, bk, wv, bv, wo, bo, wrel, wgate, out):
    def dram(name, shape, dt):
        return nc.dram_tensor(name, shape, dt, kind="Internal").ap()

    q_rows = dram("q_rows", [N, 3 * D], BF16)
    kv_rows = dram("kv_rows", [N, 2 * D], F32)
    agg_rows = dram("agg_rows", [N, AGG], F32)
    x1_rows = dram("x1_rows", [N, D], F32)
    msg_rows = dram("msg_rows", [N * R, D], F32)
    run_flags = dram("run_flags", [BLOCKS, 2 * P], F32)

    with ExitStack() as whole:
        def keep(name, shape, dt):
            return whole.enter_context(nc.sbuf_tensor(name, shape, dt))

        ident = keep("ident", [P, P], F32)
        iota_row = keep("iota_row", [P, P], F32)
        iota_col = keep("iota_col", [P, 1], F32)
        eps = keep("eps", [P, 1], F32)
        src_idx = keep("src_idx", [P, BLOCKS, B], I32)
        msg_idx = keep("msg_idx", [P, BLOCKS, B], I32)
        weight = keep("weight", [P, BLOCKS, B], F32)
        local = keep("local", [P, BLOCKS, B], F32)
        new_run = keep("new_run", [P, BLOCKS, B], F32)
        not_first = keep("not_first", [P, BLOCKS, B], F32)
        not_last = keep("not_last", [P, BLOCKS, B], F32)
        win_read = keep("win_read", [P, BLOCKS], I32)
        win_write = keep("win_write", [P, BLOCKS], I32)
        is_last = keep("is_last", [P, BLOCKS], F32)
        carry_row = keep("carry_row", [P, BLOCKS], F32)

        project(nc, x, src, dst, etype, eweight, wq, bq, wk, bk, wv, bv, q_rows, kv_rows, run_flags, ident,
                iota_row, iota_col, eps, src_idx, msg_idx, weight, local, new_run, not_first, not_last, win_read,
                win_write, is_last, carry_row)
        attend(nc, q_rows, kv_rows, run_flags, agg_rows, ident, iota_row, src_idx, local, new_run, not_first,
               not_last, win_read, win_write, is_last, carry_row)
        messages(nc, x, agg_rows, wo, bo, wrel, wgate, x1_rows, msg_rows, ident, eps)
        collect(nc, msg_rows, x1_rows, iota_row, msg_idx, weight, local, win_read, win_write, is_last, carry_row,
                out)


def project(nc, x, src, dst, etype, eweight, wq, bq, wk, bk, wv, bv, q_rows, kv_rows, run_flags, ident, iota_row,
            iota_col, eps, src_idx, msg_idx, weight, local, new_run, not_first, not_last, win_read, win_write, is_last,
            carry_row):
    with ExitStack() as ctx:
        def sb(name, shape, dt=F32):
            return ctx.enter_context(nc.sbuf_tensor(name, shape, dt))

        def ps(name, shape, dt=F32):
            return ctx.enter_context(nc.psum_tensor(name, shape, dt))

        def sem(name):
            return ctx.enter_context(nc.semaphore(name))

        w_q = sb("w_q", [P, C, D])
        w_kv = sb("w_kv", [P, C, 2 * D])
        b_q = sb("b_q", [P, D])
        b_kv = sb("b_kv", [P, 2 * D])
        xt = sb("xt", [P, 2, D])
        stats = sb("stats", [P, 2, 6])
        mv = sb("mv", [P, 2, 2])
        std = sb("std", [P, 2])
        rstd = sb("rstd", [P, 2])
        shift = sb("shift", [P, 2])
        ht = sb("ht", [P, 2, D])
        hT = sb("hT", [P, 2, C, P])
        kv = sb("kv", [P, 2, 2 * D])
        qf = sb("qf", [P, 2, D])
        q3 = sb("q3", [P, 2, 3 * D], BF16)
        dst_i = sb("dst_i", [P, BLOCKS, B], I32)
        type_i = sb("type_i", [P, BLOCKS, B], I32)
        dst_f = sb("dst_f", [P, BLOCKS, B])
        lasts = sb("lasts", [P, BLOCKS])
        before = sb("before", [P, BLOCKS])
        flags = sb("flags", [P, BLOCKS, 2])
        sel = sb("sel", [P, 2, P])
        ends = sb("ends", [P, 2, BLOCKS])
        tmp = sb("tmp", [P, BLOCKS])

        hT_ps = [ps(f"hT_ps{i}", [P, C, P]) for i in range(2)]
        kv_ps = [ps(f"kv_ps{i}", [P, 2 * D]) for i in range(2)]
        q_ps = [ps(f"q_ps{i}", [P, D]) for i in range(2)]
        ends_ps = ps("ends_ps", [P, 2, BLOCKS])

        consts = sem("consts")
        weights_in = sem("weights_in")
        bias_scaled = sem("bias_scaled")
        lists_set = sem("lists_set")
        lists_in = sem("lists_in")
        x_in = [sem(f"x_in{i}") for i in range(2)]
        stats_got, mv_got, rstd_got, shift_got = sem("stats_got"), sem("mv_got"), sem("rstd_got"), sem("shift_got")
        std_got = sem("std_got")
        h_got, hT_put, hT_got = sem("h_got"), sem("hT_put"), sem("hT_got")
        mm_done, kv_got, q_got = sem("mm_done"), sem("kv_got"), sem("q_got")
        hi_got, rest_got, mid_got, lo_got = sem("hi_got"), sem("rest_got"), sem("mid_got"), sem("lo_got")
        kv_out = [sem(f"kv_out{i}") for i in range(2)]
        q_out = [sem(f"q_out{i}") for i in range(2)]
        laid = sem("laid")
        ends_put, lasts_got, before_in, flags_got, flags_out = (sem("ends_put"), sem("lasts_got"), sem("before_in"),
                                                                sem("flags_got"), sem("flags_out"))
        block = ctx.enter_context(nc.Block())

        @block.sync
        def _(sp):
            for c in range(C):
                sp.dma_start(w_q[:, c, :], wq[c * P:(c + 1) * P, :]).then_inc(weights_in, 16)
                sp.dma_start(w_kv[:, c, 0:D], wk[c * P:(c + 1) * P, :]).then_inc(weights_in, 16)
                sp.dma_start(w_kv[:, c, D:2 * D], wv[c * P:(c + 1) * P, :]).then_inc(weights_in, 16)
            sp.dma_start(b_q[:, :], bq.partition_broadcast(P)).then_inc(weights_in, 16)
            sp.dma_start(b_kv[:, 0:D], bk.partition_broadcast(P)).then_inc(weights_in, 16)
            sp.dma_start(b_kv[:, D:2 * D], bv.partition_broadcast(P)).then_inc(weights_in, 16)

            def load_x(j, u):
                i = 2 * j + u
                wait(sp, h_got, i - 1)
                sp.nop(nofuse=True)
                sp.dma_start(xt[:, u, :], x[bass.ds(row0(i), P), :]).then_inc(x_in[u], 16)

            rounds(sp, load_x, TILES, 2)

        @block.gpsimd
        def _(pool):
            pool.iota(iota_row[:, :], [[1, P]], base=0, channel_multiplier=0,
                      allow_small_or_imprecise_dtypes=True).then_inc(consts, 1)
            pool.iota(iota_col[:, :], [[0, 1]], base=0, channel_multiplier=1,
                      allow_small_or_imprecise_dtypes=True).then_inc(consts, 1)

            def store(j, u):
                i = 2 * j + u
                if isinstance(i, int) and i == TILES - 1:
                    pool.wait_ge(kv_out[1 - u], 16 * (TILES // 2))
                    pool.wait_ge(q_out[1 - u], 16 * (TILES // 2))
                wait(pool, kv_got, i + 1)
                pool.dma_start(kv_rows[bass.ds(row0(i), P), :], kv[:, u, :]).then_inc(kv_out[u], 16)
                wait(pool, lo_got, i + 1)
                pool.dma_start(q_rows[bass.ds(row0(i), P), :], q3[:, u, :]).then_inc(q_out[u], 16)

            rounds(pool, store, TILES, 2)
            for u in range(2):
                pool.wait_ge(kv_out[u], 16 * (TILES // 2))
                pool.wait_ge(q_out[u], 16 * (TILES // 2))
            pool.wait_ge(lasts_got, 1)
            pool.dma_start(before[1:P, :], lasts[0:P - 1, :]).then_inc(before_in, 16)
            pool.dma_start(before[0:1, 1:BLOCKS], lasts[P - 1:P, 0:BLOCKS - 1]).then_inc(before_in, 16)
            pool.wait_ge(flags_got, 1)
            pool.dma_start(run_flags.rearrange("s (p j) -> p s j", j=2), flags[:, :, :]).then_inc(flags_out, 16)
            pool.wait_ge(flags_out, 16)

        @block.scalar
        def _(act):
            act.wait_ge(lists_set, 4)
            for tile, flat in ((dst_i, dst), (src_idx, src), (type_i, etype), (weight, eweight)):
                blocks = flat[0:FULL * P * B].rearrange("(s p b) -> p s b", p=P, b=B)
                act.dma_start(tile[:, 0:FULL, :], blocks).then_inc(lists_in, 16)
                tail = flat[FULL * P * B:FULL * P * B + TAIL_P * B].rearrange("(p b) -> p b", b=B)
                act.dma_start(tile[0:TAIL_P, FULL, :], tail).then_inc(lists_in, 16)
                if TAIL_B:
                    rest = flat[E - TAIL_B:E].rearrange("(p b) -> p b", p=1)
                    act.dma_start(tile[TAIL_P:TAIL_P + 1, FULL, 0:TAIL_B], rest).then_inc(lists_in, 16)

            def body(j, u):
                i = 2 * j + u
                act.wait_ge(mv_got, i + 1)
                nc.scalar.activation(std[:, u:u + 1], mv[:, u, 1:2], ACT.Sqrt, bias=eps[:, 0:1],
                                     scale=1.0).then_inc(std_got, 1)
                act.wait_ge(shift_got, i + 1)
                wait(act, hT_put, i - 1)
                nc.scalar.activation(ht[:, u, :], xt[:, u, :], ACT.Relu, bias=shift[:, u:u + 1],
                                     scale=rstd[:, u:u + 1]).then_inc(h_got, 1)
                act.wait_ge(hT_put, i + 1)
                wait(act, mm_done, i - 1)
                nc.scalar.copy(hT[:, u, :, :], hT_ps[u][:, :, :]).then_inc(hT_got, 1)
                act.wait_ge(q_got, i + 1)
                if not isinstance(j, int) or j > 0:
                    act.wait_ge(q_out[u], 16 * j)
                nc.scalar.copy(q3[:, u, 0:D], qf[:, u, :]).then_inc(hi_got, 1)
                act.wait_ge(rest_got, i + 1)
                nc.scalar.copy(q3[:, u, D:2 * D], qf[:, u, :]).then_inc(mid_got, 1)

            rounds(act, body, TILES, 2)

        @block.tensor
        def _(pe):
            pe.wait_ge(consts, 4)

            def body(j, u):
                i = 2 * j + u
                pe.wait_ge(h_got, i + 1)
                wait(pe, hT_got, i - 1)
                for c in range(C):
                    last = nc.tensor.transpose(hT_ps[u][:, c, :], ht[:, u, c * P:(c + 1) * P], ident[:, :])
                last.then_inc(hT_put, 1)
                pe.wait_ge(hT_got, i + 1)
                wait(pe, kv_got, i - 1)
                wait(pe, q_got, i - 1)
                if isinstance(i, int) and i == 0:
                    pe.wait_ge(weights_in, 16 * (3 * C + 3))
                for c in range(C):
                    nc.tensor.matmul(kv_ps[u][:, :], hT[:, u, c, :], w_kv[:, c, :], start=c == 0, stop=c == C - 1)
                for c in range(C):
                    last = nc.tensor.matmul(q_ps[u][:, :], hT[:, u, c, :], w_q[:, c, :], start=c == 0,
                                            stop=c == C - 1)
                last.then_inc(mm_done, 1)

            rounds(pe, body, TILES, 2)
            pe.wait_ge(laid, 3)
            nc.tensor.matmul(ends_ps[:, 0, :], sel[:, 0, :], dst_f[:, :, 0], start=True, stop=True)
            nc.tensor.matmul(ends_ps[:, 1, :], sel[:, 1, :], dst_f[:, :, B - 1], start=True,
                             stop=True).then_inc(ends_put, 1)

        @block.vector
        def _(dve):
            nc.vector.memset(eps[:, :], EPS).then_inc(consts, 1)
            nc.vector.memset(dst_i[:, :, :], PAD_NODE).then_inc(lists_set, 1)
            nc.vector.memset(src_idx[:, :, :], 0).then_inc(lists_set, 1)
            nc.vector.memset(type_i[:, :, :], 0).then_inc(lists_set, 1)
            nc.vector.memset(weight[:, :, :], 0.0).then_inc(lists_set, 1)
            dve.wait_ge(consts, 3)
            nc.vector.tensor_scalar(ident[:, :], iota_row[:, :], iota_col[:, 0:1], None,
                                    ALU.is_equal).then_inc(consts, 1)
            dve.wait_ge(weights_in, 16 * (3 * C + 3))
            nc.vector.tensor_scalar(b_q[:, :], b_q[:, :], HD ** -0.5, None, ALU.mult).then_inc(bias_scaled, 1)
            dve.wait_ge(bias_scaled, 1)

            def body(j, u):
                i = 2 * j + u
                dve.wait_ge(x_in[u], 16 * (j + 1))
                nc.vector.bn_stats(stats[:, u, :], xt[:, u, :]).then_inc(stats_got, 1)
                dve.wait_ge(stats_got, i + 1)
                dve.nop(nofuse=True)
                nc.vector.bn_aggr(mv[:, u, :], stats[:, u, :]).then_inc(mv_got, 1)
                dve.wait_ge(mv_got, i + 1)
                wait(dve, h_got, i - 1)
                dve.wait_ge(std_got, i + 1)
                nc.vector.reciprocal(rstd[:, u:u + 1], std[:, u:u + 1]).then_inc(rstd_got, 1)
                dve.wait_ge(rstd_got, i + 1)
                nc.vector.scalar_tensor_tensor(shift[:, u:u + 1], mv[:, u, 0:1], -1.0, rstd[:, u:u + 1], ALU.mult,
                                               ALU.mult).then_inc(shift_got, 1)
                dve.wait_ge(mm_done, i + 1)
                if not isinstance(j, int) or j > 0:
                    dve.wait_ge(kv_out[u], 16 * j)
                nc.vector.scalar_tensor_tensor(qf[:, u, :], q_ps[u][:, :], HD ** -0.5, b_q[:, :], ALU.mult,
                                               ALU.add).then_inc(q_got, 1)
                nc.vector.tensor_tensor(kv[:, u, :], kv_ps[u][:, :], b_kv[:, :], ALU.add).then_inc(kv_got, 1)
                dve.wait_ge(hi_got, i + 1)
                nc.vector.tensor_tensor(qf[:, u, :], qf[:, u, :], q3[:, u, 0:D], ALU.subtract).then_inc(rest_got, 1)
                dve.wait_ge(mid_got, i + 1)
                nc.vector.tensor_tensor(q3[:, u, 2 * D:3 * D], qf[:, u, :], q3[:, u, D:2 * D],
                                        ALU.subtract).then_inc(lo_got, 1)

            rounds(dve, body, TILES, 2)

            done = [0]

            def then(ins):
                done[0] += 1
                ins.then_inc(laid, 1)

            dve.wait_ge(lists_in, 16 * 4 * (3 if TAIL_B else 2))
            then(nc.vector.tensor_copy(dst_f[:, :, :], dst_i[:, :, :]))
            then(nc.vector.tensor_scalar(sel[:, 0, :], iota_col[:, 0:1].broadcast_to([P, P]), 0.0, None,
                                         ALU.is_equal))
            then(nc.vector.tensor_scalar(sel[:, 1, :], iota_col[:, 0:1].broadcast_to([P, P]), float(P - 1), None,
                                         ALU.is_equal))
            dve.wait_ge(laid, done[0])
            nc.vector.memset(before[0:1, 0:1], -1.0)
            nc.vector.tensor_copy(lasts[:, :], dst_f[:, :, B - 1]).then_inc(lasts_got, 1)
            then(nc.vector.scalar_tensor_tensor(msg_idx[:, :, :], src_idx[:, :, :], float(R), type_i[:, :, :],
                                                ALU.mult, ALU.add))
            first = dst_f[:, :, 0:1].broadcast_to([P, BLOCKS, B])
            final = dst_f[:, :, B - 1:B].broadcast_to([P, BLOCKS, B])
            then(nc.vector.tensor_tensor(new_run[:, :, 1:B], dst_f[:, :, 1:B], dst_f[:, :, 0:B - 1], ALU.not_equal))
            then(nc.vector.memset(new_run[:, :, 0:1], 1.0))
            then(nc.vector.tensor_tensor(not_first[:, :, :], dst_f[:, :, :], first, ALU.not_equal))
            then(nc.vector.tensor_tensor(not_last[:, :, :], dst_f[:, :, :], final, ALU.not_equal))
            dve.wait_ge(ends_put, 1)
            then(nc.vector.tensor_copy(ends[:, :, :], ends_ps[:, :, :]))
            dve.wait_ge(laid, done[0])
            for mask in (new_run, not_first, not_last):
                then(nc.vector.tensor_scalar(mask[:, :, :], mask[:, :, :], NEG, None, ALU.mult))
            then(nc.vector.tensor_tensor(local[:, :, :], dst_f[:, :, :],
                                         ends[:, 0, :].unsqueeze(2).broadcast_to([P, BLOCKS, B]), ALU.subtract))
            then(nc.vector.tensor_scalar(win_read[:, :], ends[:, 0, :], iota_col[:, 0:1], float(N - 1), ALU.add,
                                         ALU.min))
            then(nc.vector.tensor_scalar(win_write[:, :], ends[:, 0, :], iota_col[:, 0:1], None, ALU.add))
            then(nc.vector.tensor_tensor(tmp[:, :], ends[:, 1, :], ends[:, 0, :], ALU.subtract))
            then(nc.vector.tensor_tensor(carry_row[:, 1:BLOCKS], ends[:, 1, 0:BLOCKS - 1], ends[:, 0, 1:BLOCKS],
                                         ALU.subtract))
            then(nc.vector.memset(carry_row[:, 0:1], -1.0))
            dve.wait_ge(laid, done[0])
            then(nc.vector.tensor_scalar(is_last[:, :], tmp[:, :], iota_col[:, 0:1], None, ALU.is_equal))
            dve.wait_ge(before_in, 32)
            then(nc.vector.tensor_tensor(flags[:, :, 0], before[:, :], dst_f[:, :, 0], ALU.not_equal))
            then(nc.vector.tensor_tensor(flags[:, :, 1], dst_f[:, :, 0], dst_f[:, :, B - 1], ALU.not_equal))
            dve.wait_ge(laid, done[0])
            nc.vector.tensor_scalar(flags[:, :, :], flags[:, :, :], NEG, None, ALU.mult).then_inc(flags_got, 1)


def attend(nc, q_rows, kv_rows, run_flags, agg_rows, ident, iota_row, src_idx, local, new_run, not_first, not_last,
           win_read, win_write, is_last, carry_row):
    with ExitStack() as ctx:
        def sb(name, shape, dt=F32):
            return ctx.enter_context(nc.sbuf_tensor(name, shape, dt))

        def ps(name, shape, dt=F32):
            return ctx.enter_context(nc.psum_tensor(name, shape, dt))

        def sem(name):
            return ctx.enter_context(nc.semaphore(name))

        kv = [sb(f"kvg{u}", [P, B, ROW]) for u in range(RING)]
        q_win = [sb(f"q_win{u}", [P, 3 * D], BF16) for u in range(RING)]
        onehot = [sb(f"onehot{u}", [P, B, P]) for u in range(RING)]
        index = [sb(f"index{u}", [P, B], I32) for u in range(RING)]
        window = [sb(f"window{u}", [P, 1], I32) for u in range(RING)]
        target = [sb(f"target{u}", [P, 1], I32) for u in range(RING)]
        onehotT = sb("onehotT", [P, B, P], BF16)
        score = sb("score", [P, H, B])
        starts = sb("starts", [P, H * B + 1])
        run_fwd = sb("run_fwd", [P, H * B])
        run_max = sb("run_max", [P, H * B])
        list_flags = [sb(f"list_flags{u}", [H, 2 * P + 1]) for u in range(RING)]
        ends_max = sb("ends_max", [H, P, 2])
        list_fwd = sb("list_fwd", [H, RING, 2 * P])
        list_max = sb("list_max", [H, P, 2])
        seg_max = sb("seg_max", [P, H, B])
        seg_alt = sb("seg_alt", [P, H, B])
        seg_alt2 = sb("seg_alt2", [P, H, B])
        seg_two = sb("seg_two", [P, H, B])
        seg_all = sb("seg_all", [P, H, B])
        arg = sb("arg", [P, H, B])
        drop = sb("drop", [H, 1])
        drop0 = sb("drop0", [H, 1])
        fade = sb("fade", [1, H])
        sums = [sb(f"sums{u}", [P, AGG]) for u in range(RING)]
        last_hot = [sb(f"last_hot{u}", [P, 1]) for u in range(RING)]
        carried = sb("carried", [1, AGG])
        carry_hot = sb("carry_hot", [1, P])

        qe_ps = [ps(f"qe_ps{i}", [P, 2, D]) for i in range(3)]
        oT_ps = [ps(f"oT_ps{i}", [P, 4, P]) for i in range(2)]
        sum_ps = ps("sum_ps", [P, AGG])
        small_ps = ps("small_ps", [P, 512])
        carry_ps = ps("carry_ps", [1, AGG])
        list_ps = small_ps[0:H, 0:2 * P].rearrange("h (j p) -> h j p", j=2)
        back_ps = small_ps[:, 256:272].rearrange("p (j h) -> p j h", j=2)
        drop_ps = small_ps[0:1, 288:288 + H]

        kv_in = [sem(f"kv_in{u}") for u in range(RING)]
        q_in = [sem(f"q_in{u}") for u in range(RING)]
        flags_in = [sem(f"flags_in{u}") for u in range(RING)]
        index_in = [sem(f"index_in{u}") for u in range(RING)]
        target_got, last_hot_got = sem("target_got"), sem("last_hot_got")
        onehot_got, oT_put, oT_got = sem("onehot_got"), sem("oT_put"), sem("oT_got")
        qe_put, prod_got = sem("qe_put"), sem("prod_got")
        starts_set, starts_got = sem("starts_set"), sem("starts_got")
        score_got, fwd_got, run_got = sem("score_got"), sem("fwd_got"), sem("run_got")
        list_put, list_got, lfwd_got, lmax_got = sem("list_put"), sem("list_got"), sem("lfwd_got"), sem("lmax_got")
        drop_a, drop_got = sem("drop_a"), sem("drop_got")
        back_put, alts_got, two_got, all_got, arg_got = (sem("back_put"), sem("alts_got"), sem("two_got"),
                                                         sem("all_got"), sem("arg_got"))
        exp_got, fade_got = sem("exp_got"), sem("fade_got")
        ev_got, agg_done, sums_got = sem("ev_got"), sem("agg_done"), sem("sums_got")
        carry_put, hot_got, carried_got = sem("carry_put"), sem("hot_got"), sem("carried_got")
        agg_out = sem("agg_out")
        block = ctx.enter_context(nc.Block())
        GROUPS = len(OHG)

        @block.sync
        def _(sp):
            def body(j, u):
                i, _, _ = step(j, u)
                wait(sp, kv_in[u], 16 * B * j)
                sp.nop(nofuse=True)
                wait(sp, q_in[u], 16 * j)
                sp.nop(nofuse=True)
                sp.dma_start(index[u][:, :], src_idx[:, :, :].rearrange("p s b -> p (s b)")[:, bass.ds(i * B, B)]
                             ).then_inc(index_in[u], 16)
                sp.dma_start(window[u][:, :], win_read[:, bass.ds(i, 1)]).then_inc(index_in[u], 16)
                wait(sp, lmax_got, i - 2)
                sp.nop(nofuse=True)
                sp.dma_start(list_flags[u][:, 0:2 * P],
                             run_flags[bass.ds(i, 1), :].broadcast_to([H, 2 * P])).then_inc(flags_in[u], 16)

            sp.wait_ge(starts_set, 2 + RING)
            rounds(sp, body, BLOCKS, RING)

        @block.gpsimd
        def _(pool):
            def scatter(i, u):
                wait(pool, sums_got, i + 1)
                wait(pool, target_got, i + 1)
                wait(pool, agg_out, 16 * i)
                pool.nop(nofuse=True)
                pool.indirect_dma_start(
                    out=agg_rows, out_offset=bass.IndirectOffsetOnAxis(ap=target[u][:, 0:1], axis=0),
                    in_=sums[u][:, :], in_offset=None, bounds_check=N - 1, oob_is_err=False).then_inc(agg_out, 16)

            def body(j, u):
                i, _, _ = step(j, u)
                wait(pool, agg_done, i - 2)
                pool.wait_ge(index_in[u], 32 * (j + 1))
                pool.nop(nofuse=True)
                pool.indirect_dma_start(
                    out=q_win[u][:, :], out_offset=None, in_=q_rows,
                    in_offset=bass.IndirectOffsetOnAxis(ap=window[u][:, 0:1], axis=0)).then_inc(q_in[u], 16)
                for t in range(B):
                    pool.indirect_dma_start(
                        out=kv[u][:, t, 0:2 * D], out_offset=None, in_=kv_rows,
                        in_offset=bass.IndirectOffsetOnAxis(ap=index[u][:, t:t + 1],
                                                            axis=0)).then_inc(kv_in[u], 16)
                if not isinstance(i, int) or i >= RING:
                    scatter(i - RING, u)

            rounds(pool, body, BLOCKS, RING)
            for u in range(RING):
                scatter(BLOCKS - RING + u, u)
            pool.wait_ge(agg_out, 16 * BLOCKS)

        @block.vector
        def _(dve):
            nc.vector.memset(starts[:, :], NEG).then_inc(starts_set, 1)
            for u in range(RING):
                nc.vector.memset(list_flags[u][:, :], NEG).then_inc(starts_set, 1)
            nc.vector.memset(list_fwd[:, :, :], 0.0).then_inc(starts_set, 1)
            dve.wait_ge(starts_set, 2 + RING)

            def make_onehot(i, u):
                wait(dve, agg_done, i - 2)
                nc.vector.tensor_tensor(
                    onehot[u][:, :, :], iota_row[:, :].unsqueeze(1).broadcast_to([P, B, P]),
                    local[:, bass.ds(i, 1), :].rearrange("p s b -> p (s b)").unsqueeze(2).broadcast_to([P, B, P]),
                    ALU.is_equal).then_inc(onehot_got, 1)

            def weigh(i, u):
                wait(dve, exp_got, i + 1)
                for half in range(2):
                    rows = slice(half * PAIRS, (half + 1) * PAIRS)
                    v = kv[u][:, rows, D:2 * D].rearrange("p t (d h) -> p t d h", h=H)
                    e = kv[u][:, rows, 2 * D:ROW].unsqueeze(2).broadcast_to([P, PAIRS, HD, H])
                    nc.vector.tensor_tensor(v, v, e, ALU.mult).then_inc(ev_got, 1)

            def carry(i):
                wait(dve, agg_done, i)
                nc.vector.tensor_scalar(carry_hot[0:1, :], iota_row[0:1, :], carry_row[0:1, bass.ds(i, 1)], None,
                                        ALU.is_equal).then_inc(hot_got, 1)
                wait(dve, fade_got, i + 1)
                wait(dve, carry_put, i)
                nc.vector.tensor_tensor(
                    carried[:, :].rearrange("o (d h) -> o d h", h=H), carry_ps[:, :].rearrange("o (d h) -> o d h", h=H),
                    fade[:, :].unsqueeze(1).broadcast_to([1, AGG // H, H]), ALU.mult).then_inc(carried_got, 1)

            def body(j, u):
                i, _, _ = step(j, u)
                first = isinstance(i, int) and i == 0
                last = isinstance(i, int) and i == BLOCKS - 1
                if first:
                    make_onehot(0, 0)
                dve.wait_ge(kv_in[u], 16 * B * (j + 1))
                for pair in range(PAIRS):
                    wait(dve, qe_put, PAIRS * i + pair + 1)
                    k = kv[u][:, 2 * pair:2 * pair + 2, 0:D]
                    nc.vector.tensor_tensor(k, k, qe_ps[(PAIRS * u + pair) % 3][:, :, :], ALU.mult).then_inc(prod_got, 1)
                if not first:
                    ip, up, _ = step(j, u, -1)
                    weigh(ip, up)
                    if not (isinstance(i, int) and i == 1):
                        carry(ip)
                dve.wait_ge(prod_got, PAIRS * (i + 1))
                wait(dve, arg_got, i)
                nc.vector.tensor_reduce(score[:, :, :], kv[u][:, :, 0:D].rearrange("p t (d h) -> p h t d", h=H), AX.X,
                                        ALU.add).then_inc(score_got, 1)
                flat = score[:, :, :].rearrange("p h t -> p (h t)")
                dve.wait_ge(score_got, i + 1)
                dve.wait_ge(starts_got, i + 1)
                wait(dve, run_got, i)
                nc.vector.tensor_tensor_scan(run_fwd[:, :], starts[:, 0:H * B], flat, 0.0, ALU.add,
                                             ALU.max).then_inc(fwd_got, 1)
                dve.wait_ge(fwd_got, i + 1)
                wait(dve, list_put, i)
                nc.vector.tensor_tensor_scan(run_max[:, ::-1], starts[:, 1:H * B + 1][:, ::-1], run_fwd[:, ::-1], 0.0,
                                             ALU.add, ALU.max).then_inc(run_got, 1)
                dve.wait_ge(flags_in[u], 16 * (j + 1))
                dve.wait_ge(list_got, i + 1)
                now, old = u, (u - 1) % RING
                ends = ends_max[:, :, :].rearrange("h p j -> h (p j)")
                lmax = list_max[:, :, :].rearrange("h p j -> h (p j)")
                nc.vector.tensor_tensor_scan(list_fwd[:, now, :], list_flags[u][:, 0:2 * P], ends,
                                             list_fwd[:, old, 2 * P - 1:2 * P], ALU.add, ALU.max).then_inc(lfwd_got, 1)
                dve.wait_ge(lfwd_got, i + 1)
                wait(dve, back_put, i)
                nc.vector.tensor_tensor_scan(lmax[:, ::-1], list_flags[u][:, 1:2 * P + 1][:, ::-1],
                                             list_fwd[:, now, ::-1], 0.0, ALU.add, ALU.max).then_inc(lmax_got, 1)
                dve.wait_ge(lmax_got, i + 1)
                wait(dve, drop_got, i)
                nc.vector.tensor_tensor(drop0[:, :], list_fwd[:, old, 2 * P - 1:2 * P], lmax[:, 0:1],
                                        ALU.subtract).then_inc(drop_a, 1)
                dve.wait_ge(drop_a, i + 1)
                nc.vector.tensor_scalar(drop[:, :], drop0[:, :], 0.0, None, ALU.min).then_inc(drop_got, 1)
                if not last:
                    i2, u2, _ = step(j, u, 1)
                    make_onehot(i2, u2)
                dve.wait_ge(back_put, i + 1)
                wide = [P, H, B]
                mine = bass.ds(i, 1)
                nc.vector.tensor_tensor(seg_alt[:, :, :], back_ps[:, 0, :].unsqueeze(2).broadcast_to(wide),
                                        not_first[:, mine, :].broadcast_to(wide), ALU.add).then_inc(alts_got, 1)
                nc.vector.tensor_tensor(seg_alt2[:, :, :], back_ps[:, 1, :].unsqueeze(2).broadcast_to(wide),
                                        not_last[:, mine, :].broadcast_to(wide), ALU.add).then_inc(alts_got, 1)
                dve.wait_ge(alts_got, 2 * (i + 1))
                nc.vector.tensor_tensor(seg_two[:, :, :], seg_alt[:, :, :], seg_alt2[:, :, :],
                                        ALU.max).then_inc(two_got, 1)
                dve.wait_ge(two_got, i + 1)
                nc.vector.tensor_tensor(seg_all[:, :, :], seg_two[:, :, :],
                                        run_max[:, :].rearrange("p (h t) -> p h t", h=H), ALU.max).then_inc(all_got, 1)
                dve.wait_ge(all_got, i + 1)
                wait(dve, exp_got, i)
                nc.vector.tensor_tensor(arg[:, :, :], score[:, :, :], seg_all[:, :, :],
                                        ALU.subtract).then_inc(arg_got, 1)
                if last:
                    weigh(i, u)
                    carry(i)

            rounds(dve, body, BLOCKS, RING)

        @block.scalar
        def _(act):
            def transposed(i):
                for g, tiles in enumerate(OHG):
                    at = sum(OHG[:g])
                    wait(act, oT_put, GROUPS * i + g + 1)
                    if g == 0:
                        wait(act, qe_put, PAIRS * i)
                    nc.scalar.copy(onehotT[:, at:at + tiles, :],
                                   oT_ps[g % 2][:, 0:tiles, :]).then_inc(oT_got, 1)

            def sum_out(i, u):
                wait(act, agg_done, i + 1)
                wait(act, agg_out, 16 * (i - 2))
                wait(act, carry_put, i - 2)
                nc.scalar.copy(last_hot[u][:, :], is_last[:, bass.ds(i, 1)]).then_inc(last_hot_got, 1)
                nc.scalar.copy(target[u][:, :], win_write[:, bass.ds(i, 1)]).then_inc(target_got, 1)
                nc.scalar.copy(sums[u][:, :], sum_ps[:, :]).then_inc(sums_got, 1)

            def body(j, u):
                i, _, _ = step(j, u)
                first = isinstance(i, int) and i == 0
                last = isinstance(i, int) and i == BLOCKS - 1
                if first:
                    act.wait_ge(starts_set, 2 + RING)
                    transposed(0)
                wait(act, run_got, i)
                nc.scalar.copy(starts[:, 0:H * B].rearrange("p (h t) -> p h t", h=H),
                               new_run[:, bass.ds(i, 1), :].broadcast_to([P, H, B])).then_inc(starts_got, 1)
                act.wait_ge(list_put, i + 1)
                wait(act, lfwd_got, i)
                nc.scalar.copy(ends_max[:, :, :].rearrange("h p j -> h j p"), list_ps).then_inc(list_got, 1)
                if not first:
                    ip, up, _ = step(j, u, -1)
                    sum_out(ip, up)
                if not last:
                    transposed(step(j, u, 1)[0])
                act.wait_ge(arg_got, i + 1)
                nc.scalar.activation(kv[u][:, :, 2 * D:ROW].rearrange("p t h -> p h t"), arg[:, :, :],
                                     ACT.Exp).then_inc(exp_got, 1)
                wait(act, carried_got, i - 1)
                nc.scalar.activation(fade[:, :], drop_ps, ACT.Exp).then_inc(fade_got, 1)
                if last:
                    sum_out(i, u)

            rounds(act, body, BLOCKS, RING)

        @block.tensor
        def _(pe):
            def transpose_onehot(i, u):
                wait(pe, onehot_got, i + 1)
                for g, tiles in enumerate(OHG):
                    wait(pe, oT_got, GROUPS * i + g - 1)
                    for t in range(tiles):
                        last = nc.tensor.transpose(oT_ps[g % 2][:, t, :], onehot[u][:, sum(OHG[:g]) + t, :],
                                                   ident[:, :])
                    last.then_inc(oT_put, 1)

            def expand_q(i, j, u):
                pe.wait_ge(q_in[u], 16 * (j + 1))
                for pair in range(PAIRS):
                    wait(pe, prod_got, PAIRS * i + pair - 2)
                    wait(pe, oT_got, GROUPS * i + (2 * pair + 1) // 4 + 1)
                    for t in range(2):
                        for part in range(3):
                            last = nc.tensor.matmul(qe_ps[(PAIRS * u + pair) % 3][:, t, :], onehotT[:, 2 * pair + t, :],
                                                    q_win[u][:, part * D:(part + 1) * D], start=part == 0,
                                                    stop=part == 2)
                    last.then_inc(qe_put, 1)

            def add_tiles(i, u, tiles):
                for t in tiles:
                    wait(pe, ev_got, 2 * i + t // PAIRS + 1)
                    last = nc.tensor.matmul(sum_ps[:, :], onehot[u][:, t, :], kv[u][:, t, D:ROW], start=t == 0,
                                            stop=False if t < B - 1 else isinstance(i, int) and i == 0)
                return last

            def take_carry(i, u):
                wait(pe, sums_got, i + 1)
                wait(pe, last_hot_got, i + 1)
                wait(pe, carried_got, i)
                nc.tensor.matmul(carry_ps[:, :], last_hot[u][:, :], sums[u][:, :], start=True,
                                 stop=True).then_inc(carry_put, 1)

            def add_carry(i, last):
                if not (isinstance(i, int) and i == 0):
                    wait(pe, hot_got, i)
                    wait(pe, carried_got, i)
                    last = nc.tensor.matmul(sum_ps[:, :], carry_hot[0:1, :], carried[0:1, :], start=False, stop=True)
                last.then_inc(agg_done, 1)

            def list_transposes(i):
                wait(pe, run_got, i + 1)
                wait(pe, list_got, i)
                runs = run_max[:, :].rearrange("p (h t) -> p h t", h=H)
                nc.tensor.transpose(list_ps[:, 0, :], runs[:, :, 0], ident[:, :])
                nc.tensor.transpose(list_ps[:, 1, :], runs[:, :, B - 1], ident[:, :]).then_inc(list_put, 1)

            def back_transposes(i):
                wait(pe, lmax_got, i + 1)
                wait(pe, drop_got, i + 1)
                wait(pe, alts_got, 2 * i)
                wait(pe, fade_got, i)
                pe.nop(nofuse=True)
                nc.tensor.matmul(drop_ps, drop[:, :], ident[0:H, 0:H], start=True, stop=True)
                nc.tensor.transpose(back_ps[:, 0, :], list_max[:, :, 0], ident[0:H, 0:H])
                nc.tensor.transpose(back_ps[:, 1, :], list_max[:, :, 1], ident[0:H, 0:H]).then_inc(back_put, 1)

            def body(j, u):
                i, _, _ = step(j, u)
                first = isinstance(i, int) and i == 0
                last = isinstance(i, int) and i == BLOCKS - 1
                if first:
                    transpose_onehot(0, 0)
                expand_q(i, j, u)
                if first:
                    list_transposes(i)
                    back_transposes(i)
                else:
                    ip, up, _ = step(j, u, -1)
                    if not (isinstance(i, int) and i == 1):
                        i2, u2, _ = step(j, u, -2)
                        take_carry(i2, u2)
                    wait(pe, sums_got, ip)
                    add_tiles(ip, up, range(0, PAIRS))
                    list_transposes(i)
                    add_tiles(ip, up, range(PAIRS, PAIRS + 3))
                    back_transposes(i)
                    add_carry(ip, add_tiles(ip, up, range(PAIRS + 3, B)))
                if last:
                    ip, up, _ = step(j, u, -1)
                    take_carry(ip, up)
                    wait(pe, sums_got, i)
                    add_carry(i, add_tiles(i, u, range(B)))
                else:
                    i2, u2, _ = step(j, u, 1)
                    transpose_onehot(i2, u2)

            rounds(pe, body, BLOCKS, RING)


def messages(nc, x, agg_rows, wo, bo, wrel, wgate, x1_rows, msg_rows, ident, eps):
    with ExitStack() as ctx:
        def sb(name, shape, dt=F32):
            return ctx.enter_context(nc.sbuf_tensor(name, shape, dt))

        def ps(name, shape, dt=F32):
            return ctx.enter_context(nc.psum_tensor(name, shape, dt))

        def sem(name):
            return ctx.enter_context(nc.semaphore(name))

        w_o = sb("w_o", [P, C, D])
        b_o = sb("b_o", [P, D])
        w_rel = sb("w_rel", [P, C, R, D])
        w_gate = sb("w_gate", [P, C, R])
        agg = sb("agg", [P, 2, AGG])
        xt = sb("xt1", [P, 2, D])
        inv = sb("inv", [P, 2, H])
        att = sb("att", [P, D])
        xb = sb("xb", [P, D])
        attT = sb("attT", [P, C, P])
        x1 = sb("x1", [P, 2, D])
        stats = sb("stats1", [P, 6])
        mv = sb("mv1", [P, 2])
        std = sb("std1", [P, 1])
        rstd = sb("rstd1", [P, 1])
        shift = sb("shift1", [P, 1])
        ht = sb("ht1", [P, D])
        hT = sb("hT1", [P, 2, C, P])
        gate = sb("gate", [P, 2, R])
        msg = sb("msg", [P, 2, R, D])

        big_ps = [ps(f"big_ps{i}", [P, 2, D]) for i in range(4)]
        attT_ps = ps("attT_ps", [P, C, P])
        hT_ps = ps("hiddenT_ps", [P, C, P])
        o_ps = ps("o_ps", [P, D])
        gate_ps = ps("gate_ps", [P, R])

        weights_in = sem("weights_in1")
        agg_in = [sem(f"agg_in{u}") for u in range(2)]
        inv0_got, inv_got, att_got, xb_got, x1_got = (sem("inv0_got"), sem("inv_got"), sem("att_got"), sem("xb_got"),
                                                      sem("x1_got"))
        attT_put, attT_got, o_put = sem("attT_put"), sem("attT_got"), sem("o_put")
        stats_got, mv_got, rstd_got, shift_got = sem("stats_got1"), sem("mv_got1"), sem("rstd_got1"), sem("shift_got1")
        std_got = sem("std_got1")
        h_got, hT_put, hT_got = sem("h_got1"), sem("hT_put1"), sem("hT_got1")
        gate_put, gate_got = sem("gate_put"), sem("gate_got")
        big_put, even_got, odd_got = sem("big_put"), sem("even_got"), sem("odd_got")
        x1_out = [sem(f"x1_out{u}") for u in range(2)]
        msg_out = [sem(f"msg_out{u}") for u in range(2)]
        block = ctx.enter_context(nc.Block())
        G = R // 2
        msg_view = msg_rows.rearrange("(n r) d -> n r d", r=R)

        @block.gpsimd
        def _(pool):
            pool.dma_start(w_o[:, :, :], wo.rearrange("(c p) d -> p c d", p=P)).then_inc(weights_in, 16)
            pool.dma_start(b_o[:, :], bo.partition_broadcast(P)).then_inc(weights_in, 16)
            pool.dma_start(w_gate[:, :, :], wgate.rearrange("(c p) r -> p c r", p=P)).then_inc(weights_in, 16)
            for c in range(C):
                pool.dma_start(w_rel[:, c, :, :],
                               wrel[:, c * P:(c + 1) * P, :].rearrange("r p d -> p r d")).then_inc(weights_in, 16)

        @block.sync
        def _(sp):
            def load(j, u):
                i = 2 * j + u
                wait(sp, x1_got, i - 1)
                sp.nop(nofuse=True)
                sp.dma_start(agg[:, u, :], agg_rows[bass.ds(row0(i), P), :]).then_inc(agg_in[u], 16)
                sp.dma_start(xt[:, u, :], x[bass.ds(row0(i), P), :]).then_inc(agg_in[u], 16)
                if not isinstance(i, int) or i > 0:
                    store(i - 1, 1 - u)

            def store(i, u):
                if isinstance(i, int) and i == TILES - 1:
                    sp.wait_ge(x1_out[1 - u], 16 * (TILES // 2))
                    sp.wait_ge(msg_out[1 - u], 32 * (TILES // 2))
                sp.wait_ge(x1_got, i + 1)
                sp.nop(nofuse=True)
                sp.dma_start(x1_rows[bass.ds(row0(i), P), :], x1[:, u, :]).then_inc(x1_out[u], 16)
                for half in range(2):
                    rels = slice(half * R // 2, (half + 1) * R // 2)
                    sp.wait_ge(even_got, G // 2 * i + (half + 1) * G // 4)
                    sp.wait_ge(odd_got, G // 2 * i + (half + 1) * G // 4)
                    sp.nop(nofuse=True)
                    sp.dma_start(msg_view[bass.ds(row0(i), P), rels, :], msg[:, u, rels, :]).then_inc(msg_out[u], 16)

            rounds(sp, load, TILES, 2)
            store(TILES - 1, (TILES - 1) % 2)
            for u in range(2):
                sp.wait_ge(x1_out[u], 16 * (TILES // 2))
                sp.wait_ge(msg_out[u], 32 * (TILES // 2))

        @block.vector
        def _(dve):
            def front(i, j, u):
                def attention():
                    dve.wait_ge(agg_in[u], 32 * (j + 1))
                    if isinstance(i, int) and i == 0:
                        dve.wait_ge(weights_in, 16 * (3 + C))
                    nc.vector.tensor_scalar(inv[:, u, :], agg[:, u, D:AGG], TINY, None, ALU.max).then_inc(inv0_got, 1)
                    dve.wait_ge(inv0_got, i + 1)
                    nc.vector.reciprocal(inv[:, u, :], inv[:, u, :]).then_inc(inv_got, 1)
                    dve.wait_ge(inv_got, i + 1)
                    wait(dve, attT_put, i)
                    nc.vector.tensor_tensor(
                        att[:, :].rearrange("p (d h) -> p d h", h=H), agg[:, u, 0:D].rearrange("p (d h) -> p d h", h=H),
                        inv[:, u, :].unsqueeze(1).broadcast_to([P, HD, H]), ALU.mult).then_inc(att_got, 1)
                    wait(dve, x1_got, i)
                    nc.vector.tensor_tensor(xb[:, :], xt[:, u, :], b_o[:, :], ALU.add).then_inc(xb_got, 1)

                def residual():
                    dve.wait_ge(xb_got, i + 1)
                    dve.wait_ge(o_put, i + 1)
                    wait(dve, h_got, i - 1)
                    if not isinstance(j, int) or j > 0:
                        dve.wait_ge(x1_out[u], 16 * j)
                    nc.vector.tensor_tensor(x1[:, u, :], o_ps[:, :], xb[:, :], ALU.add).then_inc(x1_got, 1)
                    dve.wait_ge(x1_got, i + 1)
                    nc.vector.bn_stats(stats[:, :], x1[:, u, :]).then_inc(stats_got, 1)
                    dve.wait_ge(stats_got, i + 1)
                    dve.nop(nofuse=True)
                    nc.vector.bn_aggr(mv[:, :], stats[:, :]).then_inc(mv_got, 1)
                    dve.wait_ge(mv_got, i + 1)
                    dve.wait_ge(std_got, i + 1)
                    wait(dve, h_got, i)
                    nc.vector.reciprocal(rstd[:, :], std[:, :]).then_inc(rstd_got, 1)
                    dve.wait_ge(rstd_got, i + 1)
                    nc.vector.scalar_tensor_tensor(shift[:, :], mv[:, 0:1], -1.0, rstd[:, :], ALU.mult,
                                                   ALU.mult).then_inc(shift_got, 1)

                return {1: attention, 4: residual}

            def body(j, u):
                i = 2 * j + u
                if isinstance(i, int) and i == 0:
                    for piece in front(0, 0, 0).values():
                        piece()
                ahead = {}
                if not (isinstance(i, int) and i == TILES - 1):
                    ahead = front(i + 1, j if u == 0 else j + 1, 1 - u)
                dve.wait_ge(gate_got, i + 1)
                if not isinstance(j, int) or j > 0:
                    dve.wait_ge(msg_out[u], 32 * j)
                for g in range(G):
                    if g % 2:
                        wait(dve, big_put, G * i + g + 1)
                        for k in range(2):
                            rel = 2 * g + k
                            last = nc.vector.tensor_scalar(msg[:, u, rel, :], big_ps[g % 4][:, k, :],
                                                           gate[:, u, rel:rel + 1], None, ALU.mult)
                        last.then_inc(odd_got, 1)
                    if g in ahead:
                        ahead[g]()

            rounds(dve, body, TILES, 2)

        @block.scalar
        def _(act):
            def front(i, u):
                def attention():
                    act.wait_ge(attT_put, i + 1)
                    wait(act, o_put, i)
                    nc.scalar.copy(attT[:, :, :], attT_ps[:, :, :]).then_inc(attT_got, 1)

                def hidden():
                    act.wait_ge(mv_got, i + 1)
                    nc.scalar.activation(std[:, :], mv[:, 1:2], ACT.Sqrt, bias=eps[:, 0:1],
                                         scale=1.0).then_inc(std_got, 1)
                    act.wait_ge(shift_got, i + 1)
                    wait(act, hT_put, i)
                    nc.scalar.activation(ht[:, :], x1[:, u, :], ACT.Relu, bias=shift[:, 0:1],
                                         scale=rstd[:, 0:1]).then_inc(h_got, 1)

                def hidden_back():
                    act.wait_ge(hT_put, i + 1)
                    wait(act, big_put, G * (i - 1))
                    nc.scalar.copy(hT[:, u, :, :], hT_ps[:, :, :]).then_inc(hT_got, 1)

                return {2: attention, 4: hidden, 6: hidden_back}

            def body(j, u):
                i = 2 * j + u
                if isinstance(i, int) and i == 0:
                    for piece in front(0, 0).values():
                        piece()
                ahead = {} if isinstance(i, int) and i == TILES - 1 else front(i + 1, 1 - u)
                act.wait_ge(gate_put, i + 1)
                wait(act, odd_got, G // 2 * (i - 1))
                nc.scalar.activation(gate[:, u, :], gate_ps[:, :], ACT.Sigmoid).then_inc(gate_got, 1)
                act.wait_ge(gate_got, i + 1)
                if not isinstance(j, int) or j > 0:
                    act.wait_ge(msg_out[u], 32 * j)
                for g in range(G):
                    if g % 2 == 0:
                        wait(act, big_put, G * i + g + 1)
                        for k in range(2):
                            rel = 2 * g + k
                            last = nc.scalar.activation(msg[:, u, rel, :], big_ps[g % 4][:, k, :], ACT.Copy,
                                                        scale=gate[:, u, rel:rel + 1])
                        last.then_inc(even_got, 1)
                    if g in ahead:
                        ahead[g]()

            rounds(act, body, TILES, 2)

        @block.tensor
        def _(pe):
            def front(i):
                def attention():
                    pe.wait_ge(att_got, i + 1)
                    wait(pe, attT_got, i)
                    for c in range(C):
                        last = nc.tensor.transpose(attT_ps[:, c, :], att[:, c * P:(c + 1) * P], ident[:, :])
                    last.then_inc(attT_put, 1)

                def output():
                    pe.wait_ge(attT_got, i + 1)
                    wait(pe, x1_got, i)
                    for c in range(C):
                        last = nc.tensor.matmul(o_ps[:, :], attT[:, c, :], w_o[:, c, :], start=c == 0, stop=c == C - 1)
                    last.then_inc(o_put, 1)

                def hidden():
                    pe.wait_ge(h_got, i + 1)
                    wait(pe, hT_got, i)
                    for c in range(C):
                        last = nc.tensor.transpose(hT_ps[:, c, :], ht[:, c * P:(c + 1) * P], ident[:, :])
                    last.then_inc(hT_put, 1)

                return {2: attention, 3: output, 6: hidden}

            def body(j, u):
                i = 2 * j + u
                if isinstance(i, int) and i == 0:
                    pe.wait_ge(weights_in, 16 * (3 + C))
                    for piece in front(0).values():
                        piece()
                ahead = {} if isinstance(i, int) and i == TILES - 1 else front(i + 1)
                pe.wait_ge(hT_got, i + 1)
                wait(pe, gate_got, i)
                for c in range(C):
                    last = nc.tensor.matmul(gate_ps[:, :], hT[:, u, c, :], w_gate[:, c, :], start=c == 0,
                                            stop=c == C - 1)
                last.then_inc(gate_put, 1)
                for g in range(G):
                    wait(pe, odd_got if g % 2 else even_got, G // 2 * i + g // 2 - 1)
                    for c in range(C):
                        last = nc.tensor.matmul(big_ps[g % 4][:, :, :], hT[:, u, c, :], w_rel[:, c, 2 * g:2 * g + 2, :],
                                                start=c == 0, stop=c == C - 1)
                    last.then_inc(big_put, 1)
                    if g in ahead:
                        ahead[g]()

            rounds(pe, body, TILES, 2)


def collect(nc, msg_rows, x1_rows, iota_row, msg_idx, weight, local, win_read, win_write, is_last, carry_row, out):
    with ExitStack() as ctx:
        def sb(name, shape, dt=F32):
            return ctx.enter_context(nc.sbuf_tensor(name, shape, dt))

        def sem(name):
            return ctx.enter_context(nc.semaphore(name))

        msg = [sb(f"msg_in{u}", [P, B, D]) for u in range(RING)]
        x1 = [sb(f"x1_in{u}", [P, D]) for u in range(RING)]
        index = [sb(f"index_c{u}", [P, B], I32) for u in range(RING)]
        window = [sb(f"window_c{u}", [P, 1], I32) for u in range(RING)]
        target = [sb(f"target_c{u}", [P, 1], I32) for u in range(RING)]
        hot = [sb(f"hot{u}", [P, B, P]) for u in range(RING)]
        onward = [sb(f"onward{u}", [P, P]) for u in range(RING)]
        sums = [sb(f"sums_c{u}", [P, D]) for u in range(RING)]
        result = [sb(f"result{u}", [P, D]) for u in range(RING)]
        sum_ps = [ctx.enter_context(nc.psum_tensor(f"sum_ps_c{u}", [P, D], F32)) for u in range(RING)]

        msg_in_ = [sem(f"msg_landed{u}") for u in range(RING)]
        x1_in = [sem(f"x1_landed{u}") for u in range(RING)]
        index_in = [sem(f"index_in_c{u}") for u in range(RING)]
        hot_got, onward_got, target_got = sem("hot_got_c"), sem("onward_got"), sem("target_got_c")
        sum_done, sums_got, result_got, out_done = sem("sum_done"), sem("sums_got_c"), sem("result_got"), sem("out_done")
        block = ctx.enter_context(nc.Block())

        @block.sync
        def _(sp):
            def body(j, u):
                i, _, _ = step(j, u)
                wait(sp, msg_in_[u], 16 * B * j)
                sp.nop(nofuse=True)
                wait(sp, x1_in[u], 16 * j)
                sp.nop(nofuse=True)
                sp.dma_start(index[u][:, :], msg_idx[:, :, :].rearrange("p s b -> p (s b)")[:, bass.ds(i * B, B)]
                             ).then_inc(index_in[u], 16)
                sp.dma_start(window[u][:, :], win_read[:, bass.ds(i, 1)]).then_inc(index_in[u], 16)

            rounds(sp, body, BLOCKS, RING)

        @block.gpsimd
        def _(pool):
            def scatter(i, u):
                wait(pool, result_got, i + 1)
                wait(pool, target_got, i + 1)
                wait(pool, out_done, 16 * i)
                pool.nop(nofuse=True)
                pool.indirect_dma_start(
                    out=out, out_offset=bass.IndirectOffsetOnAxis(ap=target[u][:, 0:1], axis=0),
                    in_=result[u][:, :], in_offset=None, bounds_check=N - 1, oob_is_err=False).then_inc(out_done, 16)

            def body(j, u):
                i, _, _ = step(j, u)
                wait(pool, result_got, i - 2)
                wait(pool, sum_done, i - 2)
                pool.wait_ge(index_in[u], 32 * (j + 1))
                pool.nop(nofuse=True)
                pool.indirect_dma_start(
                    out=x1[u][:, :], out_offset=None, in_=x1_rows,
                    in_offset=bass.IndirectOffsetOnAxis(ap=window[u][:, 0:1], axis=0)).then_inc(x1_in[u], 16)
                for t in range(B):
                    pool.indirect_dma_start(
                        out=msg[u][:, t, :], out_offset=None, in_=msg_rows,
                        in_offset=bass.IndirectOffsetOnAxis(ap=index[u][:, t:t + 1],
                                                            axis=0)).then_inc(msg_in_[u], 16)
                if not isinstance(i, int) or i >= RING:
                    scatter(i - RING, u)

            rounds(pool, body, BLOCKS, RING)
            for u in range(RING):
                scatter(BLOCKS - RING + u, u)
            pool.wait_ge(out_done, 16 * BLOCKS)

        @block.vector
        def _(dve):
            local_flat = local[:, :, :].rearrange("p s b -> p (s b)")
            weight_flat = weight[:, :, :].rearrange("p s b -> p (s b)")

            def finish(i, j, u):
                wait(dve, sums_got, i + 1)
                wait(dve, x1_in[u], 16 * (j + 1))
                wait(dve, out_done, 16 * (i - 2))
                nc.vector.tensor_copy(target[u][:, :], win_write[:, bass.ds(i, 1)]).then_inc(target_got, 1)
                nc.vector.scalar_tensor_tensor(result[u][:, :], sums[u][:, :], 0.0, x1[u][:, :], ALU.max,
                                               ALU.add).then_inc(result_got, 1)

            def body(j, u):
                i, _, _ = step(j, u)
                wait(dve, sum_done, i - 2)
                for t in range(B):
                    last = nc.vector.tensor_scalar(hot[u][:, t, :], iota_row[:, :], local_flat[:, bass.ds(i * B + t, 1)],
                                                   weight_flat[:, bass.ds(i * B + t, 1)], ALU.is_equal, ALU.mult)
                last.then_inc(hot_got, 1)
                if not (isinstance(i, int) and i == 0):
                    ip, up, jp = step(j, u, -1)
                    nc.vector.tensor_scalar(onward[u][:, :], iota_row[:, :], carry_row[:, bass.ds(i, 1)],
                                            is_last[:, bass.ds(ip, 1)], ALU.is_equal, ALU.mult).then_inc(onward_got, 1)
                    finish(ip, jp, up)

            rounds(dve, body, BLOCKS, RING)
            finish(BLOCKS - 1, BLOCKS // RING - 1, RING - 1)

        @block.scalar
        def _(act):
            def body(j, u):
                i, _, _ = step(j, u)
                act.wait_ge(sum_done, i + 1)
                wait(act, result_got, i - 2)
                nc.scalar.copy(sums[u][:, :], sum_ps[u][:, :]).then_inc(sums_got, 1)

            rounds(act, body, BLOCKS, RING)

        @block.tensor
        def _(pe):
            def body(j, u):
                i, _, _ = step(j, u)
                wait(pe, hot_got, i + 1)
                wait(pe, sums_got, i - 2)
                pe.wait_ge(msg_in_[u], 16 * B * (j + 1))
                for t in range(B):
                    last = nc.tensor.matmul(sum_ps[u][:, :], hot[u][:, t, :], msg[u][:, t, :], start=t == 0,
                                            stop=t == B - 1 and isinstance(i, int) and i == 0)
                if not (isinstance(i, int) and i == 0):
                    wait(pe, onward_got, i)
                    wait(pe, sums_got, i)
                    last = nc.tensor.matmul(sum_ps[u][:, :], onward[u][:, :], sums[(u - 1) % RING][:, :], start=False,
                                            stop=True)
                last.then_inc(sum_done, 1)

            rounds(pe, body, BLOCKS, RING)


def kernel(**inputs):
    import numpy as np
    import concourse.bacc as bacc
    from concourse.bass_utils import run_bass_kernel_spmd as run

    arrays = {name: np.ascontiguousarray(a) for name, a in inputs.items()}
    arrays["edge_weight1"] = arrays["edge_weight1"].reshape(E)
    arrays["L1_gnn_gate_weight"] = np.ascontiguousarray(arrays["L1_gnn_gate_weight"].reshape(R, D).T)
    names = ["x", "src", "dst", "edge_type_16", "edge_weight1", "L0_gnn_Wq", "L0_gnn_bq", "L0_gnn_Wk", "L0_gnn_bk",
             "L0_gnn_Wv", "L0_gnn_bv", "L0_gnn_Wo", "L0_gnn_bo", "L1_gnn_weight", "L1_gnn_gate_weight"]
    nc = bacc.Bacc("TRN2", target_bir_lowering=False, num_devices=1)
    args = [nc.dram_tensor("in_" + name, arrays[name].shape, mybir.dt.from_np(arrays[name].dtype),
                           kind="ExternalInput").ap() for name in names]
    out = nc.dram_tensor("out_rows", [N, D], F32, kind="ExternalOutput").ap()
    build(nc, *args, out)
    result = run(nc, [{"in_" + name: arrays[name] for name in names}], core_ids=[0])
    return result.results[0]["out_rows"]
```

```python
import concourse.bass as bass
from concourse import mybir
from contextlib import ExitStack

F32 = mybir.dt.float32
BF16 = mybir.dt.bfloat16
I32 = mybir.dt.int32
ALU = mybir.AluOpType
ACT = mybir.ActivationFunctionType
AX = mybir.AxisListType

P = 128
D = 256
C = D // P
H = 8
HD = D // H
R = 16
N = 12500
E = 212500
B = 14
PAIRS = B // 2
RING = 3
BLOCKS = -(-E // (P * B))
BLOCKS += -BLOCKS % RING
FULL = E // (P * B)
TAIL = E - FULL * P * B
TAIL_P, TAIL_B = TAIL // B, TAIL % B
TILES = -(-N // P)
PAD_NODE = 16384
ROW = 2 * D + H
AGG = D + H
EPS = 1e-5
NEG = -3e38
TINY = 1e-30
OHG = [4, 4, 4, 2]


def row0(i):
    return N - P if isinstance(i, int) and i == TILES - 1 else i * P


def wait(eng, sem, value):
    if not isinstance(value, int) or value > 0:
        eng.wait_ge(sem, value)


def step(j, u, by=0):
    k = u + by
    return RING * (j + k // RING) + k % RING, k % RING, j + k // RING


def rounds(eng, body, count, unroll):
    first = unroll - 1
    for j in range(first):
        for u in range(unroll):
            body(j, u)
    with eng.Fori(first, count // unroll - 1) as j:
        for u in range(unroll):
            body(j, u)
    for u in range(unroll):
        body(count // unroll - 1, u)


def build(nc, x, src, dst, etype, eweight, wq, bq, wk, bk, wv, bv, wo, bo, wrel, wgate, out):
    def dram(name, shape, dt):
        return nc.dram_tensor(name, shape, dt, kind="Internal").ap()

    q_rows = dram("q_rows", [N + P, 3 * D], BF16)
    kv_rows = dram("kv_rows", [N, 2 * D], F32)
    agg_rows = dram("agg_rows", [N + P, AGG], F32)
    x1_rows = dram("x1_rows", [N, D], F32)
    msg_rows = dram("msg_rows", [N * R, D], F32)
    run_flags = dram("run_flags", [BLOCKS, 2 * P], F32)

    with ExitStack() as whole:
        def keep(name, shape, dt):
            return whole.enter_context(nc.sbuf_tensor(name, shape, dt))

        ident = keep("ident", [P, P], F32)
        iota_row = keep("iota_row", [P, P], F32)
        iota_col = keep("iota_col", [P, 1], F32)
        eps = keep("eps", [P, 1], F32)
        src_idx = keep("src_idx", [P, BLOCKS, B], I32)
        msg_idx = keep("msg_idx", [P, BLOCKS, B], I32)
        weight = keep("weight", [P, BLOCKS, B], F32)
        local = keep("local", [P, BLOCKS, B], F32)
        new_run = keep("new_run", [P, BLOCKS, B], F32)
        not_first = keep("not_first", [P, BLOCKS, B], F32)
        not_last = keep("not_last", [P, BLOCKS, B], F32)
        base = keep("base", [P, BLOCKS], I32)
        low_base = keep("low_base", [P, BLOCKS], I32)
        low_local = keep("low_local", [P, BLOCKS, B], F32)
        low_shift = keep("low_shift", [P, BLOCKS], F32)
        is_last = keep("is_last", [P, BLOCKS], F32)
        carry_row = keep("carry_row", [P, BLOCKS], F32)

        project(nc, x, src, dst, etype, eweight, wq, bq, wk, bk, wv, bv, q_rows, kv_rows, run_flags, ident,
                iota_row, iota_col, eps, src_idx, msg_idx, weight, local, new_run, not_first, not_last, base,
                low_base, low_local, low_shift, is_last, carry_row)
        attend(nc, q_rows, kv_rows, run_flags, agg_rows, ident, iota_row, src_idx, local, new_run, not_first,
               not_last, base, is_last, carry_row)
        messages(nc, x, agg_rows, wo, bo, wrel, wgate, x1_rows, msg_rows, ident, eps)
        collect(nc, msg_rows, x1_rows, iota_row, msg_idx, weight, low_base, low_local, low_shift, out)


def project(nc, x, src, dst, etype, eweight, wq, bq, wk, bk, wv, bv, q_rows, kv_rows, run_flags, ident, iota_row,
            iota_col, eps, src_idx, msg_idx, weight, local, new_run, not_first, not_last, base, low_base, low_local, low_shift,
            is_last, carry_row):
    with ExitStack() as ctx:
        def sb(name, shape, dt=F32):
            return ctx.enter_context(nc.sbuf_tensor(name, shape, dt))

        def ps(name, shape, dt=F32):
            return ctx.enter_context(nc.psum_tensor(name, shape, dt))

        def sem(name):
            return ctx.enter_context(nc.semaphore(name))

        w_q = sb("w_q", [P, C, D])
        w_kv = sb("w_kv", [P, C, 2 * D])
        b_q = sb("b_q", [P, D])
        b_kv = sb("b_kv", [P, 2 * D])
        xt = sb("xt", [P, 2, D])
        stats = sb("stats", [P, 2, 6])
        mv = sb("mv", [P, 2, 2])
        std = sb("std", [P, 2])
        rstd = sb("rstd", [P, 2])
        shift = sb("shift", [P, 2])
        ht = sb("ht", [P, 2, D])
        hT = sb("hT", [P, 2, C, P])
        kv = sb("kv", [P, 2, 2 * D])
        qf = sb("qf", [P, 2, D])
        q3 = sb("q3", [P, 2, 3 * D], BF16)
        dst_i = sb("dst_i", [P, BLOCKS, B], I32)
        type_i = sb("type_i", [P, BLOCKS, B], I32)
        dst_f = sb("dst_f", [P, BLOCKS, B])
        lasts = sb("lasts", [P, BLOCKS])
        before = sb("before", [P, BLOCKS])
        flags = sb("flags", [P, BLOCKS, 2])
        sel = sb("sel", [P, 2, P])
        ends = sb("ends", [P, 2, BLOCKS])
        first_f = sb("first_f", [P, BLOCKS])
        low_first = sb("low_first", [P, BLOCKS])
        tmp = sb("tmp", [P, BLOCKS])
        tmp2 = sb("tmp2", [P, BLOCKS])
        zeros = sb("zeros", [P, 3 * D], BF16)

        hT_ps = [ps(f"hT_ps{i}", [P, C, P]) for i in range(2)]
        kv_ps = [ps(f"kv_ps{i}", [P, 2 * D]) for i in range(2)]
        q_ps = [ps(f"q_ps{i}", [P, D]) for i in range(2)]
        ends_ps = ps("ends_ps", [P, 2, BLOCKS])

        consts = sem("consts")
        weights_in = sem("weights_in")
        bias_scaled = sem("bias_scaled")
        lists_set = sem("lists_set")
        lists_in = sem("lists_in")
        x_in = [sem(f"x_in{i}") for i in range(2)]
        stats_got, mv_got, rstd_got, shift_got = sem("stats_got"), sem("mv_got"), sem("rstd_got"), sem("shift_got")
        std_got = sem("std_got")
        h_got, hT_put, hT_got = sem("h_got"), sem("hT_put"), sem("hT_got")
        q_put, mm_done, kv_got, q_got = sem("q_put"), sem("mm_done"), sem("kv_got"), sem("q_got")
        hi_got, rest_got, mid_got, lo_got = sem("hi_got"), sem("rest_got"), sem("mid_got"), sem("lo_got")
        kv_out = [sem(f"kv_out{i}") for i in range(2)]
        q_out = [sem(f"q_out{i}") for i in range(2)]
        laid = sem("laid")
        zeros_set, zeros_out = sem("zeros_set"), sem("zeros_out")
        ends_put, lasts_got, before_in, flags_got, flags_out = (sem("ends_put"), sem("lasts_got"), sem("before_in"),
                                                                sem("flags_got"), sem("flags_out"))
        block = ctx.enter_context(nc.Block())

        @block.sync
        def _(sp):
            for c in range(C):
                sp.dma_start(w_q[:, c, :], wq[c * P:(c + 1) * P, :]).then_inc(weights_in, 16)
                sp.dma_start(w_kv[:, c, 0:D], wk[c * P:(c + 1) * P, :]).then_inc(weights_in, 16)
                sp.dma_start(w_kv[:, c, D:2 * D], wv[c * P:(c + 1) * P, :]).then_inc(weights_in, 16)
            sp.dma_start(b_q[:, :], bq.partition_broadcast(P)).then_inc(weights_in, 16)
            sp.dma_start(b_kv[:, 0:D], bk.partition_broadcast(P)).then_inc(weights_in, 16)
            sp.dma_start(b_kv[:, D:2 * D], bv.partition_broadcast(P)).then_inc(weights_in, 16)

            def load_x(j, u):
                i = 2 * j + u
                wait(sp, h_got, i - 1)
                sp.nop(nofuse=True)
                sp.dma_start(xt[:, u, :], x[bass.ds(row0(i), P), :]).then_inc(x_in[u], 16)

            rounds(sp, load_x, TILES, 2)
            sp.wait_ge(zeros_set, 1)
            sp.dma_start(q_rows[N:N + P, :], zeros[:, :]).then_inc(zeros_out, 16)
            sp.wait_ge(zeros_out, 16)

        @block.gpsimd
        def _(pool):
            pool.iota(iota_row[:, :], [[1, P]], base=0, channel_multiplier=0,
                      allow_small_or_imprecise_dtypes=True).then_inc(consts, 1)
            pool.iota(iota_col[:, :], [[0, 1]], base=0, channel_multiplier=1,
                      allow_small_or_imprecise_dtypes=True).then_inc(consts, 1)

            def store(j, u):
                i = 2 * j + u
                if isinstance(i, int) and i == TILES - 1:
                    pool.wait_ge(kv_out[1 - u], 16 * (TILES // 2))
                    pool.wait_ge(q_out[1 - u], 16 * (TILES // 2))
                wait(pool, kv_got, i + 1)
                pool.dma_start(kv_rows[bass.ds(row0(i), P), :], kv[:, u, :]).then_inc(kv_out[u], 16)
                wait(pool, lo_got, i + 1)
                pool.dma_start(q_rows[bass.ds(row0(i), P), :], q3[:, u, :]).then_inc(q_out[u], 16)

            rounds(pool, store, TILES, 2)
            for u in range(2):
                pool.wait_ge(kv_out[u], 16 * (TILES // 2))
                pool.wait_ge(q_out[u], 16 * (TILES // 2))
            pool.wait_ge(lasts_got, 1)
            pool.dma_start(before[1:P, :], lasts[0:P - 1, :]).then_inc(before_in, 16)
            pool.dma_start(before[0:1, 1:BLOCKS], lasts[P - 1:P, 0:BLOCKS - 1]).then_inc(before_in, 16)
            pool.wait_ge(flags_got, 1)
            pool.dma_start(run_flags.rearrange("s (p j) -> p s j", j=2), flags[:, :, :]).then_inc(flags_out, 16)
            pool.wait_ge(flags_out, 16)

        @block.scalar
        def _(act):
            act.wait_ge(lists_set, 4)
            for tile, flat in ((dst_i, dst), (src_idx, src), (type_i, etype), (weight, eweight)):
                blocks = flat[0:FULL * P * B].rearrange("(s p b) -> p s b", p=P, b=B)
                act.dma_start(tile[:, 0:FULL, :], blocks).then_inc(lists_in, 16)
                tail = flat[FULL * P * B:FULL * P * B + TAIL_P * B].rearrange("(p b) -> p b", b=B)
                act.dma_start(tile[0:TAIL_P, FULL, :], tail).then_inc(lists_in, 16)
                if TAIL_B:
                    rest = flat[E - TAIL_B:E].rearrange("(p b) -> p b", p=1)
                    act.dma_start(tile[TAIL_P:TAIL_P + 1, FULL, 0:TAIL_B], rest).then_inc(lists_in, 16)

            def normalise(i, u):
                act.wait_ge(mv_got, i + 1)
                nc.scalar.activation(std[:, u:u + 1], mv[:, u, 1:2], ACT.Sqrt, bias=eps[:, 0:1],
                                     scale=1.0).then_inc(std_got, 1)
                act.wait_ge(shift_got, i + 1)
                wait(act, hT_put, i - 1)
                nc.scalar.activation(ht[:, u, :], xt[:, u, :], ACT.Relu, bias=shift[:, u:u + 1],
                                     scale=rstd[:, u:u + 1]).then_inc(h_got, 1)

            def transposed(i, u):
                act.wait_ge(hT_put, i + 1)
                wait(act, mm_done, i - 1)
                nc.scalar.copy(hT[:, u, :, :], hT_ps[u][:, :, :]).then_inc(hT_got, 1)

            def body(j, u):
                i = 2 * j + u
                if isinstance(i, int) and i == 0:
                    normalise(0, 0)
                    transposed(0, 0)
                if not (isinstance(i, int) and i == TILES - 1):
                    normalise(i + 1, 1 - u)
                    transposed(i + 1, 1 - u)
                act.wait_ge(q_got, i + 1)
                if not isinstance(j, int) or j > 0:
                    act.wait_ge(q_out[u], 16 * j)
                nc.scalar.copy(q3[:, u, 0:D], qf[:, u, :]).then_inc(hi_got, 1)
                act.wait_ge(rest_got, i + 1)
                nc.scalar.copy(q3[:, u, D:2 * D], qf[:, u, :]).then_inc(mid_got, 1)

            rounds(act, body, TILES, 2)

        @block.tensor
        def _(pe):
            pe.wait_ge(consts, 4)

            def transposes(i, u):
                pe.wait_ge(h_got, i + 1)
                wait(pe, hT_got, i - 1)
                for c in range(C):
                    last = nc.tensor.transpose(hT_ps[u][:, c, :], ht[:, u, c * P:(c + 1) * P], ident[:, :])
                last.then_inc(hT_put, 1)

            def body(j, u):
                i = 2 * j + u
                if isinstance(i, int) and i == 0:
                    transposes(0, 0)
                    pe.wait_ge(weights_in, 16 * (3 * C + 3))
                pe.wait_ge(hT_got, i + 1)
                wait(pe, q_got, i - 1)
                for c in range(C):
                    last = nc.tensor.matmul(q_ps[u][:, :], hT[:, u, c, :], w_q[:, c, :], start=c == 0,
                                            stop=c == C - 1)
                last.then_inc(q_put, 1)
                wait(pe, kv_got, i - 1)
                nc.tensor.matmul(kv_ps[u][:, :], hT[:, u, 0, :], w_kv[:, 0, :], start=True, stop=False)
                if not (isinstance(i, int) and i == TILES - 1):
                    transposes(i + 1, 1 - u)
                nc.tensor.matmul(kv_ps[u][:, :], hT[:, u, 1, :], w_kv[:, 1, :], start=False,
                                 stop=True).then_inc(mm_done, 1)

            rounds(pe, body, TILES, 2)
            pe.wait_ge(laid, 3)
            nc.tensor.matmul(ends_ps[:, 0, :], sel[:, 0, :], dst_f[:, :, 0], start=True, stop=True)
            nc.tensor.matmul(ends_ps[:, 1, :], sel[:, 1, :], dst_f[:, :, B - 1], start=True,
                             stop=True).then_inc(ends_put, 1)

        @block.vector
        def _(dve):
            nc.vector.memset(eps[:, :], EPS).then_inc(consts, 1)
            nc.vector.memset(zeros[:, :], 0.0).then_inc(zeros_set, 1)
            nc.vector.memset(dst_i[:, :, :], PAD_NODE).then_inc(lists_set, 1)
            nc.vector.memset(src_idx[:, :, :], 0).then_inc(lists_set, 1)
            nc.vector.memset(type_i[:, :, :], 0).then_inc(lists_set, 1)
            nc.vector.memset(weight[:, :, :], 0.0).then_inc(lists_set, 1)
            dve.wait_ge(consts, 3)
            nc.vector.tensor_scalar(ident[:, :], iota_row[:, :], iota_col[:, 0:1], None,
                                    ALU.is_equal).then_inc(consts, 1)
            dve.wait_ge(weights_in, 16 * (3 * C + 3))
            nc.vector.tensor_scalar(b_q[:, :], b_q[:, :], HD ** -0.5, None, ALU.mult).then_inc(bias_scaled, 1)
            dve.wait_ge(bias_scaled, 1)

            def moments(i, j, u):
                dve.wait_ge(x_in[u], 16 * (j + 1))
                nc.vector.bn_stats(stats[:, u, :], xt[:, u, :]).then_inc(stats_got, 1)
                dve.wait_ge(stats_got, i + 1)
                dve.nop(nofuse=True)
                nc.vector.bn_aggr(mv[:, u, :], stats[:, u, :]).then_inc(mv_got, 1)
                dve.wait_ge(std_got, i + 1)
                wait(dve, h_got, i - 1)
                nc.vector.reciprocal(rstd[:, u:u + 1], std[:, u:u + 1]).then_inc(rstd_got, 1)
                dve.wait_ge(rstd_got, i + 1)
                nc.vector.scalar_tensor_tensor(shift[:, u:u + 1], mv[:, u, 0:1], -1.0, rstd[:, u:u + 1], ALU.mult,
                                               ALU.mult).then_inc(shift_got, 1)

            def body(j, u):
                i = 2 * j + u
                if isinstance(i, int) and i == 0:
                    moments(0, 0, 0)
                if not (isinstance(i, int) and i == TILES - 1):
                    moments(i + 1, j if u == 0 else j + 1, 1 - u)
                dve.wait_ge(q_put, i + 1)
                wait(dve, lo_got, i - 1)
                nc.vector.scalar_tensor_tensor(qf[:, u, :], q_ps[u][:, :], HD ** -0.5, b_q[:, :], ALU.mult,
                                               ALU.add).then_inc(q_got, 1)
                dve.wait_ge(hi_got, i + 1)
                nc.vector.tensor_tensor(qf[:, u, :], qf[:, u, :], q3[:, u, 0:D], ALU.subtract).then_inc(rest_got, 1)
                dve.wait_ge(mm_done, i + 1)
                if not isinstance(j, int) or j > 0:
                    dve.wait_ge(kv_out[u], 16 * j)
                nc.vector.tensor_tensor(kv[:, u, :], kv_ps[u][:, :], b_kv[:, :], ALU.add).then_inc(kv_got, 1)
                dve.wait_ge(mid_got, i + 1)
                nc.vector.tensor_tensor(q3[:, u, 2 * D:3 * D], qf[:, u, :], q3[:, u, D:2 * D],
                                        ALU.subtract).then_inc(lo_got, 1)

            rounds(dve, body, TILES, 2)

            done = [0]

            def then(ins):
                done[0] += 1
                ins.then_inc(laid, 1)

            dve.wait_ge(lists_in, 16 * 4 * (3 if TAIL_B else 2))
            then(nc.vector.tensor_copy(dst_f[:, :, :], dst_i[:, :, :]))
            then(nc.vector.tensor_scalar(sel[:, 0, :], iota_col[:, 0:1].broadcast_to([P, P]), 0.0, None,
                                         ALU.is_equal))
            then(nc.vector.tensor_scalar(sel[:, 1, :], iota_col[:, 0:1].broadcast_to([P, P]), float(P - 1), None,
                                         ALU.is_equal))
            dve.wait_ge(laid, done[0])
            nc.vector.memset(before[0:1, 0:1], -1.0)
            nc.vector.tensor_copy(lasts[:, :], dst_f[:, :, B - 1]).then_inc(lasts_got, 1)
            then(nc.vector.scalar_tensor_tensor(msg_idx[:, :, :], src_idx[:, :, :], float(R), type_i[:, :, :],
                                                ALU.mult, ALU.add))
            first = dst_f[:, :, 0:1].broadcast_to([P, BLOCKS, B])
            final = dst_f[:, :, B - 1:B].broadcast_to([P, BLOCKS, B])
            then(nc.vector.tensor_tensor(new_run[:, :, 1:B], dst_f[:, :, 1:B], dst_f[:, :, 0:B - 1], ALU.not_equal))
            then(nc.vector.memset(new_run[:, :, 0:1], 1.0))
            then(nc.vector.tensor_tensor(not_first[:, :, :], dst_f[:, :, :], first, ALU.not_equal))
            then(nc.vector.tensor_tensor(not_last[:, :, :], dst_f[:, :, :], final, ALU.not_equal))
            dve.wait_ge(ends_put, 1)
            then(nc.vector.tensor_copy(ends[:, :, :], ends_ps[:, :, :]))
            dve.wait_ge(laid, done[0])
            for mask in (new_run, not_first, not_last):
                then(nc.vector.tensor_scalar(mask[:, :, :], mask[:, :, :], NEG, None, ALU.mult))
            then(nc.vector.tensor_scalar(first_f[:, :], ends[:, 0, :], float(N), None, ALU.min))
            then(nc.vector.tensor_scalar(low_first[:, :], ends[:, 0, :], float(N - P), None, ALU.min))
            dve.wait_ge(laid, done[0])
            then(nc.vector.tensor_copy(base[:, :], first_f[:, :]))
            then(nc.vector.tensor_copy(low_base[:, :], low_first[:, :]))
            wide = [P, BLOCKS, B]
            then(nc.vector.tensor_tensor(local[:, :, :], dst_f[:, :, :], first_f[:, :].unsqueeze(2).broadcast_to(wide),
                                         ALU.subtract))
            then(nc.vector.tensor_tensor(low_local[:, :, :], dst_f[:, :, :],
                                         low_first[:, :].unsqueeze(2).broadcast_to(wide), ALU.subtract))
            then(nc.vector.tensor_tensor(tmp[:, :], ends[:, 1, :], first_f[:, :], ALU.subtract))
            then(nc.vector.tensor_tensor(carry_row[:, 1:BLOCKS], ends[:, 1, 0:BLOCKS - 1], first_f[:, 1:BLOCKS],
                                         ALU.subtract))
            then(nc.vector.memset(carry_row[:, 0:1], -1.0))
            then(nc.vector.tensor_tensor(tmp2[:, 1:BLOCKS], low_first[:, 0:BLOCKS - 1], low_first[:, 1:BLOCKS],
                                         ALU.subtract))
            then(nc.vector.memset(tmp2[:, 0:1], 0.0))
            dve.wait_ge(laid, done[0])
            then(nc.vector.tensor_scalar(is_last[:, :], tmp[:, :], iota_col[:, 0:1], None, ALU.is_equal))
            then(nc.vector.tensor_scalar(low_shift[:, :], tmp2[:, :], iota_col[:, 0:1], None, ALU.add))
            dve.wait_ge(before_in, 32)
            then(nc.vector.tensor_tensor(flags[:, :, 0], before[:, :], dst_f[:, :, 0], ALU.not_equal))
            then(nc.vector.tensor_tensor(flags[:, :, 1], dst_f[:, :, 0], dst_f[:, :, B - 1], ALU.not_equal))
            dve.wait_ge(laid, done[0])
            nc.vector.tensor_scalar(flags[:, :, :], flags[:, :, :], NEG, None, ALU.mult).then_inc(flags_got, 1)


def attend(nc, q_rows, kv_rows, run_flags, agg_rows, ident, iota_row, src_idx, local, new_run, not_first, not_last,
           base, is_last, carry_row):
    with ExitStack() as ctx:
        def sb(name, shape, dt=F32):
            return ctx.enter_context(nc.sbuf_tensor(name, shape, dt))

        def ps(name, shape, dt=F32):
            return ctx.enter_context(nc.psum_tensor(name, shape, dt))

        def sem(name):
            return ctx.enter_context(nc.semaphore(name))

        kv = [sb(f"kvg{u}", [P, B, ROW]) for u in range(RING)]
        q_win = [sb(f"q_win{u}", [P, 3 * D], BF16) for u in range(RING)]
        onehot = [sb(f"onehot{u}", [P, B, P]) for u in range(RING)]
        index = [sb(f"index{u}", [P, B], I32) for u in range(RING)]
        rows_of = sb("rows_of", [P, B])
        one = sb("one", [P, 1])
        onehotT = sb("onehotT", [P, B, P], BF16)
        score = sb("score", [P, H, B])
        starts = sb("starts", [P, H * B + 1])
        run_fwd = sb("run_fwd", [P, H * B])
        run_max = sb("run_max", [P, H * B])
        list_flags = [sb(f"list_flags{u}", [H, 2 * P + 1]) for u in range(RING)]
        ends_max = sb("ends_max", [H, P, 2])
        list_fwd = sb("list_fwd", [H, RING, 2 * P])
        list_max = sb("list_max", [H, P, 2])
        seg_first = sb("seg_first", [P, H, B])
        seg_last = sb("seg_last", [P, H, B])
        seg_two = sb("seg_two", [P, H, B])
        seg_all = sb("seg_all", [P, H, B])
        arg = sb("arg", [P, H, B])
        fall = sb("fall", [H, 1])
        drop = sb("drop", [H, 1])
        fade = sb("fade", [1, H])
        sums = [sb(f"sums{u}", [P, AGG]) for u in range(RING)]
        last_hot = [sb(f"last_hot{u}", [P, 1]) for u in range(RING)]
        carried = sb("carried", [1, AGG])
        carry_hot = sb("carry_hot", [1, P])

        qe_ps = [ps(f"qe_ps{i}", [P, 2, D]) for i in range(3)]
        oT_ps = [ps(f"oT_ps{i}", [P, 4, P]) for i in range(2)]
        sum_ps = ps("sum_ps", [P, AGG])
        small_ps = ps("small_ps", [P, 512])
        carry_ps = ps("carry_ps", [1, AGG])
        list_ps = small_ps[0:H, 0:2 * P].rearrange("h (j p) -> h j p", j=2)
        back_ps = small_ps[:, 256:272].rearrange("p (j h) -> p j h", j=2)
        drop_ps = small_ps[0:1, 288:288 + H]

        kv_in = [[sem(f"kv_in{u}_{half}") for half in range(2)] for u in range(RING)]
        q_in = [sem(f"q_in{u}") for u in range(RING)]
        flags_in = [sem(f"flags_in{u}") for u in range(RING)]
        index_in = [sem(f"index_in{u}") for u in range(RING)]
        agg_out = [sem(f"agg_out{u}") for u in range(RING)]
        one_set, rows_got, dist_got, onehot_got = sem("one_set"), sem("rows_got"), sem("dist_got"), sem("onehot_got")
        oT_put, oT_got, qe_put, prod_got = sem("oT_put"), sem("oT_got"), sem("qe_put"), sem("prod_got")
        starts_set, starts_got = sem("starts_set"), sem("starts_got")
        score_got, fwd_got, run_got = sem("score_got"), sem("fwd_got"), sem("run_got")
        list_put, list_got, lfwd_got, lmax_got = sem("list_put"), sem("list_got"), sem("lfwd_got"), sem("lmax_got")
        fall_got, drop_got, back_put = sem("fall_got"), sem("drop_got"), sem("back_put")
        segs_got, two_got, all_got, arg_got = sem("segs_got"), sem("two_got"), sem("all_got"), sem("arg_got")
        exp_got, fade_got, ev_got = sem("exp_got"), sem("fade_got"), sem("ev_got")
        half_done, agg_done, sums_got, last_hot_got = (sem("half_done"), sem("agg_done"), sem("sums_got"),
                                                       sem("last_hot_got"))
        carry_put, hot_got, carried_got = sem("carry_put"), sem("hot_got"), sem("carried_got")
        block = ctx.enter_context(nc.Block())
        GROUPS = len(OHG)
        LAST = BLOCKS - 1
        EARLY = 12
        halves = (range(0, PAIRS), range(PAIRS, B))

        def at(i, n):
            return isinstance(i, int) and i == n

        @block.sync
        def _(sp):
            def store(i, j, u):
                wait(sp, sums_got, i + 1)
                sp.nop(nofuse=True)
                if at(i, 0):
                    pass
                else:
                    _, up, jp = step(j, u, -1)
                    wait(sp, agg_out[up], 16 * (jp + 1))
                    sp.nop(nofuse=True)
                first = sp.value_load(base[0:1, bass.ds(i, 1)], min_val=0, max_val=N)
                sp.dma_start(agg_rows[bass.ds(first, P), :], sums[u][:, :]).then_inc(agg_out[u], 16)

            def body(j, u):
                i, _, _ = step(j, u)
                wait(sp, kv_in[u][1], 16 * PAIRS * j)
                sp.nop(nofuse=True)
                sp.dma_start(index[u][:, :], src_idx[:, :, :].rearrange("p s b -> p (s b)")[:, bass.ds(i * B, B)]
                             ).then_inc(index_in[u], 16)
                wait(sp, lmax_got, i - 2)
                sp.nop(nofuse=True)
                sp.dma_start(list_flags[u][:, 0:2 * P],
                             run_flags[bass.ds(i, 1), :].broadcast_to([H, 2 * P])).then_inc(flags_in[u], 16)
                wait(sp, qe_put, PAIRS * (i - 2))
                sp.nop(nofuse=True)
                first = sp.value_load(base[0:1, bass.ds(i, 1)], min_val=0, max_val=N)
                sp.dma_start(q_win[u][:, :], q_rows[bass.ds(first, P), :]).then_inc(q_in[u], 16)
                if not isinstance(i, int) or i >= RING:
                    store(i - RING, j - 1, u)

            sp.wait_ge(starts_set, 2 + RING)
            rounds(sp, body, BLOCKS, RING)
            for u in range(RING):
                store(BLOCKS - RING + u, BLOCKS // RING - 1, u)
            for u in range(RING):
                sp.wait_ge(agg_out[u], 16 * (BLOCKS // RING))

        @block.gpsimd
        def _(pool):
            def body(j, u):
                i, _, _ = step(j, u)
                pool.wait_ge(index_in[u], 16 * (j + 1))
                pool.nop(nofuse=True)
                for half in range(2):
                    wait(pool, agg_done if half else half_done, i - 2)
                    pool.nop(nofuse=True)
                    for t in halves[half]:
                        pool.indirect_dma_start(
                            out=kv[u][:, t, 0:2 * D], out_offset=None, in_=kv_rows,
                            in_offset=bass.IndirectOffsetOnAxis(ap=index[u][:, t:t + 1],
                                                                axis=0)).then_inc(kv_in[u][half], 16)

            rounds(pool, body, BLOCKS, RING)

        @block.vector
        def _(dve):
            nc.vector.memset(one[:, :], 1.0).then_inc(one_set, 1)
            nc.vector.memset(starts[:, :], NEG).then_inc(starts_set, 1)
            for u in range(RING):
                nc.vector.memset(list_flags[u][:, :], NEG).then_inc(starts_set, 1)
            nc.vector.memset(list_fwd[:, :, :], 0.0).then_inc(starts_set, 1)
            dve.wait_ge(starts_set, 2 + RING)

            def products(i, j, u, pairs):
                for pair in pairs:
                    if pair in (0, PAIRS // 2):
                        dve.wait_ge(kv_in[u][pair > 0], 16 * PAIRS * (j + 1))
                    wait(dve, qe_put, PAIRS * i + pair + 1)
                    k = kv[u][:, 2 * pair:2 * pair + 2, 0:D]
                    nc.vector.tensor_tensor(k, k, qe_ps[(PAIRS * u + pair) % 3][:, :, :], ALU.mult).then_inc(prod_got, 1)

            def run_maxima(i, u):
                dve.wait_ge(prod_got, PAIRS * (i + 1))
                wait(dve, arg_got, i)
                nc.vector.tensor_reduce(score[:, :, :], kv[u][:, :, 0:D].rearrange("p t (d h) -> p h t d", h=H), AX.X,
                                        ALU.add).then_inc(score_got, 1)
                flat = score[:, :, :].rearrange("p h t -> p (h t)")
                dve.wait_ge(score_got, i + 1)
                dve.wait_ge(starts_got, i + 1)
                wait(dve, run_got, i)
                nc.vector.tensor_tensor_scan(run_fwd[:, :], starts[:, 0:H * B], flat, 0.0, ALU.add,
                                             ALU.max).then_inc(fwd_got, 1)
                dve.wait_ge(fwd_got, i + 1)
                wait(dve, list_put, i)
                nc.vector.tensor_tensor_scan(run_max[:, ::-1], starts[:, 1:H * B + 1][:, ::-1], run_fwd[:, ::-1], 0.0,
                                             ALU.add, ALU.max).then_inc(run_got, 1)

            def border_maxima(i, j, u):
                dve.wait_ge(flags_in[u], 16 * (j + 1))
                dve.wait_ge(list_got, i + 1)
                now, old = u, (u - 1) % RING
                ends = ends_max[:, :, :].rearrange("h p j -> h (p j)")
                lmax = list_max[:, :, :].rearrange("h p j -> h (p j)")
                nc.vector.tensor_tensor_scan(list_fwd[:, now, :], list_flags[u][:, 0:2 * P], ends,
                                             list_fwd[:, old, 2 * P - 1:2 * P], ALU.add, ALU.max).then_inc(lfwd_got, 1)
                dve.wait_ge(lfwd_got, i + 1)
                wait(dve, back_put, i)
                nc.vector.tensor_tensor_scan(lmax[:, ::-1], list_flags[u][:, 1:2 * P + 1][:, ::-1],
                                             list_fwd[:, now, ::-1], 0.0, ALU.add, ALU.max).then_inc(lmax_got, 1)
                dve.wait_ge(lmax_got, i + 1)
                wait(dve, drop_got, i)
                nc.vector.tensor_tensor(fall[:, :], list_fwd[:, old, 2 * P - 1:2 * P], lmax[:, 0:1],
                                        ALU.subtract).then_inc(fall_got, 1)
                dve.wait_ge(fall_got, i + 1)
                nc.vector.tensor_scalar(drop[:, :], fall[:, :], 0.0, None, ALU.min).then_inc(drop_got, 1)

            def exponents(i):
                dve.wait_ge(back_put, i + 1)
                wide = [P, H, B]
                mine = bass.ds(i, 1)
                nc.vector.tensor_tensor(seg_first[:, :, :], back_ps[:, 0, :].unsqueeze(2).broadcast_to(wide),
                                        not_first[:, mine, :].broadcast_to(wide), ALU.add).then_inc(segs_got, 1)
                nc.vector.tensor_tensor(seg_last[:, :, :], back_ps[:, 1, :].unsqueeze(2).broadcast_to(wide),
                                        not_last[:, mine, :].broadcast_to(wide), ALU.add).then_inc(segs_got, 1)
                dve.wait_ge(segs_got, 2 * (i + 1))
                nc.vector.tensor_tensor(seg_two[:, :, :], seg_first[:, :, :], seg_last[:, :, :],
                                        ALU.max).then_inc(two_got, 1)
                dve.wait_ge(two_got, i + 1)
                nc.vector.tensor_tensor(seg_all[:, :, :], seg_two[:, :, :],
                                        run_max[:, :].rearrange("p (h t) -> p h t", h=H), ALU.max).then_inc(all_got, 1)
                dve.wait_ge(all_got, i + 1)
                wait(dve, exp_got, i)
                nc.vector.tensor_tensor(arg[:, :, :], score[:, :, :], seg_all[:, :, :],
                                        ALU.subtract).then_inc(arg_got, 1)

            def weigh(i, u):
                wait(dve, exp_got, i + 1)
                for half in halves:
                    rows = slice(half[0], half[-1] + 1)
                    v = kv[u][:, rows, D:2 * D].rearrange("p t (d h) -> p t d h", h=H)
                    e = kv[u][:, rows, 2 * D:ROW].unsqueeze(2).broadcast_to([P, len(half), HD, H])
                    nc.vector.tensor_tensor(v, v, e, ALU.mult).then_inc(ev_got, 1)

            def carry(i):
                wait(dve, agg_done, i)
                nc.vector.tensor_scalar(carry_hot[0:1, :], iota_row[0:1, :], carry_row[0:1, bass.ds(i, 1)], None,
                                        ALU.is_equal).then_inc(hot_got, 1)
                wait(dve, fade_got, i + 1)
                wait(dve, carry_put, i)
                nc.vector.tensor_tensor(
                    carried[:, :].rearrange("o (d h) -> o d h", h=H), carry_ps[:, :].rearrange("o (d h) -> o d h", h=H),
                    fade[:, :].unsqueeze(1).broadcast_to([1, AGG // H, H]), ALU.mult).then_inc(carried_got, 1)

            def body(j, u):
                i, _, _ = step(j, u)
                ip, up, jp = step(j, u, -1)
                products(i, j, u, range(0, 3))
                if not at(i, 0):
                    border_maxima(ip, jp, up)
                products(i, j, u, range(3, 5))
                if not at(i, 0):
                    exponents(ip)
                products(i, j, u, range(5, PAIRS))
                if not at(i, 0):
                    weigh(ip, up)
                    if not at(i, 1):
                        carry(ip)
                run_maxima(i, u)

            rounds(dve, body, BLOCKS, RING)
            border_maxima(LAST, BLOCKS // RING - 1, RING - 1)
            exponents(LAST)
            weigh(LAST, RING - 1)
            carry(LAST)

        @block.scalar
        def _(act):
            def distances(i, u, tiles):
                for t in tiles:
                    if t == 0:
                        wait(act, dist_got, i)
                        nc.scalar.copy(rows_of[:, :].unsqueeze(1), local[:, bass.ds(i, 1), :]).then_inc(rows_got, 1)
                        wait(act, agg_done, i - 2)
                        wait(act, rows_got, i + 1)
                    last = nc.scalar.activation(onehot[u][:, t, :], iota_row[:, :], ACT.Abs, bias=rows_of[:, t:t + 1],
                                                scale=-1.0)
                    if t == B - 1:
                        last.then_inc(dist_got, 1)

            def onehots(i, u):
                wait(act, dist_got, i + 1)
                nc.scalar.activation(onehot[u][:, :, :], onehot[u][:, :, :], ACT.Relu, bias=one[:, 0:1],
                                     scale=-1.0).then_inc(onehot_got, 1)

            def transposed(i):
                for g, tiles in enumerate(OHG):
                    first = sum(OHG[:g])
                    wait(act, oT_put, GROUPS * i + g + 1)
                    if g == 0:
                        wait(act, qe_put, PAIRS * i)
                    nc.scalar.copy(onehotT[:, first:first + tiles, :],
                                   oT_ps[g % 2][:, 0:tiles, :]).then_inc(oT_got, 1)

            def take_sums(i, j, u):
                wait(act, agg_done, i + 1)
                if not isinstance(j, int) or j > 0:
                    act.wait_ge(agg_out[u], 16 * j)
                wait(act, carry_put, i - 2)
                nc.scalar.copy(sums[u][:, :], sum_ps[:, :]).then_inc(sums_got, 1)
                nc.scalar.copy(last_hot[u][:, :], is_last[:, bass.ds(i, 1)]).then_inc(last_hot_got, 1)

            def list_out(i):
                act.wait_ge(list_put, i + 1)
                wait(act, lfwd_got, i)
                nc.scalar.copy(ends_max[:, :, :].rearrange("h p j -> h j p"), list_ps).then_inc(list_got, 1)

            def exponentials(i, u):
                act.wait_ge(arg_got, i + 1)
                nc.scalar.activation(kv[u][:, :, 2 * D:ROW].rearrange("p t h -> p h t"), arg[:, :, :],
                                     ACT.Exp).then_inc(exp_got, 1)
                wait(act, carried_got, i - 1)
                nc.scalar.activation(fade[:, :], drop_ps, ACT.Exp).then_inc(fade_got, 1)

            def run_starts(i):
                wait(act, run_got, i)
                nc.scalar.copy(starts[:, 0:H * B].rearrange("p (h t) -> p h t", h=H),
                               new_run[:, bass.ds(i, 1), :].broadcast_to([P, H, B])).then_inc(starts_got, 1)

            def body(j, u):
                i, _, _ = step(j, u)
                if at(i, 0):
                    act.wait_ge(one_set, 1)
                    act.wait_ge(starts_set, 2 + RING)
                    for k in range(2):
                        distances(k, k, range(B))
                        onehots(k, k)
                        transposed(k)
                        if k == 0:
                            run_starts(0)
                    return
                ip, up, _ = step(j, u, -1)
                list_out(ip)
                if not at(i, 1):
                    i2, u2, j2 = step(j, u, -2)
                    take_sums(i2, j2, u2)
                run_starts(i)
                ahead = None if at(i, LAST) else step(j, u, 1)
                if ahead:
                    distances(ahead[0], ahead[1], range(EARLY))
                exponentials(ip, up)
                if ahead:
                    distances(ahead[0], ahead[1], range(EARLY, B))
                    onehots(ahead[0], ahead[1])
                    transposed(ahead[0])

            rounds(act, body, BLOCKS, RING)
            list_out(LAST)
            take_sums(LAST - 1, BLOCKS // RING - 1, RING - 2)
            exponentials(LAST, RING - 1)
            take_sums(LAST, BLOCKS // RING - 1, RING - 1)

        @block.tensor
        def _(pe):
            def transpose_onehot(i, u):
                wait(pe, onehot_got, i + 1)
                for g, tiles in enumerate(OHG):
                    wait(pe, oT_got, GROUPS * i + g - 1)
                    for t in range(tiles):
                        last = nc.tensor.transpose(oT_ps[g % 2][:, t, :], onehot[u][:, sum(OHG[:g]) + t, :],
                                                   ident[:, :])
                    last.then_inc(oT_put, 1)

            def expand_q(i, j, u, pairs):
                for pair in pairs:
                    if pair == 0:
                        pe.wait_ge(q_in[u], 16 * (j + 1))
                    wait(pe, prod_got, PAIRS * i + pair - 2)
                    wait(pe, oT_got, GROUPS * i + (2 * pair + 1) // 4 + 1)
                    for t in range(2):
                        for part in range(3):
                            last = nc.tensor.matmul(qe_ps[(PAIRS * u + pair) % 3][:, t, :], onehotT[:, 2 * pair + t, :],
                                                    q_win[u][:, part * D:(part + 1) * D], start=part == 0,
                                                    stop=part == 2)
                    last.then_inc(qe_put, 1)

            def add_tiles(i, u, half):
                wait(pe, ev_got, 2 * i + half + 1)
                if half == 0:
                    wait(pe, sums_got, i)
                for t in halves[half]:
                    last = nc.tensor.matmul(sum_ps[:, :], onehot[u][:, t, :], kv[u][:, t, D:ROW], start=t == 0,
                                            stop=t == B - 1 and at(i, 0))
                if half == 0:
                    last.then_inc(half_done, 1)
                elif at(i, 0):
                    last.then_inc(agg_done, 1)
                else:
                    wait(pe, hot_got, i)
                    wait(pe, carried_got, i)
                    nc.tensor.matmul(sum_ps[:, :], carry_hot[0:1, :], carried[0:1, :], start=False,
                                     stop=True).then_inc(agg_done, 1)

            def take_carry(i, u):
                wait(pe, sums_got, i + 1)
                wait(pe, last_hot_got, i + 1)
                wait(pe, carried_got, i)
                nc.tensor.matmul(carry_ps[:, :], last_hot[u][:, :], sums[u][:, :], start=True,
                                 stop=True).then_inc(carry_put, 1)

            def list_transposes(i):
                wait(pe, run_got, i + 1)
                wait(pe, list_got, i)
                wait(pe, segs_got, 2 * i)
                wait(pe, fade_got, i)
                runs = run_max[:, :].rearrange("p (h t) -> p h t", h=H)
                nc.tensor.transpose(list_ps[:, 0, :], runs[:, :, 0], ident[:, :])
                nc.tensor.transpose(list_ps[:, 1, :], runs[:, :, B - 1], ident[:, :]).then_inc(list_put, 1)

            def back_transposes(i):
                wait(pe, lmax_got, i + 1)
                wait(pe, drop_got, i + 1)
                pe.nop(nofuse=True)
                nc.tensor.matmul(drop_ps, drop[:, :], ident[0:H, 0:H], start=True, stop=True)
                nc.tensor.transpose(back_ps[:, 0, :], list_max[:, :, 0], ident[0:H, 0:H])
                nc.tensor.transpose(back_ps[:, 1, :], list_max[:, :, 1], ident[0:H, 0:H]).then_inc(back_put, 1)

            def body(j, u):
                i, _, _ = step(j, u)
                if at(i, 0):
                    transpose_onehot(0, 0)
                    expand_q(0, 0, 0, range(PAIRS))
                    transpose_onehot(1, 1)
                    return
                ip, up, _ = step(j, u, -1)
                expand_q(i, j, u, range(0, 1))
                list_transposes(ip)
                expand_q(i, j, u, range(1, 4))
                back_transposes(ip)
                expand_q(i, j, u, range(4, PAIRS))
                if not at(i, 1):
                    i2, u2, _ = step(j, u, -2)
                    take_carry(i2, u2)
                add_tiles(ip, up, 0)
                if not at(i, LAST):
                    i2, u2, _ = step(j, u, 1)
                    transpose_onehot(i2, u2)
                add_tiles(ip, up, 1)

            rounds(pe, body, BLOCKS, RING)
            list_transposes(LAST)
            back_transposes(LAST)
            take_carry(LAST - 1, RING - 2)
            add_tiles(LAST, RING - 1, 0)
            add_tiles(LAST, RING - 1, 1)


def messages(nc, x, agg_rows, wo, bo, wrel, wgate, x1_rows, msg_rows, ident, eps):
    with ExitStack() as ctx:
        def sb(name, shape, dt=F32):
            return ctx.enter_context(nc.sbuf_tensor(name, shape, dt))

        def ps(name, shape, dt=F32):
            return ctx.enter_context(nc.psum_tensor(name, shape, dt))

        def sem(name):
            return ctx.enter_context(nc.semaphore(name))

        w_o = sb("w_o", [P, C, D])
        b_o = sb("b_o", [P, D])
        w_rel = sb("w_rel", [P, C, R, D])
        w_gate = sb("w_gate", [P, C, R])
        agg = sb("agg", [P, 2, AGG])
        xt = sb("xt1", [P, 2, D])
        inv = sb("inv", [P, 2, H])
        att = sb("att", [P, D])
        xb = sb("xb", [P, D])
        attT = sb("attT", [P, C, P])
        x1 = sb("x1", [P, 2, D])
        stats = sb("stats1", [P, 6])
        mv = sb("mv1", [P, 2])
        std = sb("std1", [P, 1])
        rstd = sb("rstd1", [P, 1])
        shift = sb("shift1", [P, 1])
        ht = sb("ht1", [P, D])
        hT = sb("hT1", [P, 2, C, P])
        gate = sb("gate", [P, 2, R])
        msg = sb("msg", [P, 2, R, D])

        big_ps = [ps(f"big_ps{i}", [P, 2, D]) for i in range(4)]
        attT_ps = ps("attT_ps", [P, C, P])
        hT_ps = ps("hiddenT_ps", [P, C, P])
        o_ps = ps("o_ps", [P, D])
        gate_ps = ps("gate_ps", [P, R])

        weights_in = sem("weights_in1")
        agg_in = [sem(f"agg_in{u}") for u in range(2)]
        inv0_got, inv_got, att_got, xb_got, x1_got = (sem("inv0_got"), sem("inv_got"), sem("att_got"), sem("xb_got"),
                                                      sem("x1_got"))
        attT_put, attT_got, o_put = sem("attT_put"), sem("attT_got"), sem("o_put")
        stats_got, mv_got, rstd_got, shift_got = sem("stats_got1"), sem("mv_got1"), sem("rstd_got1"), sem("shift_got1")
        std_got = sem("std_got1")
        h_got, hT_put, hT_got = sem("h_got1"), sem("hT_put1"), sem("hT_got1")
        gate_put, gate_got = sem("gate_put"), sem("gate_got")
        big_put, even_got, odd_got = sem("big_put"), sem("even_got"), sem("odd_got")
        x1_out = [sem(f"x1_out{u}") for u in range(2)]
        msg_out = [sem(f"msg_out{u}") for u in range(2)]
        block = ctx.enter_context(nc.Block())
        G = R // 2
        msg_view = msg_rows.rearrange("(n r) d -> n r d", r=R)

        @block.gpsimd
        def _(pool):
            pool.dma_start(w_o[:, :, :], wo.rearrange("(c p) d -> p c d", p=P)).then_inc(weights_in, 16)
            pool.dma_start(b_o[:, :], bo.partition_broadcast(P)).then_inc(weights_in, 16)
            pool.dma_start(w_gate[:, :, :], wgate.rearrange("(c p) r -> p c r", p=P)).then_inc(weights_in, 16)
            for c in range(C):
                pool.dma_start(w_rel[:, c, :, :],
                               wrel[:, c * P:(c + 1) * P, :].rearrange("r p d -> p r d")).then_inc(weights_in, 16)

            def load(j, u):
                i = 2 * j + u
                wait(pool, x1_got, i - 1)
                pool.nop(nofuse=True)
                pool.dma_start(agg[:, u, :], agg_rows[bass.ds(row0(i), P), :]).then_inc(agg_in[u], 16)
                pool.dma_start(xt[:, u, :], x[bass.ds(row0(i), P), :]).then_inc(agg_in[u], 16)

            rounds(pool, load, TILES, 2)

        @block.sync
        def _(sp):
            def store(i, u):
                if isinstance(i, int) and i == TILES - 1:
                    sp.wait_ge(x1_out[1 - u], 16 * (TILES // 2))
                    sp.wait_ge(msg_out[1 - u], 32 * (TILES // 2))
                sp.wait_ge(x1_got, i + 1)
                sp.nop(nofuse=True)
                sp.dma_start(x1_rows[bass.ds(row0(i), P), :], x1[:, u, :]).then_inc(x1_out[u], 16)
                for half in range(2):
                    rels = slice(half * R // 2, (half + 1) * R // 2)
                    sp.wait_ge(even_got, G // 2 * i + (half + 1) * G // 4)
                    sp.wait_ge(odd_got, G // 2 * i + (half + 1) * G // 4)
                    sp.nop(nofuse=True)
                    sp.dma_start(msg_view[bass.ds(row0(i), P), rels, :], msg[:, u, rels, :]).then_inc(msg_out[u], 16)

            rounds(sp, lambda j, u: store(2 * j + u, u), TILES, 2)
            for u in range(2):
                sp.wait_ge(x1_out[u], 16 * (TILES // 2))
                sp.wait_ge(msg_out[u], 32 * (TILES // 2))

        @block.vector
        def _(dve):
            def front(i, j, u):
                def attention():
                    dve.wait_ge(agg_in[u], 32 * (j + 1))
                    if isinstance(i, int) and i == 0:
                        dve.wait_ge(weights_in, 16 * (3 + C))
                    nc.vector.tensor_scalar(inv[:, u, :], agg[:, u, D:AGG], TINY, None, ALU.max).then_inc(inv0_got, 1)
                    dve.wait_ge(inv0_got, i + 1)
                    nc.vector.reciprocal(inv[:, u, :], inv[:, u, :]).then_inc(inv_got, 1)
                    dve.wait_ge(inv_got, i + 1)
                    wait(dve, attT_put, i)
                    nc.vector.tensor_tensor(
                        att[:, :].rearrange("p (d h) -> p d h", h=H), agg[:, u, 0:D].rearrange("p (d h) -> p d h", h=H),
                        inv[:, u, :].unsqueeze(1).broadcast_to([P, HD, H]), ALU.mult).then_inc(att_got, 1)
                    wait(dve, x1_got, i)
                    nc.vector.tensor_tensor(xb[:, :], xt[:, u, :], b_o[:, :], ALU.add).then_inc(xb_got, 1)

                def residual():
                    dve.wait_ge(xb_got, i + 1)
                    dve.wait_ge(o_put, i + 1)
                    wait(dve, h_got, i - 1)
                    if not isinstance(j, int) or j > 0:
                        dve.wait_ge(x1_out[u], 16 * j)
                    nc.vector.tensor_tensor(x1[:, u, :], o_ps[:, :], xb[:, :], ALU.add).then_inc(x1_got, 1)
                    dve.wait_ge(x1_got, i + 1)
                    nc.vector.bn_stats(stats[:, :], x1[:, u, :]).then_inc(stats_got, 1)
                    dve.wait_ge(stats_got, i + 1)
                    dve.nop(nofuse=True)
                    nc.vector.bn_aggr(mv[:, :], stats[:, :]).then_inc(mv_got, 1)
                    dve.wait_ge(mv_got, i + 1)
                    dve.wait_ge(std_got, i + 1)
                    wait(dve, h_got, i)
                    nc.vector.reciprocal(rstd[:, :], std[:, :]).then_inc(rstd_got, 1)
                    dve.wait_ge(rstd_got, i + 1)
                    nc.vector.scalar_tensor_tensor(shift[:, :], mv[:, 0:1], -1.0, rstd[:, :], ALU.mult,
                                                   ALU.mult).then_inc(shift_got, 1)

                return {1: attention, 4: residual}

            def body(j, u):
                i = 2 * j + u
                if isinstance(i, int) and i == 0:
                    for piece in front(0, 0, 0).values():
                        piece()
                ahead = {}
                if not (isinstance(i, int) and i == TILES - 1):
                    ahead = front(i + 1, j if u == 0 else j + 1, 1 - u)
                dve.wait_ge(gate_got, i + 1)
                if not isinstance(j, int) or j > 0:
                    dve.wait_ge(msg_out[u], 32 * j)
                for g in range(G):
                    if g % 2:
                        wait(dve, big_put, G * i + g + 1)
                        for k in range(2):
                            rel = 2 * g + k
                            last = nc.vector.tensor_scalar(msg[:, u, rel, :], big_ps[g % 4][:, k, :],
                                                           gate[:, u, rel:rel + 1], None, ALU.mult)
                        last.then_inc(odd_got, 1)
                    if g in ahead:
                        ahead[g]()

            rounds(dve, body, TILES, 2)

        @block.scalar
        def _(act):
            def front(i, u):
                def attention():
                    act.wait_ge(attT_put, i + 1)
                    wait(act, o_put, i)
                    nc.scalar.copy(attT[:, :, :], attT_ps[:, :, :]).then_inc(attT_got, 1)

                def hidden():
                    act.wait_ge(mv_got, i + 1)
                    nc.scalar.activation(std[:, :], mv[:, 1:2], ACT.Sqrt, bias=eps[:, 0:1],
                                         scale=1.0).then_inc(std_got, 1)
                    act.wait_ge(shift_got, i + 1)
                    wait(act, hT_put, i)
                    nc.scalar.activation(ht[:, :], x1[:, u, :], ACT.Relu, bias=shift[:, 0:1],
                                         scale=rstd[:, 0:1]).then_inc(h_got, 1)

                def hidden_back():
                    act.wait_ge(hT_put, i + 1)
                    wait(act, big_put, G * (i - 1))
                    nc.scalar.copy(hT[:, u, :, :], hT_ps[:, :, :]).then_inc(hT_got, 1)

                return {2: attention, 4: hidden, 6: hidden_back}

            def body(j, u):
                i = 2 * j + u
                if isinstance(i, int) and i == 0:
                    for piece in front(0, 0).values():
                        piece()
                ahead = {} if isinstance(i, int) and i == TILES - 1 else front(i + 1, 1 - u)
                act.wait_ge(gate_put, i + 1)
                wait(act, odd_got, G // 2 * (i - 1))
                nc.scalar.activation(gate[:, u, :], gate_ps[:, :], ACT.Sigmoid).then_inc(gate_got, 1)
                act.wait_ge(gate_got, i + 1)
                if not isinstance(j, int) or j > 0:
                    act.wait_ge(msg_out[u], 32 * j)
                for g in range(G):
                    if g % 2 == 0:
                        wait(act, big_put, G * i + g + 1)
                        for k in range(2):
                            rel = 2 * g + k
                            last = nc.scalar.activation(msg[:, u, rel, :], big_ps[g % 4][:, k, :], ACT.Copy,
                                                        scale=gate[:, u, rel:rel + 1])
                        last.then_inc(even_got, 1)
                    if g in ahead:
                        ahead[g]()

            rounds(act, body, TILES, 2)

        @block.tensor
        def _(pe):
            def front(i):
                def attention():
                    pe.wait_ge(att_got, i + 1)
                    wait(pe, attT_got, i)
                    for c in range(C):
                        last = nc.tensor.transpose(attT_ps[:, c, :], att[:, c * P:(c + 1) * P], ident[:, :])
                    last.then_inc(attT_put, 1)

                def output():
                    pe.wait_ge(attT_got, i + 1)
                    wait(pe, x1_got, i)
                    for c in range(C):
                        last = nc.tensor.matmul(o_ps[:, :], attT[:, c, :], w_o[:, c, :], start=c == 0, stop=c == C - 1)
                    last.then_inc(o_put, 1)

                def hidden():
                    pe.wait_ge(h_got, i + 1)
                    wait(pe, hT_got, i)
                    for c in range(C):
                        last = nc.tensor.transpose(hT_ps[:, c, :], ht[:, c * P:(c + 1) * P], ident[:, :])
                    last.then_inc(hT_put, 1)

                return {2: attention, 3: output, 6: hidden}

            def body(j, u):
                i = 2 * j + u
                if isinstance(i, int) and i == 0:
                    pe.wait_ge(weights_in, 16 * (3 + C))
                    for piece in front(0).values():
                        piece()
                ahead = {} if isinstance(i, int) and i == TILES - 1 else front(i + 1)
                pe.wait_ge(hT_got, i + 1)
                wait(pe, gate_got, i)
                for c in range(C):
                    last = nc.tensor.matmul(gate_ps[:, :], hT[:, u, c, :], w_gate[:, c, :], start=c == 0,
                                            stop=c == C - 1)
                last.then_inc(gate_put, 1)
                for g in range(G):
                    wait(pe, odd_got if g % 2 else even_got, G // 2 * i + g // 2 - 1)
                    for c in range(C):
                        last = nc.tensor.matmul(big_ps[g % 4][:, :, :], hT[:, u, c, :], w_rel[:, c, 2 * g:2 * g + 2, :],
                                                start=c == 0, stop=c == C - 1)
                    last.then_inc(big_put, 1)
                    if g in ahead:
                        ahead[g]()

            rounds(pe, body, TILES, 2)


def collect(nc, msg_rows, x1_rows, iota_row, msg_idx, weight, low_base, low_local, low_shift, out):
    with ExitStack() as ctx:
        def sb(name, shape, dt=F32):
            return ctx.enter_context(nc.sbuf_tensor(name, shape, dt))

        def sem(name):
            return ctx.enter_context(nc.semaphore(name))

        msg = [sb(f"msg_in{u}", [P, B, D]) for u in range(RING)]
        x1 = [sb(f"x1_in{u}", [P, D]) for u in range(RING)]
        index = [sb(f"index_c{u}", [P, B], I32) for u in range(RING)]
        hot = [sb(f"hot{u}", [P, B, P]) for u in range(RING)]
        onward = [sb(f"onward{u}", [P, P]) for u in range(RING)]
        sums = [sb(f"sums_c{u}", [P, D]) for u in range(RING)]
        result = [sb(f"result{u}", [P, D]) for u in range(RING)]
        sum_ps = [ctx.enter_context(nc.psum_tensor(f"sum_ps_c{u}", [P, D], F32)) for u in range(RING)]

        msg_here = [sem(f"msg_here{u}") for u in range(RING)]
        x1_in = [sem(f"x1_landed{u}") for u in range(RING)]
        index_in = [sem(f"index_in_c{u}") for u in range(RING)]
        out_done = [sem(f"out_done{u}") for u in range(RING)]
        hot_got, onward_got = sem("hot_got_c"), sem("onward_got")
        sum_done, sums_got, result_got = sem("sum_done"), sem("sums_got_c"), sem("result_got")
        block = ctx.enter_context(nc.Block())

        @block.sync
        def _(sp):
            def store(i, j, u):
                wait(sp, result_got, i + 1)
                sp.nop(nofuse=True)
                if not isinstance(i, int) or i > 0:
                    _, up, jp = step(j, u, -1)
                    wait(sp, out_done[up], 16 * (jp + 1))
                    sp.nop(nofuse=True)
                first = sp.value_load(low_base[0:1, bass.ds(i, 1)], min_val=0, max_val=N - P)
                sp.dma_start(out[bass.ds(first, P), :], result[u][:, :]).then_inc(out_done[u], 16)

            def body(j, u):
                i, _, _ = step(j, u)
                wait(sp, msg_here[u], 16 * B * j)
                sp.nop(nofuse=True)
                sp.dma_start(index[u][:, :], msg_idx[:, :, :].rearrange("p s b -> p (s b)")[:, bass.ds(i * B, B)]
                             ).then_inc(index_in[u], 16)
                wait(sp, result_got, i - 2)
                sp.nop(nofuse=True)
                first = sp.value_load(low_base[0:1, bass.ds(i, 1)], min_val=0, max_val=N - P)
                sp.dma_start(x1[u][:, :], x1_rows[bass.ds(first, P), :]).then_inc(x1_in[u], 16)
                if not isinstance(i, int) or i >= RING:
                    store(i - RING, j - 1, u)

            rounds(sp, body, BLOCKS, RING)
            for u in range(RING):
                store(BLOCKS - RING + u, BLOCKS // RING - 1, u)
            for u in range(RING):
                sp.wait_ge(out_done[u], 16 * (BLOCKS // RING))

        @block.gpsimd
        def _(pool):
            def body(j, u):
                i, _, _ = step(j, u)
                wait(pool, sum_done, i - 2)
                pool.nop(nofuse=True)
                pool.wait_ge(index_in[u], 16 * (j + 1))
                pool.nop(nofuse=True)
                for t in range(B):
                    pool.indirect_dma_start(
                        out=msg[u][:, t, :], out_offset=None, in_=msg_rows,
                        in_offset=bass.IndirectOffsetOnAxis(ap=index[u][:, t:t + 1],
                                                            axis=0)).then_inc(msg_here[u], 16)

            rounds(pool, body, BLOCKS, RING)

        @block.vector
        def _(dve):
            local_flat = low_local[:, :, :].rearrange("p s b -> p (s b)")
            weight_flat = weight[:, :, :].rearrange("p s b -> p (s b)")

            def finish(i, j, u):
                wait(dve, sums_got, i + 1)
                wait(dve, x1_in[u], 16 * (j + 1))
                if not isinstance(j, int) or j > 0:
                    dve.wait_ge(out_done[u], 16 * j)
                nc.vector.scalar_tensor_tensor(result[u][:, :], sums[u][:, :], 0.0, x1[u][:, :], ALU.max,
                                               ALU.add).then_inc(result_got, 1)

            def body(j, u):
                i, _, _ = step(j, u)
                wait(dve, sum_done, i - 2)
                for t in range(B):
                    last = nc.vector.tensor_scalar(hot[u][:, t, :], iota_row[:, :],
                                                   local_flat[:, bass.ds(i * B + t, 1)],
                                                   weight_flat[:, bass.ds(i * B + t, 1)], ALU.is_equal, ALU.mult)
                last.then_inc(hot_got, 1)
                if not (isinstance(i, int) and i == 0):
                    ip, up, jp = step(j, u, -1)
                    nc.vector.tensor_scalar(onward[u][:, :], iota_row[:, :], low_shift[:, bass.ds(i, 1)], None,
                                            ALU.is_equal).then_inc(onward_got, 1)
                    finish(ip, jp, up)

            rounds(dve, body, BLOCKS, RING)
            finish(BLOCKS - 1, BLOCKS // RING - 1, RING - 1)

        @block.scalar
        def _(act):
            def body(j, u):
                i, _, _ = step(j, u)
                act.wait_ge(sum_done, i + 1)
                wait(act, result_got, i - 2)
                nc.scalar.copy(sums[u][:, :], sum_ps[u][:, :]).then_inc(sums_got, 1)

            rounds(act, body, BLOCKS, RING)

        @block.tensor
        def _(pe):
            def body(j, u):
                i, _, _ = step(j, u)
                wait(pe, hot_got, i + 1)
                wait(pe, sums_got, i - 2)
                pe.wait_ge(msg_here[u], 16 * B * (j + 1))
                for t in range(B):
                    last = nc.tensor.matmul(sum_ps[u][:, :], hot[u][:, t, :], msg[u][:, t, :], start=t == 0,
                                            stop=t == B - 1 and isinstance(i, int) and i == 0)
                if not (isinstance(i, int) and i == 0):
                    wait(pe, onward_got, i)
                    wait(pe, sums_got, i)
                    last = nc.tensor.matmul(sum_ps[u][:, :], onward[u][:, :], sums[(u - 1) % RING][:, :], start=False,
                                            stop=True)
                last.then_inc(sum_done, 1)

            rounds(pe, body, BLOCKS, RING)


def kernel(**inputs):
    import numpy as np
    import concourse.bacc as bacc
    from concourse.bass_utils import run_bass_kernel_spmd as run

    arrays = {name: np.ascontiguousarray(a) for name, a in inputs.items()}
    arrays["edge_weight1"] = arrays["edge_weight1"].reshape(E)
    arrays["L1_gnn_gate_weight"] = np.ascontiguousarray(arrays["L1_gnn_gate_weight"].reshape(R, D).T)
    names = ["x", "src", "dst", "edge_type_16", "edge_weight1", "L0_gnn_Wq", "L0_gnn_bq", "L0_gnn_Wk", "L0_gnn_bk",
             "L0_gnn_Wv", "L0_gnn_bv", "L0_gnn_Wo", "L0_gnn_bo", "L1_gnn_weight", "L1_gnn_gate_weight"]
    nc = bacc.Bacc("TRN2", target_bir_lowering=False, num_devices=1)
    args = [nc.dram_tensor("in_" + name, arrays[name].shape, mybir.dt.from_np(arrays[name].dtype),
                           kind="ExternalInput").ap() for name in names]
    out = nc.dram_tensor("out_rows", [N, D], F32, kind="ExternalOutput").ap()
    build(nc, *args, out)
    result = run(nc, [{"in_" + name: arrays[name] for name in names}], core_ids=[0])
    return result.results[0]["out_rows"]
```

```python
import concourse.bass as bass
from concourse import mybir
from contextlib import ExitStack

F32 = mybir.dt.float32
F32R = mybir.dt.float32r
BF16 = mybir.dt.bfloat16
I32 = mybir.dt.int32
ALU = mybir.AluOpType
ACT = mybir.ActivationFunctionType
AX = mybir.AxisListType

P = 128
D = 256
C = D // P
H = 8
HD = D // H
R = 16
N = 12500
E = 212500
B = 14
PAIRS = B // 2
RING = 3
BLOCKS = -(-E // (P * B))
FULL = E // (P * B)
TAIL = E - FULL * P * B
TAIL_P, TAIL_B = TAIL // B, TAIL % B
TILES = -(-N // P)
COLUMNS = BLOCKS * B
PAD_NODE = 16384
ROW = 2 * D + H
AGG = D + H
EPS = 1e-5
NEG = -3e38
TINY = 1e-30
OHG = [4, 4, 4, 2]

GROUP_STEPS = 11
WEIGH_STEPS = 15
ANY_SEMS = ("any_ready", "any_filled", "any_kv_in", "any_q_in", "any_max_in", "any_acc_in", "any_max_out",
            "any_written", "any_grouped", "any_weighed", "any_put", "any_exps_got", "any_msg_in", "any_total_in",
            "any_total_out", "any_grouped_c", "any_added")


def row0(i):
    return N - P if isinstance(i, int) and i == TILES - 1 else i * P


def wait(eng, sem, value):
    if not isinstance(value, int) or value > 0:
        eng.wait_ge(sem, value)


def step(j, u, by=0):
    k = u + by
    return RING * (j + k // RING) + k % RING, k % RING, j + k // RING


def rounds(eng, body, count, unroll):
    first, last = unroll - 1, (count - 1) // unroll
    for j in range(first):
        for u in range(unroll):
            body(j, u)
    with eng.Fori(first, last) as j:
        for u in range(unroll):
            body(j, u)
    for u in range(count - unroll * last):
        body(last, u)


def build(nc, x, src, dst, etype, eweight, wq, bq, wk, bk, wv, bv, wo, bo, wrel, wgate, out):
    def dram(name, shape, dt):
        return nc.dram_tensor(name, shape, dt, kind="Internal").ap()

    q_rows = dram("q_rows", [N + P, 3 * D], BF16)
    kv_rows = dram("kv_rows", [N, 2 * D], F32)
    agg_rows = dram("agg_rows", [N + P, AGG], F32)
    x1_rows = dram("x1_rows", [N, D], F32)
    msg_rows = dram("msg_rows", [N * R, D], F32)
    run_flags = dram("run_flags", [BLOCKS, 2 * P], F32)
    max_rows = dram("max_rows", [N + P, H], F32)
    acc_rows = dram("acc_rows", [N + P, D], F32)

    with ExitStack() as whole:
        def keep(name, shape, dt):
            return whole.enter_context(nc.sbuf_tensor(name, shape, dt))

        any_sems = {name: whole.enter_context(nc.semaphore(name)) for name in ANY_SEMS}
        ident = keep("ident", [P, P], F32)
        iota_row = keep("iota_row", [P, P], F32)
        iota_col = keep("iota_col", [P, 1], F32)
        eps = keep("eps", [P, 1], F32)
        src_idx = keep("src_idx", [P, BLOCKS, B], I32)
        msg_idx = keep("msg_idx", [P, BLOCKS, B], I32)
        weight = keep("weight", [P, BLOCKS, B], F32)
        local = keep("local", [P, BLOCKS, B], F32)
        new_run = keep("new_run", [P, BLOCKS, B], F32)
        not_first = keep("not_first", [P, BLOCKS, B], F32)
        not_last = keep("not_last", [P, BLOCKS, B], F32)
        base = keep("base", [P, BLOCKS], I32)
        low_base = keep("low_base", [P, BLOCKS], I32)
        low_local = keep("low_local", [P, BLOCKS, B], F32)
        low_shift = keep("low_shift", [P, BLOCKS], F32)
        is_last = keep("is_last", [P, BLOCKS], F32)
        irregular = keep("irregular", [P, 1], I32)
        carry_row = keep("carry_row", [P, BLOCKS], F32)

        project(nc, x, src, dst, etype, eweight, wq, bq, wk, bk, wv, bv, q_rows, kv_rows, run_flags, ident,
                iota_row, iota_col, eps, src_idx, msg_idx, weight, local, new_run, not_first, not_last, base,
                low_base, low_local, low_shift, is_last, carry_row, irregular)
        attend(nc, q_rows, kv_rows, run_flags, agg_rows, ident, iota_row, src_idx, local, new_run, not_first,
               not_last, base, is_last, carry_row)
        attend_any(nc, any_sems, q_rows, kv_rows, agg_rows, max_rows, irregular, ident, iota_row, iota_col, src_idx, local, base)
        messages(nc, x, agg_rows, wo, bo, wrel, wgate, x1_rows, msg_rows, ident, eps)
        collect(nc, msg_rows, x1_rows, iota_row, msg_idx, weight, low_base, low_local, low_shift, out)
        collect_any(nc, any_sems, msg_rows, x1_rows, acc_rows, irregular, ident, iota_row, iota_col, msg_idx, weight, local,
                    base, out)


def project(nc, x, src, dst, etype, eweight, wq, bq, wk, bk, wv, bv, q_rows, kv_rows, run_flags, ident, iota_row,
            iota_col, eps, src_idx, msg_idx, weight, local, new_run, not_first, not_last, base, low_base, low_local, low_shift,
            is_last, carry_row, irregular):
    with ExitStack() as ctx:
        def sb(name, shape, dt=F32):
            return ctx.enter_context(nc.sbuf_tensor(name, shape, dt))

        def ps(name, shape, dt=F32):
            return ctx.enter_context(nc.psum_tensor(name, shape, dt))

        def sem(name):
            return ctx.enter_context(nc.semaphore(name))

        w_all = sb("w_all", [P, C, 3 * D])
        w_hi = sb("wp_hi", [P, C, 3 * D], F32R)
        w_lo = sb("wp_lo", [P, C, 3 * D], F32R)
        b_q = sb("b_q", [P, D])
        b_kv = sb("b_kv", [P, 2 * D])
        xt = sb("xt", [P, 2, D])
        stats = sb("stats", [P, 2, 6])
        mv = sb("mv", [P, 2, 2])
        std = sb("std", [P, 2])
        rstd = sb("rstd", [P, 2])
        shift = sb("shift", [P, 2])
        ht = sb("ht", [P, 2, D])
        h_hi = sb("hp_hi", [P, 2, C, P], F32R)
        h_lo = sb("hp_lo", [P, 2, C, P], F32R)
        kv = sb("kv", [P, 2, 2 * D])
        qf = sb("qf", [P, 2, D])
        q3 = sb("q3", [P, 2, 3 * D], BF16)
        dst_i = sb("dst_i", [P, BLOCKS, B], I32)
        type_i = sb("type_i", [P, BLOCKS, B], I32)
        dst_f = sb("dst_f", [P, BLOCKS, B])
        lasts = sb("lasts", [P, BLOCKS])
        before = sb("before", [P, BLOCKS])
        flags = sb("flags", [P, BLOCKS, 2])
        sel = sb("sel", [P, 2, P])
        ends = sb("ends", [P, 2, BLOCKS])
        first_f = sb("first_f", [P, BLOCKS])
        low_first = sb("low_first", [P, BLOCKS])
        tmp = sb("tmp", [P, BLOCKS])
        tmp2 = sb("tmp2", [P, BLOCKS])
        zeros = sb("zeros", [P, 3 * D], BF16)
        all_ones = sb("all_ones", [P, P])
        steps = sb("steps", [P, BLOCKS, B])
        faults = sb("faults", [P, BLOCKS, B])
        fault = sb("fault", [P, 2])
        fault_max = sb("fault_max", [P, 1])

        hT_ps = [ps(f"hT_ps{i}", [P, C, P]) for i in range(2)]
        kv_ps = [ps(f"kv_ps{i}", [P, 2 * D]) for i in range(2)]
        q_ps = [ps(f"q_ps{i}", [P, D]) for i in range(2)]
        ends_ps = ps("ends_ps", [P, 2, BLOCKS])
        fault_ps = ps("fault_ps", [P, 2])

        consts = sem("consts")
        weights_in = sem("weights_in")
        bias_scaled = sem("bias_scaled")
        lists_set = sem("lists_set")
        lists_in = sem("lists_in")
        x_in = [sem(f"x_in{i}") for i in range(2)]
        stats_got, mv_got, rstd_got, shift_got = sem("stats_got"), sem("mv_got"), sem("rstd_got"), sem("shift_got")
        std_got = sem("std_got")
        h_got, hT_put, h_hi_got, h_lo_got = sem("h_got"), sem("hT_put"), sem("h_hi_got"), sem("h_lo_got")
        w_hi_got, w_lo_got = sem("wp_hi_got"), sem("wp_lo_got")
        q_put, mm_done, kv_got, q_got = sem("q_put"), sem("mm_done"), sem("kv_got"), sem("q_got")
        hi_got, rest_got, mid_got, lo_got = sem("hi_got"), sem("rest_got"), sem("mid_got"), sem("lo_got")
        kv_out = [sem(f"kv_out{i}") for i in range(2)]
        q_out = [sem(f"q_out{i}") for i in range(2)]
        laid, fault_got = sem("laid"), sem("fault_got")
        zeros_set, zeros_out = sem("zeros_set"), sem("zeros_out")
        ends_put, lasts_got, before_in, flags_got, flags_out = (sem("ends_put"), sem("lasts_got"), sem("before_in"),
                                                                sem("flags_got"), sem("flags_out"))
        block = ctx.enter_context(nc.Block())

        @block.sync
        def _(sp):
            for c in range(C):
                sp.dma_start(w_all[:, c, 0:D], wq[c * P:(c + 1) * P, :]).then_inc(weights_in, 16)
                sp.dma_start(w_all[:, c, D:2 * D], wk[c * P:(c + 1) * P, :]).then_inc(weights_in, 16)
                sp.dma_start(w_all[:, c, 2 * D:3 * D], wv[c * P:(c + 1) * P, :]).then_inc(weights_in, 16)
            sp.dma_start(b_q[:, :], bq.partition_broadcast(P)).then_inc(weights_in, 16)
            sp.dma_start(b_kv[:, 0:D], bk.partition_broadcast(P)).then_inc(weights_in, 16)
            sp.dma_start(b_kv[:, D:2 * D], bv.partition_broadcast(P)).then_inc(weights_in, 16)

            def load_x(j, u):
                i = 2 * j + u
                wait(sp, h_got, i - 1)
                sp.nop(nofuse=True)
                sp.dma_start(xt[:, u, :], x[bass.ds(row0(i), P), :]).then_inc(x_in[u], 16)

            rounds(sp, load_x, TILES, 2)
            sp.wait_ge(zeros_set, 1)
            sp.dma_start(q_rows[N:N + P, :], zeros[:, :]).then_inc(zeros_out, 16)
            sp.wait_ge(zeros_out, 16)

        @block.gpsimd
        def _(pool):
            pool.iota(iota_row[:, :], [[1, P]], base=0, channel_multiplier=0,
                      allow_small_or_imprecise_dtypes=True).then_inc(consts, 1)
            pool.iota(iota_col[:, :], [[0, 1]], base=0, channel_multiplier=1,
                      allow_small_or_imprecise_dtypes=True).then_inc(consts, 1)

            def store(j, u):
                i = 2 * j + u
                if isinstance(i, int) and i == TILES - 1:
                    pool.wait_ge(kv_out[1 - u], 16 * (TILES // 2))
                    pool.wait_ge(q_out[1 - u], 16 * (TILES // 2))
                wait(pool, kv_got, i + 1)
                pool.dma_start(kv_rows[bass.ds(row0(i), P), :], kv[:, u, :]).then_inc(kv_out[u], 16)
                wait(pool, lo_got, i + 1)
                pool.dma_start(q_rows[bass.ds(row0(i), P), :], q3[:, u, :]).then_inc(q_out[u], 16)

            rounds(pool, store, TILES, 2)
            for u in range(2):
                pool.wait_ge(kv_out[u], 16 * (TILES // 2))
                pool.wait_ge(q_out[u], 16 * (TILES // 2))
            pool.wait_ge(lasts_got, 1)
            pool.dma_start(before[1:P, :], lasts[0:P - 1, :]).then_inc(before_in, 16)
            pool.dma_start(before[0:1, 1:BLOCKS], lasts[P - 1:P, 0:BLOCKS - 1]).then_inc(before_in, 16)
            pool.wait_ge(flags_got, 1)
            pool.dma_start(run_flags.rearrange("s (p j) -> p s j", j=2), flags[:, :, :]).then_inc(flags_out, 16)
            pool.wait_ge(flags_out, 16)

        @block.scalar
        def _(act):
            act.wait_ge(lists_set, 4)
            for tile, flat in ((dst_i, dst), (src_idx, src), (type_i, etype), (weight, eweight)):
                blocks = flat[0:FULL * P * B].rearrange("(s p b) -> p s b", p=P, b=B)
                act.dma_start(tile[:, 0:FULL, :], blocks).then_inc(lists_in, 16)
                tail = flat[FULL * P * B:FULL * P * B + TAIL_P * B].rearrange("(p b) -> p b", b=B)
                act.dma_start(tile[0:TAIL_P, FULL, :], tail).then_inc(lists_in, 16)
                if TAIL_B:
                    rest = flat[E - TAIL_B:E].rearrange("(p b) -> p b", p=1)
                    act.dma_start(tile[TAIL_P:TAIL_P + 1, FULL, 0:TAIL_B], rest).then_inc(lists_in, 16)

            def normalise(i, u):
                act.wait_ge(mv_got, i + 1)
                nc.scalar.activation(std[:, u:u + 1], mv[:, u, 1:2], ACT.Sqrt, bias=eps[:, 0:1],
                                     scale=1.0).then_inc(std_got, 1)
                act.wait_ge(shift_got, i + 1)
                wait(act, hT_put, i - 1)
                nc.scalar.activation(ht[:, u, :], xt[:, u, :], ACT.Relu, bias=shift[:, u:u + 1],
                                     scale=rstd[:, u:u + 1]).then_inc(h_got, 1)

            def high_part(i, u):
                act.wait_ge(hT_put, i + 1)
                wait(act, mm_done, i - 1)
                nc.scalar.copy(h_hi[:, u, :, :], hT_ps[u][:, :, :]).then_inc(h_hi_got, 1)

            act.wait_ge(weights_in, 16 * (3 * C + 3))
            nc.scalar.copy(w_hi[:, :, :], w_all[:, :, :]).then_inc(w_hi_got, 1)
            normalise(0, 0)
            high_part(0, 0)
            normalise(1, 1)

            def body(j, u):
                i = 2 * j + u
                if not (isinstance(i, int) and i == TILES - 1):
                    high_part(i + 1, 1 - u)
                if not (isinstance(i, int) and i >= TILES - 2):
                    normalise(i + 2, u)
                act.wait_ge(q_got, i + 1)
                if not isinstance(j, int) or j > 0:
                    act.wait_ge(q_out[u], 16 * j)
                nc.scalar.copy(q3[:, u, 0:D], qf[:, u, :]).then_inc(hi_got, 1)
                act.wait_ge(rest_got, i + 1)
                nc.scalar.copy(q3[:, u, D:2 * D], qf[:, u, :]).then_inc(mid_got, 1)

            rounds(act, body, TILES, 2)

        @block.tensor
        def _(pe):
            pe.wait_ge(consts, 4)

            def transposes(i, u):
                pe.wait_ge(h_got, i + 1)
                wait(pe, h_lo_got, i - 1)
                for c in range(C):
                    last = nc.tensor.transpose(hT_ps[u][:, c, :], ht[:, u, c * P:(c + 1) * P], ident[:, :])
                last.then_inc(hT_put, 1)

            def split_products(out, u, c, cols, start, stop):
                nc.tensor.matmul(out, h_hi[:, u, c, :], w_hi[:, c, cols], start=start, stop=False)
                nc.tensor.matmul(out, h_hi[:, u, c, :], w_lo[:, c, cols], start=False, stop=False)
                return nc.tensor.matmul(out, h_lo[:, u, c, :], w_hi[:, c, cols], start=False, stop=stop)

            def body(j, u):
                i = 2 * j + u
                if isinstance(i, int) and i == 0:
                    transposes(0, 0)
                    pe.wait_ge(w_lo_got, 1)
                pe.wait_ge(h_lo_got, i + 1)
                wait(pe, q_got, i - 1)
                split_products(q_ps[u][:, :], u, 0, slice(0, D), True, False)
                split_products(q_ps[u][:, :], u, 1, slice(0, D), False, True).then_inc(q_put, 1)
                wait(pe, kv_got, i - 1)
                split_products(kv_ps[u][:, :], u, 0, slice(D, 3 * D), True, False)
                if not (isinstance(i, int) and i == TILES - 1):
                    transposes(i + 1, 1 - u)
                split_products(kv_ps[u][:, :], u, 1, slice(D, 3 * D), False, True).then_inc(mm_done, 1)

            rounds(pe, body, TILES, 2)
            pe.wait_ge(laid, 3)
            nc.tensor.matmul(ends_ps[:, 0, :], sel[:, 0, :], dst_f[:, :, 0], start=True, stop=True)
            nc.tensor.matmul(ends_ps[:, 1, :], sel[:, 1, :], dst_f[:, :, B - 1], start=True,
                             stop=True).then_inc(ends_put, 1)
            pe.wait_ge(fault_got, 2)
            nc.tensor.matmul(fault_ps[:, :], all_ones[:, :], fault[:, :], start=True, stop=True).then_inc(ends_put, 1)

        @block.vector
        def _(dve):
            nc.vector.memset(eps[:, :], EPS).then_inc(consts, 1)
            nc.vector.memset(zeros[:, :], 0.0).then_inc(zeros_set, 1)
            nc.vector.memset(dst_i[:, :, :], PAD_NODE).then_inc(lists_set, 1)
            nc.vector.memset(src_idx[:, :, :], 0).then_inc(lists_set, 1)
            nc.vector.memset(type_i[:, :, :], 0).then_inc(lists_set, 1)
            nc.vector.memset(weight[:, :, :], 0.0).then_inc(lists_set, 1)
            dve.wait_ge(consts, 3)
            nc.vector.tensor_scalar(ident[:, :], iota_row[:, :], iota_col[:, 0:1], None,
                                    ALU.is_equal).then_inc(consts, 1)
            dve.wait_ge(weights_in, 16 * (3 * C + 3))
            nc.vector.tensor_scalar(b_q[:, :], b_q[:, :], HD ** -0.5, None, ALU.mult).then_inc(bias_scaled, 1)
            dve.wait_ge(bias_scaled, 1)

            def moments(i, j, u):
                dve.wait_ge(x_in[u], 16 * (j + 1))
                nc.vector.bn_stats(stats[:, u, :], xt[:, u, :]).then_inc(stats_got, 1)
                dve.wait_ge(stats_got, i + 1)
                dve.nop(nofuse=True)
                nc.vector.bn_aggr(mv[:, u, :], stats[:, u, :]).then_inc(mv_got, 1)

            def affine(i, u):
                dve.wait_ge(std_got, i + 1)
                wait(dve, h_got, i - 1)
                nc.vector.reciprocal(rstd[:, u:u + 1], std[:, u:u + 1]).then_inc(rstd_got, 1)
                dve.wait_ge(rstd_got, i + 1)
                nc.vector.scalar_tensor_tensor(shift[:, u:u + 1], mv[:, u, 0:1], -1.0, rstd[:, u:u + 1], ALU.mult,
                                               ALU.mult).then_inc(shift_got, 1)

            def low_part(i, u):
                dve.wait_ge(h_hi_got, i + 1)
                wait(dve, mm_done, i - 1)
                nc.vector.tensor_tensor(h_lo[:, u, :, :], hT_ps[u][:, :, :], h_hi[:, u, :, :].bitcast(F32),
                                        ALU.subtract).then_inc(h_lo_got, 1)

            dve.wait_ge(w_hi_got, 1)
            nc.vector.tensor_tensor(w_lo[:, :, :], w_all[:, :, :], w_hi[:, :, :].bitcast(F32),
                                    ALU.subtract).then_inc(w_lo_got, 1)
            moments(0, 0, 0)
            affine(0, 0)
            moments(1, 0, 1)
            low_part(0, 0)
            affine(1, 1)

            def body(j, u):
                i = 2 * j + u
                two_more = not (isinstance(i, int) and i >= TILES - 2)
                if two_more:
                    moments(i + 2, j + 1, u)
                dve.wait_ge(q_put, i + 1)
                wait(dve, lo_got, i - 1)
                nc.vector.scalar_tensor_tensor(qf[:, u, :], q_ps[u][:, :], HD ** -0.5, b_q[:, :], ALU.mult,
                                               ALU.add).then_inc(q_got, 1)
                if two_more:
                    affine(i + 2, u)
                dve.wait_ge(hi_got, i + 1)
                nc.vector.tensor_tensor(qf[:, u, :], qf[:, u, :], q3[:, u, 0:D], ALU.subtract).then_inc(rest_got, 1)
                if not (isinstance(i, int) and i == TILES - 1):
                    low_part(i + 1, 1 - u)
                dve.wait_ge(mm_done, i + 1)
                if not isinstance(j, int) or j > 0:
                    dve.wait_ge(kv_out[u], 16 * j)
                nc.vector.tensor_tensor(kv[:, u, :], kv_ps[u][:, :], b_kv[:, :], ALU.add).then_inc(kv_got, 1)
                dve.wait_ge(mid_got, i + 1)
                nc.vector.tensor_tensor(q3[:, u, 2 * D:3 * D], qf[:, u, :], q3[:, u, D:2 * D],
                                        ALU.subtract).then_inc(lo_got, 1)

            rounds(dve, body, TILES, 2)

            done = [0]

            def then(ins):
                done[0] += 1
                ins.then_inc(laid, 1)

            dve.wait_ge(lists_in, 16 * 4 * (3 if TAIL_B else 2))
            then(nc.vector.tensor_copy(dst_f[:, :, :], dst_i[:, :, :]))
            then(nc.vector.tensor_scalar(sel[:, 0, :], iota_col[:, 0:1].broadcast_to([P, P]), 0.0, None,
                                         ALU.is_equal))
            then(nc.vector.tensor_scalar(sel[:, 1, :], iota_col[:, 0:1].broadcast_to([P, P]), float(P - 1), None,
                                         ALU.is_equal))
            dve.wait_ge(laid, done[0])
            nc.vector.memset(before[0:1, 0:1], -1.0)
            nc.vector.tensor_copy(lasts[:, :], dst_f[:, :, B - 1]).then_inc(lasts_got, 1)
            then(nc.vector.scalar_tensor_tensor(msg_idx[:, :, :], src_idx[:, :, :], float(R), type_i[:, :, :],
                                                ALU.mult, ALU.add))
            first = dst_f[:, :, 0:1].broadcast_to([P, BLOCKS, B])
            final = dst_f[:, :, B - 1:B].broadcast_to([P, BLOCKS, B])
            then(nc.vector.tensor_tensor(new_run[:, :, 1:B], dst_f[:, :, 1:B], dst_f[:, :, 0:B - 1], ALU.not_equal))
            then(nc.vector.memset(new_run[:, :, 0:1], 1.0))
            then(nc.vector.tensor_tensor(not_first[:, :, :], dst_f[:, :, :], first, ALU.not_equal))
            then(nc.vector.tensor_tensor(not_last[:, :, :], dst_f[:, :, :], final, ALU.not_equal))
            dve.wait_ge(ends_put, 1)
            then(nc.vector.tensor_copy(ends[:, :, :], ends_ps[:, :, :]))
            dve.wait_ge(laid, done[0])
            for mask in (new_run, not_first, not_last):
                then(nc.vector.tensor_scalar(mask[:, :, :], mask[:, :, :], NEG, None, ALU.mult))
            then(nc.vector.tensor_scalar(first_f[:, :], ends[:, 0, :], float(N), None, ALU.min))
            then(nc.vector.tensor_scalar(low_first[:, :], ends[:, 0, :], float(N - P), None, ALU.min))
            dve.wait_ge(laid, done[0])
            then(nc.vector.tensor_copy(base[:, :], first_f[:, :]))
            then(nc.vector.tensor_copy(low_base[:, :], low_first[:, :]))
            wide = [P, BLOCKS, B]
            then(nc.vector.tensor_tensor(local[:, :, :], dst_f[:, :, :], first_f[:, :].unsqueeze(2).broadcast_to(wide),
                                         ALU.subtract))
            then(nc.vector.tensor_tensor(low_local[:, :, :], dst_f[:, :, :],
                                         low_first[:, :].unsqueeze(2).broadcast_to(wide), ALU.subtract))
            then(nc.vector.tensor_tensor(tmp[:, :], ends[:, 1, :], first_f[:, :], ALU.subtract))
            then(nc.vector.tensor_tensor(carry_row[:, 1:BLOCKS], ends[:, 1, 0:BLOCKS - 1], first_f[:, 1:BLOCKS],
                                         ALU.subtract))
            then(nc.vector.memset(carry_row[:, 0:1], -1.0))
            then(nc.vector.tensor_tensor(tmp2[:, 1:BLOCKS], low_first[:, 0:BLOCKS - 1], low_first[:, 1:BLOCKS],
                                         ALU.subtract))
            then(nc.vector.memset(tmp2[:, 0:1], 0.0))
            dve.wait_ge(laid, done[0])
            then(nc.vector.tensor_scalar(is_last[:, :], tmp[:, :], iota_col[:, 0:1], None, ALU.is_equal))
            then(nc.vector.tensor_scalar(low_shift[:, :], tmp2[:, :], iota_col[:, 0:1], None, ALU.add))
            dve.wait_ge(before_in, 32)
            then(nc.vector.tensor_tensor(flags[:, :, 0], before[:, :], dst_f[:, :, 0], ALU.not_equal))
            then(nc.vector.tensor_tensor(flags[:, :, 1], dst_f[:, :, 0], dst_f[:, :, B - 1], ALU.not_equal))
            dve.wait_ge(laid, done[0])
            nc.vector.tensor_scalar(flags[:, :, :], flags[:, :, :], NEG, None, ALU.mult).then_inc(flags_got, 1)

            then(nc.vector.tensor_scalar(dst_f[:, :, :], dst_f[:, :, :], float(N), None, ALU.min))
            then(nc.vector.tensor_scalar(before[:, :], before[:, :], float(N), None, ALU.min))
            then(nc.vector.memset(all_ones[:, :], 1.0))
            dve.wait_ge(laid, done[0])
            then(nc.vector.tensor_tensor(steps[:, :, 1:B], dst_f[:, :, 1:B], dst_f[:, :, 0:B - 1], ALU.subtract))
            then(nc.vector.tensor_tensor(steps[:, :, 0], dst_f[:, :, 0], before[:, :], ALU.subtract))
            then(nc.vector.scalar_tensor_tensor(tmp[:, :], dst_f[:, :, B - 1], float(N - 1), first_f[:, :],
                                                ALU.min, ALU.subtract))
            dve.wait_ge(laid, done[0])
            then(nc.vector.scalar_tensor_tensor(faults[:, :, :], steps[:, :, :], 1.0, steps[:, :, :], ALU.subtract,
                                                ALU.mult))
            then(nc.vector.tensor_scalar(tmp2[:, :], tmp[:, :], float(P - 1), None, ALU.is_gt))
            dve.wait_ge(laid, done[0])
            nc.vector.tensor_reduce(fault[:, 0:1], faults[:, :, :], AX.XY, ALU.max).then_inc(fault_got, 1)
            nc.vector.tensor_reduce(fault[:, 1:2], tmp2[:, :], AX.X, ALU.max).then_inc(fault_got, 1)
            dve.wait_ge(ends_put, 2)
            nc.vector.tensor_reduce(fault_max[:, :], fault_ps[:, :], AX.X, ALU.max).then_inc(fault_got, 1)
            dve.wait_ge(fault_got, 3)
            nc.vector.tensor_scalar(irregular[:, :], fault_max[:, :], 0.5, None, ALU.is_gt)


def attend(nc, q_rows, kv_rows, run_flags, agg_rows, ident, iota_row, src_idx, local, new_run, not_first, not_last,
           base, is_last, carry_row):
    with ExitStack() as ctx:
        def sb(name, shape, dt=F32):
            return ctx.enter_context(nc.sbuf_tensor(name, shape, dt))

        def ps(name, shape, dt=F32):
            return ctx.enter_context(nc.psum_tensor(name, shape, dt))

        def sem(name):
            return ctx.enter_context(nc.semaphore(name))

        kv = [sb(f"kvg{u}", [P, B, ROW]) for u in range(RING)]
        q_win = [sb(f"q_win{u}", [P, 3 * D], BF16) for u in range(RING)]
        onehot = [sb(f"onehot{u}", [P, B, P]) for u in range(RING)]
        index = [sb(f"index{u}", [P, B], I32) for u in range(RING)]
        rows_of = [sb(f"rows_of{u}", [P, B]) for u in range(RING)]
        one = sb("one", [P, 1])
        onehotT = sb("onehotT", [P, B, P], BF16)
        score = sb("score", [P, H, B])
        starts = sb("starts", [P, H * B + 1])
        run_fwd = sb("run_fwd", [P, H * B])
        run_max = sb("run_max", [P, H * B])
        list_flags = [sb(f"list_flags{u}", [H, 2 * P + 1]) for u in range(RING)]
        ends_max = sb("ends_max", [H, P, 2])
        list_fwd = sb("list_fwd", [H, RING, 2 * P])
        list_max = sb("list_max", [H, P, 2])
        seg_first = sb("seg_first", [P, H, B])
        seg_last = sb("seg_last", [P, H, B])
        seg_two = sb("seg_two", [P, H, B])
        seg_all = sb("seg_all", [P, H, B])
        arg = sb("arg", [P, H, B])
        drop = sb("drop", [H, 1])
        fade = sb("fade", [1, H])
        sums = [sb(f"sums{u}", [P, AGG]) for u in range(RING)]
        last_hot = [sb(f"last_hot{u}", [P, 1]) for u in range(RING)]
        carried = sb("carried", [1, AGG])
        carry_hot = sb("carry_hot", [1, P])

        qe_ps = [ps(f"qe_ps{i}", [P, 2, D]) for i in range(3)]
        oT_ps = [ps(f"oT_ps{i}", [P, 4, P]) for i in range(2)]
        sum_ps = ps("sum_ps", [P, AGG])
        small_ps = ps("small_ps", [P, 512])
        carry_ps = ps("carry_ps", [1, AGG])
        list_ps = small_ps[0:H, 0:2 * P].rearrange("h (j p) -> h j p", j=2)
        back_ps = small_ps[:, 256:272].rearrange("p (j h) -> p j h", j=2)
        drop_ps = small_ps[0:1, 288:288 + H]

        kv_in = [[sem(f"kv_in{u}_{half}") for half in range(2)] for u in range(RING)]
        q_in = [sem(f"q_in{u}") for u in range(RING)]
        flags_in = [sem(f"flags_in{u}") for u in range(RING)]
        index_in = [sem(f"index_in{u}") for u in range(RING)]
        agg_out = [sem(f"agg_out{u}") for u in range(RING)]
        one_set, rows_got, dist_got, onehot_got = sem("one_set"), sem("rows_got"), sem("dist_got"), sem("onehot_got")
        oT_put, oT_got, qe_put, prod_got = sem("oT_put"), sem("oT_got"), sem("qe_put"), sem("prod_got")
        starts_set, starts_got = sem("starts_set"), sem("starts_got")
        score_got, fwd_got, run_got = sem("score_got"), sem("fwd_got"), sem("run_got")
        list_put, list_got, lfwd_got, lmax_got = sem("list_put"), sem("list_got"), sem("lfwd_got"), sem("lmax_got")
        drop_got, back_put = sem("drop_got"), sem("back_put")
        segs_got, two_got, all_got, arg_got = sem("segs_got"), sem("two_got"), sem("all_got"), sem("arg_got")
        exp_got, fade_got, ev_got = sem("exp_got"), sem("fade_got"), sem("ev_got")
        half_done, agg_done, sums_got, last_hot_got = (sem("half_done"), sem("agg_done"), sem("sums_got"),
                                                       sem("last_hot_got"))
        carry_put, hot_got, carried_got = sem("carry_put"), sem("hot_got"), sem("carried_got")
        block = ctx.enter_context(nc.Block())
        GROUPS = len(OHG)
        LAST = BLOCKS - 1
        LAST_SLOT, LAST_ROUND = LAST % RING, LAST // RING
        halves = (range(0, PAIRS), range(PAIRS, B))
        parts = (range(0, 4), range(4, PAIRS), range(PAIRS, 11), range(11, B))

        def at(i, n):
            return isinstance(i, int) and i == n

        @block.sync
        def _(sp):
            def store(i, j, u):
                wait(sp, sums_got, i + 1)
                sp.nop(nofuse=True)
                if at(i, 0):
                    pass
                else:
                    _, up, jp = step(j, u, -1)
                    wait(sp, agg_out[up], 16 * (jp + 1))
                    sp.nop(nofuse=True)
                first = sp.value_load(base[0:1, bass.ds(i, 1)], min_val=0, max_val=N)
                sp.dma_start(agg_rows[bass.ds(first, P), :], sums[u][:, :]).then_inc(agg_out[u], 16)

            def body(j, u):
                i, _, _ = step(j, u)
                wait(sp, kv_in[u][1], 16 * PAIRS * j)
                sp.nop(nofuse=True)
                sp.dma_start(index[u][:, :], src_idx[:, :, :].rearrange("p s b -> p (s b)")[:, bass.ds(i * B, B)]
                             ).then_inc(index_in[u], 16)
                wait(sp, lmax_got, i - 2)
                sp.nop(nofuse=True)
                sp.dma_start(list_flags[u][:, 0:2 * P],
                             run_flags[bass.ds(i, 1), :].broadcast_to([H, 2 * P])).then_inc(flags_in[u], 16)
                wait(sp, qe_put, PAIRS * (i - 2))
                sp.nop(nofuse=True)
                first = sp.value_load(base[0:1, bass.ds(i, 1)], min_val=0, max_val=N)
                sp.dma_start(q_win[u][:, :], q_rows[bass.ds(first, P), :]).then_inc(q_in[u], 16)
                if not isinstance(i, int) or i >= RING:
                    store(i - RING, j - 1, u)

            sp.wait_ge(starts_set, 2 + RING)
            rounds(sp, body, BLOCKS, RING)
            for i in range(BLOCKS - RING, BLOCKS):
                store(i, i // RING, i % RING)
            for u in range(RING):
                sp.wait_ge(agg_out[u], 16 * len(range(u, BLOCKS, RING)))

        @block.gpsimd
        def _(pool):
            def body(j, u):
                i, _, _ = step(j, u)
                pool.wait_ge(index_in[u], 16 * (j + 1))
                pool.nop(nofuse=True)
                for half in range(2):
                    wait(pool, agg_done if half else half_done, i - 2)
                    pool.nop(nofuse=True)
                    for t in halves[half]:
                        pool.indirect_dma_start(
                            out=kv[u][:, t, 0:2 * D], out_offset=None, in_=kv_rows,
                            in_offset=bass.IndirectOffsetOnAxis(ap=index[u][:, t:t + 1],
                                                                axis=0)).then_inc(kv_in[u][half], 16)

            rounds(pool, body, BLOCKS, RING)

        @block.vector
        def _(dve):
            nc.vector.memset(one[:, :], 1.0).then_inc(one_set, 1)
            nc.vector.memset(starts[:, :], NEG).then_inc(starts_set, 1)
            for u in range(RING):
                nc.vector.memset(list_flags[u][:, :], NEG).then_inc(starts_set, 1)
            nc.vector.memset(list_fwd[:, :, :], 0.0).then_inc(starts_set, 1)
            dve.wait_ge(starts_set, 2 + RING)

            def product(i, j, u, pair):
                if pair in (0, PAIRS // 2):
                    dve.wait_ge(kv_in[u][pair > 0], 16 * PAIRS * (j + 1))
                wait(dve, qe_put, PAIRS * i + pair + 1)
                k = kv[u][:, 2 * pair:2 * pair + 2, 0:D]
                nc.vector.tensor_tensor(k, k, qe_ps[(PAIRS * u + pair) % 3][:, :, :], ALU.mult).then_inc(prod_got, 1)

            def run_maxima(i, u):
                dve.wait_ge(prod_got, PAIRS * (i + 1))
                wait(dve, arg_got, i)
                nc.vector.tensor_reduce(score[:, :, :], kv[u][:, :, 0:D].rearrange("p t (d h) -> p h t d", h=H), AX.X,
                                        ALU.add).then_inc(score_got, 1)
                flat = score[:, :, :].rearrange("p h t -> p (h t)")
                dve.wait_ge(score_got, i + 1)
                dve.wait_ge(starts_got, i + 1)
                wait(dve, run_got, i)
                nc.vector.tensor_tensor_scan(run_fwd[:, :], starts[:, 0:H * B], flat, 0.0, ALU.add,
                                             ALU.max).then_inc(fwd_got, 1)
                dve.wait_ge(fwd_got, i + 1)
                wait(dve, list_put, i)
                nc.vector.tensor_tensor_scan(run_max[:, ::-1], starts[:, 1:H * B + 1][:, ::-1], run_fwd[:, ::-1], 0.0,
                                             ALU.add, ALU.max).then_inc(run_got, 1)

            def border_forward(i, j, u):
                dve.wait_ge(flags_in[u], 16 * (j + 1))
                dve.wait_ge(list_got, i + 1)
                ends = ends_max[:, :, :].rearrange("h p j -> h (p j)")
                nc.vector.tensor_tensor_scan(list_fwd[:, u, :], list_flags[u][:, 0:2 * P], ends,
                                             list_fwd[:, (u - 1) % RING, 2 * P - 1:2 * P], ALU.add,
                                             ALU.max).then_inc(lfwd_got, 1)

            def border_backward(i, u):
                lmax = list_max[:, :, :].rearrange("h p j -> h (p j)")
                dve.wait_ge(lfwd_got, i + 1)
                wait(dve, back_put, i)
                nc.vector.tensor_tensor_scan(lmax[:, ::-1], list_flags[u][:, 1:2 * P + 1][:, ::-1],
                                             list_fwd[:, u, ::-1], 0.0, ALU.add, ALU.max).then_inc(lmax_got, 1)

            def border_drop(i, u):
                dve.wait_ge(lmax_got, i + 1)
                nc.vector.tensor_scalar(drop[:, :], list_fwd[:, (u - 1) % RING, 2 * P - 1:2 * P],
                                        list_max[:, 0, 0:1], 0.0, ALU.subtract, ALU.min).then_inc(drop_got, 1)

            def seg_borders(i):
                dve.wait_ge(back_put, i + 1)
                wide = [P, H, B]
                mine = bass.ds(i, 1)
                nc.vector.tensor_tensor(seg_first[:, :, :], back_ps[:, 0, :].unsqueeze(2).broadcast_to(wide),
                                        not_first[:, mine, :].broadcast_to(wide), ALU.add).then_inc(segs_got, 1)
                nc.vector.tensor_tensor(seg_last[:, :, :], back_ps[:, 1, :].unsqueeze(2).broadcast_to(wide),
                                        not_last[:, mine, :].broadcast_to(wide), ALU.add).then_inc(segs_got, 1)

            def seg_either(i):
                dve.wait_ge(segs_got, 2 * (i + 1))
                nc.vector.tensor_tensor(seg_two[:, :, :], seg_first[:, :, :], seg_last[:, :, :],
                                        ALU.max).then_inc(two_got, 1)

            def seg_maxima(i):
                dve.wait_ge(two_got, i + 1)
                nc.vector.tensor_tensor(seg_all[:, :, :], seg_two[:, :, :],
                                        run_max[:, :].rearrange("p (h t) -> p h t", h=H), ALU.max).then_inc(all_got, 1)

            def exponents(i):
                dve.wait_ge(all_got, i + 1)
                wait(dve, exp_got, i)
                nc.vector.tensor_tensor(arg[:, :, :], score[:, :, :], seg_all[:, :, :],
                                        ALU.subtract).then_inc(arg_got, 1)

            def weigh(i, u):
                wait(dve, exp_got, i + 1)
                for part in parts:
                    rows = slice(part[0], part[-1] + 1)
                    v = kv[u][:, rows, D:2 * D].rearrange("p t (d h) -> p t d h", h=H)
                    e = kv[u][:, rows, 2 * D:ROW].unsqueeze(2).broadcast_to([P, len(part), HD, H])
                    nc.vector.tensor_tensor(v, v, e, ALU.mult).then_inc(ev_got, 1)

            def carry(i):
                wait(dve, agg_done, i)
                nc.vector.tensor_scalar(carry_hot[0:1, :], iota_row[0:1, :], carry_row[0:1, bass.ds(i, 1)], None,
                                        ALU.is_equal).then_inc(hot_got, 1)
                wait(dve, fade_got, i + 1)
                wait(dve, carry_put, i)
                nc.vector.tensor_tensor(
                    carried[:, :].rearrange("o (d h) -> o d h", h=H), carry_ps[:, :].rearrange("o (d h) -> o d h", h=H),
                    fade[:, :].unsqueeze(1).broadcast_to([1, AGG // H, H]), ALU.mult).then_inc(carried_got, 1)

            def body(j, u):
                i, _, _ = step(j, u)
                ip, up, jp = step(j, u, -1)
                for pair in range(PAIRS):
                    product(i, j, u, pair)
                    if at(i, 0):
                        continue
                    if pair == 1:
                        border_forward(ip, jp, up)
                    elif pair == 2:
                        border_backward(ip, up)
                        border_drop(ip, up)
                    elif pair == 3:
                        seg_borders(ip)
                    elif pair == 4:
                        seg_either(ip)
                        seg_maxima(ip)
                    elif pair == 5:
                        exponents(ip)
                if not at(i, 0):
                    weigh(ip, up)
                    if not at(i, 1):
                        carry(ip)
                run_maxima(i, u)

            rounds(dve, body, BLOCKS, RING)
            border_forward(LAST, LAST_ROUND, LAST_SLOT)
            border_backward(LAST, LAST_SLOT)
            border_drop(LAST, LAST_SLOT)
            seg_borders(LAST)
            seg_either(LAST)
            seg_maxima(LAST)
            exponents(LAST)
            weigh(LAST, LAST_SLOT)
            carry(LAST)

        @block.scalar
        def _(act):
            def onehots(i, u, half):
                tiles = halves[half]
                if half == 0:
                    nc.scalar.copy(rows_of[u][:, :].unsqueeze(1), local[:, bass.ds(i, 1), :]).then_inc(rows_got, 1)
                    wait(act, rows_got, i + 1)
                wait(act, agg_done if half else half_done, i - 2)
                for t in tiles:
                    last = nc.scalar.activation(onehot[u][:, t, :], iota_row[:, :], ACT.Abs,
                                                bias=rows_of[u][:, t:t + 1], scale=-1.0)
                last.then_inc(dist_got, 1)
                wait(act, dist_got, 2 * i + half + 1)
                mine = onehot[u][:, tiles[0]:tiles[-1] + 1, :]
                nc.scalar.activation(mine, mine, ACT.Relu, bias=one[:, 0:1], scale=-1.0).then_inc(onehot_got, 1)

            def transposed(i):
                for g, tiles in enumerate(OHG):
                    first = sum(OHG[:g])
                    wait(act, oT_put, GROUPS * i + g + 1)
                    if g == 0:
                        wait(act, qe_put, PAIRS * i)
                    nc.scalar.copy(onehotT[:, first:first + tiles, :],
                                   oT_ps[g % 2][:, 0:tiles, :]).then_inc(oT_got, 1)

            def take_sums(i, j, u):
                wait(act, agg_done, i + 1)
                if not isinstance(j, int) or j > 0:
                    act.wait_ge(agg_out[u], 16 * j)
                wait(act, carry_put, i - 2)
                nc.scalar.copy(sums[u][:, :], sum_ps[:, :]).then_inc(sums_got, 1)
                nc.scalar.copy(last_hot[u][:, :], is_last[:, bass.ds(i, 1)]).then_inc(last_hot_got, 1)

            def list_out(i):
                act.wait_ge(list_put, i + 1)
                wait(act, lfwd_got, i)
                nc.scalar.copy(ends_max[:, :, :].rearrange("h p j -> h j p"), list_ps).then_inc(list_got, 1)

            def exponentials(i, u):
                act.wait_ge(arg_got, i + 1)
                nc.scalar.activation(kv[u][:, :, 2 * D:ROW].rearrange("p t h -> p h t"), arg[:, :, :],
                                     ACT.Exp).then_inc(exp_got, 1)
                wait(act, carried_got, i - 1)
                nc.scalar.activation(fade[:, :], drop_ps, ACT.Exp).then_inc(fade_got, 1)

            def run_starts(i):
                wait(act, run_got, i)
                nc.scalar.copy(starts[:, 0:H * B].rearrange("p (h t) -> p h t", h=H),
                               new_run[:, bass.ds(i, 1), :].broadcast_to([P, H, B])).then_inc(starts_got, 1)

            def body(j, u):
                i, _, _ = step(j, u)
                if at(i, 0):
                    act.wait_ge(one_set, 1)
                    act.wait_ge(starts_set, 2 + RING)
                    onehots(0, 0, 0)
                    onehots(0, 0, 1)
                    transposed(0)
                    run_starts(0)
                    onehots(1, 1, 0)
                else:
                    ip, up, _ = step(j, u, -1)
                    list_out(ip)
                    if not at(i, 1):
                        i2, u2, j2 = step(j, u, -2)
                        take_sums(i2, j2, u2)
                    run_starts(i)
                i1, u1, _ = step(j, u, 1)
                i2, u2, _ = step(j, u, 2)
                if not at(i, LAST):
                    onehots(i1, u1, 1)
                if not at(i, 0):
                    exponentials(ip, up)
                if not at(i, LAST):
                    transposed(i1)
                if not at(i, LAST) and not at(i, LAST - 1):
                    onehots(i2, u2, 0)

            rounds(act, body, BLOCKS, RING)
            list_out(LAST)
            take_sums(LAST - 1, (LAST - 1) // RING, (LAST - 1) % RING)
            exponentials(LAST, LAST_SLOT)
            take_sums(LAST, LAST_ROUND, LAST_SLOT)

        @block.tensor
        def _(pe):
            def transpose_onehot(i, u):
                wait(pe, onehot_got, 2 * (i + 1))
                for g, tiles in enumerate(OHG):
                    wait(pe, oT_got, GROUPS * i + g - 1)
                    for t in range(tiles):
                        last = nc.tensor.transpose(oT_ps[g % 2][:, t, :], onehot[u][:, sum(OHG[:g]) + t, :],
                                                   ident[:, :])
                    last.then_inc(oT_put, 1)

            def expand_q(i, j, u, pairs):
                for pair in pairs:
                    if pair == 0:
                        pe.wait_ge(q_in[u], 16 * (j + 1))
                    wait(pe, prod_got, PAIRS * i + pair - 2)
                    wait(pe, oT_got, GROUPS * i + (2 * pair + 1) // 4 + 1)
                    for t in range(2):
                        for part in range(3):
                            last = nc.tensor.matmul(qe_ps[(PAIRS * u + pair) % 3][:, t, :], onehotT[:, 2 * pair + t, :],
                                                    q_win[u][:, part * D:(part + 1) * D], start=part == 0,
                                                    stop=part == 2)
                    last.then_inc(qe_put, 1)

            def add_tiles(i, u):
                for n, part in enumerate(parts):
                    wait(pe, ev_got, len(parts) * i + n + 1)
                    if n == 0:
                        wait(pe, sums_got, i)
                    for t in part:
                        last = nc.tensor.matmul(sum_ps[:, :], onehot[u][:, t, :], kv[u][:, t, D:ROW], start=t == 0,
                                                stop=t == B - 1 and at(i, 0))
                        if t == PAIRS - 1:
                            last.then_inc(half_done, 1)
                if at(i, 0):
                    last.then_inc(agg_done, 1)
                else:
                    wait(pe, hot_got, i)
                    wait(pe, carried_got, i)
                    nc.tensor.matmul(sum_ps[:, :], carry_hot[0:1, :], carried[0:1, :], start=False,
                                     stop=True).then_inc(agg_done, 1)

            def take_carry(i, u):
                wait(pe, sums_got, i + 1)
                wait(pe, last_hot_got, i + 1)
                wait(pe, carried_got, i)
                nc.tensor.matmul(carry_ps[:, :], last_hot[u][:, :], sums[u][:, :], start=True,
                                 stop=True).then_inc(carry_put, 1)

            def list_transposes(i):
                wait(pe, run_got, i + 1)
                wait(pe, list_got, i)
                wait(pe, segs_got, 2 * i)
                wait(pe, fade_got, i)
                runs = run_max[:, :].rearrange("p (h t) -> p h t", h=H)
                nc.tensor.transpose(list_ps[:, 0, :], runs[:, :, 0], ident[:, :])
                nc.tensor.transpose(list_ps[:, 1, :], runs[:, :, B - 1], ident[:, :]).then_inc(list_put, 1)

            def back_transposes(i):
                wait(pe, lmax_got, i + 1)
                wait(pe, drop_got, i + 1)
                pe.nop(nofuse=True)
                nc.tensor.matmul(drop_ps, drop[:, :], ident[0:H, 0:H], start=True, stop=True)
                nc.tensor.transpose(back_ps[:, 0, :], list_max[:, :, 0], ident[0:H, 0:H])
                nc.tensor.transpose(back_ps[:, 1, :], list_max[:, :, 1], ident[0:H, 0:H]).then_inc(back_put, 1)

            def body(j, u):
                i, _, _ = step(j, u)
                if at(i, 0):
                    transpose_onehot(0, 0)
                    expand_q(0, 0, 0, range(PAIRS))
                    transpose_onehot(1, 1)
                    return
                ip, up, _ = step(j, u, -1)
                expand_q(i, j, u, range(0, 1))
                list_transposes(ip)
                expand_q(i, j, u, range(1, 4))
                back_transposes(ip)
                expand_q(i, j, u, range(4, PAIRS))
                if not at(i, 1):
                    i2, u2, _ = step(j, u, -2)
                    take_carry(i2, u2)
                if not at(i, LAST):
                    i2, u2, _ = step(j, u, 1)
                    transpose_onehot(i2, u2)
                add_tiles(ip, up)

            rounds(pe, body, BLOCKS, RING)
            list_transposes(LAST)
            back_transposes(LAST)
            take_carry(LAST - 1, (LAST - 1) % RING)
            add_tiles(LAST, LAST_SLOT)


def messages(nc, x, agg_rows, wo, bo, wrel, wgate, x1_rows, msg_rows, ident, eps):
    with ExitStack() as ctx:
        def sb(name, shape, dt=F32):
            return ctx.enter_context(nc.sbuf_tensor(name, shape, dt))

        def ps(name, shape, dt=F32):
            return ctx.enter_context(nc.psum_tensor(name, shape, dt))

        def sem(name):
            return ctx.enter_context(nc.semaphore(name))

        w_o = sb("w_o", [P, C, D])
        b_o = sb("b_o", [P, D])
        w_hi = sb("w_hi", [P, C, R, D], F32R)
        w_lo = sb("w_lo", [P, C, R, D], F32R)
        gate_w = sb("gate_w", [P, C, R])
        gate_hi = sb("gate_hi", [P, C, R], F32R)
        gate_lo = sb("gate_lo", [P, C, R], F32R)
        agg = sb("agg", [P, 2, AGG])
        xt = sb("xt1", [P, 2, D])
        inv = sb("inv", [P, 2, H])
        att = sb("att", [P, D])
        xb = sb("xb", [P, D])
        attT = sb("attT", [P, C, P])
        x1 = sb("x1", [P, 2, D])
        stats = sb("stats1", [P, 6])
        mv = sb("mv1", [P, 2])
        std = sb("std1", [P, 1])
        rstd = sb("rstd1", [P, 1])
        shift = sb("shift1", [P, 1])
        ht = sb("ht1", [P, D])
        h_hi = sb("h_hi", [P, 2, C, P], F32R)
        h_lo = sb("h_lo", [P, 2, C, P], F32R)
        gate = sb("gate", [P, 2, R])
        msg = sb("msg", [P, 2, R, D])

        big_ps = [ps(f"big_ps{i}", [P, 2, D]) for i in range(4)]
        attT_ps = ps("attT_ps", [P, C, P])
        hT_ps = ps("hiddenT_ps", [P, C, P])
        o_ps = ps("o_ps", [P, D])
        gate_ps = ps("gate_ps", [P, R])

        weights_in = sem("weights_in1")
        rel_in = [sem(f"rel_in{c}") for c in range(C)]
        w_hi_got, w_lo_got = sem("w_hi_got"), sem("w_lo_got")
        agg_in = [sem(f"agg_in{u}") for u in range(2)]
        inv0_got, inv_got, att_got, xb_got, x1_got = (sem("inv0_got"), sem("inv_got"), sem("att_got"), sem("xb_got"),
                                                      sem("x1_got"))
        attT_put, attT_got, o_put = sem("attT_put"), sem("attT_got"), sem("o_put")
        stats_got, mv_got, std_got, rstd_got, shift_got = (sem("stats_got1"), sem("mv_got1"), sem("std_got1"),
                                                           sem("rstd_got1"), sem("shift_got1"))
        h_got, hT_put, hi_got, lo_got = sem("h_got1"), sem("hT_put1"), sem("hi_got1"), sem("lo_got1")
        gate_put, gate_got = sem("gate_put"), sem("gate_got")
        big_put, even_got, odd_got = sem("big_put"), sem("even_got"), sem("odd_got")
        x1_out = [sem(f"x1_out{u}") for u in range(2)]
        msg_out = [sem(f"msg_out{u}") for u in range(2)]
        block = ctx.enter_context(nc.Block())
        G = R // 2
        msg_view = msg_rows.rearrange("(n r) d -> n r d", r=R)

        def at(i, n):
            return isinstance(i, int) and i == n

        @block.gpsimd
        def _(pool):
            pool.dma_start(w_o[:, :, :], wo.rearrange("(c p) d -> p c d", p=P)).then_inc(weights_in, 16)
            pool.dma_start(b_o[:, :], bo.partition_broadcast(P)).then_inc(weights_in, 16)
            pool.dma_start(gate_w[:, :, :], wgate.rearrange("(c p) r -> p c r", p=P)).then_inc(weights_in, 16)

            def load(j, u):
                i = 2 * j + u
                wait(pool, x1_got, i - 1)
                pool.nop(nofuse=True)
                pool.dma_start(agg[:, u, :], agg_rows[bass.ds(row0(i), P), :]).then_inc(agg_in[u], 16)
                pool.dma_start(xt[:, u, :], x[bass.ds(row0(i), P), :]).then_inc(agg_in[u], 16)

            rounds(pool, load, TILES, 2)

        @block.sync
        def _(sp):
            for c in range(C):
                sp.dma_start(msg[:, c, :, :],
                             wrel[:, c * P:(c + 1) * P, :].rearrange("r p d -> p r d")).then_inc(rel_in[c], 16)

            def store(j, u):
                i = 2 * j + u
                if at(i, TILES - 1):
                    sp.wait_ge(x1_out[1 - u], 16 * (TILES // 2))
                    sp.wait_ge(msg_out[1 - u], 32 * (TILES // 2))
                sp.wait_ge(x1_got, i + 1)
                sp.nop(nofuse=True)
                sp.dma_start(x1_rows[bass.ds(row0(i), P), :], x1[:, u, :]).then_inc(x1_out[u], 16)
                for half in range(2):
                    rels = slice(half * R // 2, (half + 1) * R // 2)
                    sp.wait_ge(even_got, G // 2 * i + (half + 1) * G // 4)
                    sp.wait_ge(odd_got, G // 2 * i + (half + 1) * G // 4)
                    sp.nop(nofuse=True)
                    sp.dma_start(msg_view[bass.ds(row0(i), P), rels, :], msg[:, u, rels, :]).then_inc(msg_out[u], 16)

            rounds(sp, store, TILES, 2)
            for u in range(2):
                sp.wait_ge(x1_out[u], 16 * (TILES // 2))
                sp.wait_ge(msg_out[u], 32 * (TILES // 2))

        @block.vector
        def _(dve):
            def attention(i, j, u):
                dve.wait_ge(agg_in[u], 32 * (j + 1))
                nc.vector.tensor_scalar(inv[:, u, :], agg[:, u, D:AGG], TINY, None, ALU.max).then_inc(inv0_got, 1)
                dve.wait_ge(inv0_got, i + 1)
                nc.vector.reciprocal(inv[:, u, :], inv[:, u, :]).then_inc(inv_got, 1)
                dve.wait_ge(inv_got, i + 1)
                wait(dve, attT_put, i)
                nc.vector.tensor_tensor(
                    att[:, :].rearrange("p (d h) -> p d h", h=H), agg[:, u, 0:D].rearrange("p (d h) -> p d h", h=H),
                    inv[:, u, :].unsqueeze(1).broadcast_to([P, HD, H]), ALU.mult).then_inc(att_got, 1)
                wait(dve, x1_got, i)
                nc.vector.tensor_tensor(xb[:, :], xt[:, u, :], b_o[:, :], ALU.add).then_inc(xb_got, 1)

            def residual(i, j, u):
                dve.wait_ge(xb_got, i + 1)
                dve.wait_ge(o_put, i + 1)
                wait(dve, h_got, i - 1)
                if not isinstance(j, int) or j > 0:
                    dve.wait_ge(x1_out[u], 16 * j)
                nc.vector.tensor_tensor(x1[:, u, :], o_ps[:, :], xb[:, :], ALU.add).then_inc(x1_got, 1)
                dve.wait_ge(x1_got, i + 1)
                nc.vector.bn_stats(stats[:, :], x1[:, u, :]).then_inc(stats_got, 1)
                dve.wait_ge(stats_got, i + 1)
                dve.nop(nofuse=True)
                nc.vector.bn_aggr(mv[:, :], stats[:, :]).then_inc(mv_got, 1)

            def affine(i):
                dve.wait_ge(std_got, i + 1)
                wait(dve, h_got, i)
                nc.vector.reciprocal(rstd[:, :], std[:, :]).then_inc(rstd_got, 1)
                dve.wait_ge(rstd_got, i + 1)
                nc.vector.scalar_tensor_tensor(shift[:, :], mv[:, 0:1], -1.0, rstd[:, :], ALU.mult,
                                               ALU.mult).then_inc(shift_got, 1)

            def low_part(i, u):
                dve.wait_ge(hi_got, i + 1)
                wait(dve, big_put, G * (i - 1))
                nc.vector.tensor_tensor(h_lo[:, u, :, :], hT_ps[:, :, :], h_hi[:, u, :, :].bitcast(F32),
                                        ALU.subtract).then_inc(lo_got, 1)

            def scaled(i, u, g):
                wait(dve, big_put, G * i + g + 1)
                for rel in (2 * g, 2 * g + 1):
                    last = nc.vector.tensor_scalar(msg[:, u, rel, :], big_ps[g % 4][:, rel % 2, :],
                                                   gate[:, u, rel:rel + 1], None, ALU.mult)
                last.then_inc(odd_got, 1)

            def body(j, u):
                i = 2 * j + u
                more = not at(i, TILES - 1)
                i1, j1, u1 = i + 1, j if u == 0 else j + 1, 1 - u
                if more:
                    attention(i1, j1, u1)
                dve.wait_ge(gate_got, i + 1)
                if not isinstance(j, int) or j > 0:
                    dve.wait_ge(msg_out[u], 32 * j)
                scaled(i, u, 1)
                if more:
                    residual(i1, j1, u1)
                scaled(i, u, 3)
                if more:
                    affine(i1)
                scaled(i, u, 5)
                if more:
                    low_part(i1, u1)
                scaled(i, u, 7)

            dve.wait_ge(weights_in, 48)
            attention(0, 0, 0)
            for c in range(C):
                dve.wait_ge(w_hi_got, c + 1)
                nc.vector.tensor_tensor(w_lo[:, c, :, :], msg[:, c, :, :], w_hi[:, c, :, :].bitcast(F32),
                                        ALU.subtract).then_inc(w_lo_got, 1)
            dve.wait_ge(w_hi_got, C + 1)
            nc.vector.tensor_tensor(gate_lo[:, :, :], gate_w[:, :, :], gate_hi[:, :, :].bitcast(F32),
                                    ALU.subtract).then_inc(w_lo_got, 1)
            dve.wait_ge(w_lo_got, C + 1)
            residual(0, 0, 0)
            affine(0)
            low_part(0, 0)
            rounds(dve, body, TILES, 2)

        @block.scalar
        def _(act):
            def attention_turned(i):
                act.wait_ge(attT_put, i + 1)
                wait(act, o_put, i)
                nc.scalar.copy(attT[:, :, :], attT_ps[:, :, :]).then_inc(attT_got, 1)

            def hidden(i, u):
                act.wait_ge(mv_got, i + 1)
                nc.scalar.activation(std[:, :], mv[:, 1:2], ACT.Sqrt, bias=eps[:, 0:1], scale=1.0).then_inc(std_got, 1)
                act.wait_ge(shift_got, i + 1)
                wait(act, hT_put, i)
                nc.scalar.activation(ht[:, :], x1[:, u, :], ACT.Relu, bias=shift[:, 0:1],
                                     scale=rstd[:, 0:1]).then_inc(h_got, 1)

            def high_part(i, u):
                act.wait_ge(hT_put, i + 1)
                wait(act, big_put, G * (i - 1))
                nc.scalar.copy(h_hi[:, u, :, :], hT_ps[:, :, :]).then_inc(hi_got, 1)

            def gates(i, u):
                act.wait_ge(gate_put, i + 1)
                wait(act, odd_got, G // 2 * (i - 1))
                nc.scalar.activation(gate[:, u, :], gate_ps[:, :], ACT.Sigmoid).then_inc(gate_got, 1)

            def scaled(i, u, g):
                wait(act, big_put, G * i + g + 1)
                for rel in (2 * g, 2 * g + 1):
                    last = nc.scalar.activation(msg[:, u, rel, :], big_ps[g % 4][:, rel % 2, :], ACT.Copy,
                                                scale=gate[:, u, rel:rel + 1])
                last.then_inc(even_got, 1)

            def body(j, u):
                i = 2 * j + u
                more = not at(i, TILES - 1)
                i1, u1 = i + 1, 1 - u
                act.wait_ge(gate_got, i + 1)
                if not isinstance(j, int) or j > 0:
                    act.wait_ge(msg_out[u], 32 * j)
                scaled(i, u, 0)
                if more:
                    attention_turned(i1)
                scaled(i, u, 2)
                if more:
                    hidden(i1, u1)
                scaled(i, u, 4)
                if more:
                    high_part(i1, u1)
                scaled(i, u, 6)
                if more:
                    gates(i1, u1)

            for c in range(C):
                act.wait_ge(rel_in[c], 16)
                nc.scalar.copy(w_hi[:, c, :, :], msg[:, c, :, :]).then_inc(w_hi_got, 1)
            act.wait_ge(weights_in, 48)
            nc.scalar.copy(gate_hi[:, :, :], gate_w[:, :, :]).then_inc(w_hi_got, 1)
            attention_turned(0)
            hidden(0, 0)
            high_part(0, 0)
            gates(0, 0)
            act.wait_ge(w_lo_got, C + 1)
            rounds(act, body, TILES, 2)

        @block.tensor
        def _(pe):
            def attention_turned(i):
                pe.wait_ge(att_got, i + 1)
                wait(pe, attT_got, i)
                for c in range(C):
                    last = nc.tensor.transpose(attT_ps[:, c, :], att[:, c * P:(c + 1) * P], ident[:, :])
                last.then_inc(attT_put, 1)

            def output(i):
                pe.wait_ge(attT_got, i + 1)
                wait(pe, x1_got, i)
                for c in range(C):
                    last = nc.tensor.matmul(o_ps[:, :], attT[:, c, :], w_o[:, c, :], start=c == 0, stop=c == C - 1)
                last.then_inc(o_put, 1)

            def hidden_turned(i):
                pe.wait_ge(h_got, i + 1)
                wait(pe, lo_got, i)
                for c in range(C):
                    last = nc.tensor.transpose(hT_ps[:, c, :], ht[:, c * P:(c + 1) * P], ident[:, :])
                last.then_inc(hT_put, 1)

            def split_products(out, u, hi, lo):
                n = 0
                for c in range(C):
                    for h, w in ((h_hi, hi), (h_hi, lo), (h_lo, hi)):
                        last = nc.tensor.matmul(out, h[:, u, c, :], w(c), start=n == 0, stop=n == 3 * C - 1)
                        n += 1
                return last

            def gates(i, u):
                pe.wait_ge(lo_got, i + 1)
                wait(pe, gate_got, i)
                split_products(gate_ps[:, :], u, lambda c: gate_hi[:, c, :],
                               lambda c: gate_lo[:, c, :]).then_inc(gate_put, 1)

            def body(j, u):
                i = 2 * j + u
                i1, u1 = i + 1, 1 - u
                for g in range(G):
                    wait(pe, odd_got if g % 2 else even_got, G // 2 * i + g // 2 - 1)
                    split_products(big_ps[g % 4][:, :, :], u, lambda c: w_hi[:, c, 2 * g:2 * g + 2, :],
                                   lambda c: w_lo[:, c, 2 * g:2 * g + 2, :]).then_inc(big_put, 1)
                    if at(i, TILES - 1):
                        continue
                    if g == 1:
                        attention_turned(i1)
                    elif g == 2:
                        output(i1)
                    elif g == 5:
                        hidden_turned(i1)
                    elif g == 6:
                        gates(i1, u1)

            pe.wait_ge(weights_in, 48)
            attention_turned(0)
            output(0)
            hidden_turned(0)
            pe.wait_ge(w_lo_got, C + 1)
            gates(0, 0)
            rounds(pe, body, TILES, 2)


def collect(nc, msg_rows, x1_rows, iota_row, msg_idx, weight, low_base, low_local, low_shift, out):
    with ExitStack() as ctx:
        def sb(name, shape, dt=F32):
            return ctx.enter_context(nc.sbuf_tensor(name, shape, dt))

        def sem(name):
            return ctx.enter_context(nc.semaphore(name))

        msg = [sb(f"msg_in{u}", [P, B, D]) for u in range(RING)]
        x1 = [sb(f"x1_in{u}", [P, D]) for u in range(RING)]
        index = [sb(f"index_c{u}", [P, B], I32) for u in range(RING)]
        hot = [sb(f"hot{u}", [P, B, P]) for u in range(RING)]
        onward = [sb(f"onward{u}", [P, P]) for u in range(RING)]
        sums = [sb(f"sums_c{u}", [P, D]) for u in range(RING)]
        result = [sb(f"result{u}", [P, D]) for u in range(RING)]
        sum_ps = [ctx.enter_context(nc.psum_tensor(f"sum_ps_c{u}", [P, D], F32)) for u in range(RING)]

        msg_here = [sem(f"msg_here{u}") for u in range(RING)]
        x1_in = [sem(f"x1_landed{u}") for u in range(RING)]
        index_in = [sem(f"index_in_c{u}") for u in range(RING)]
        out_done = [sem(f"out_done{u}") for u in range(RING)]
        hot_got, onward_got = sem("hot_got_c"), sem("onward_got")
        sum_done, sums_got, result_got = sem("sum_done"), sem("sums_got_c"), sem("result_got")
        block = ctx.enter_context(nc.Block())

        @block.sync
        def _(sp):
            def store(i, j, u):
                wait(sp, result_got, i + 1)
                sp.nop(nofuse=True)
                if not isinstance(i, int) or i > 0:
                    _, up, jp = step(j, u, -1)
                    wait(sp, out_done[up], 16 * (jp + 1))
                    sp.nop(nofuse=True)
                first = sp.value_load(low_base[0:1, bass.ds(i, 1)], min_val=0, max_val=N - P)
                sp.dma_start(out[bass.ds(first, P), :], result[u][:, :]).then_inc(out_done[u], 16)

            def body(j, u):
                i, _, _ = step(j, u)
                wait(sp, msg_here[u], 16 * B * j)
                sp.nop(nofuse=True)
                sp.dma_start(index[u][:, :], msg_idx[:, :, :].rearrange("p s b -> p (s b)")[:, bass.ds(i * B, B)]
                             ).then_inc(index_in[u], 16)
                wait(sp, result_got, i - 2)
                sp.nop(nofuse=True)
                first = sp.value_load(low_base[0:1, bass.ds(i, 1)], min_val=0, max_val=N - P)
                sp.dma_start(x1[u][:, :], x1_rows[bass.ds(first, P), :]).then_inc(x1_in[u], 16)
                if not isinstance(i, int) or i >= RING:
                    store(i - RING, j - 1, u)

            rounds(sp, body, BLOCKS, RING)
            for i in range(BLOCKS - RING, BLOCKS):
                store(i, i // RING, i % RING)
            for u in range(RING):
                sp.wait_ge(out_done[u], 16 * len(range(u, BLOCKS, RING)))

        @block.gpsimd
        def _(pool):
            def body(j, u):
                i, _, _ = step(j, u)
                wait(pool, sum_done, i - 2)
                pool.nop(nofuse=True)
                pool.wait_ge(index_in[u], 16 * (j + 1))
                pool.nop(nofuse=True)
                for t in range(B):
                    pool.indirect_dma_start(
                        out=msg[u][:, t, :], out_offset=None, in_=msg_rows,
                        in_offset=bass.IndirectOffsetOnAxis(ap=index[u][:, t:t + 1],
                                                            axis=0)).then_inc(msg_here[u], 16)

            rounds(pool, body, BLOCKS, RING)

        @block.vector
        def _(dve):
            local_flat = low_local[:, :, :].rearrange("p s b -> p (s b)")
            weight_flat = weight[:, :, :].rearrange("p s b -> p (s b)")

            def finish(i, j, u):
                wait(dve, sums_got, i + 1)
                wait(dve, x1_in[u], 16 * (j + 1))
                if not isinstance(j, int) or j > 0:
                    dve.wait_ge(out_done[u], 16 * j)
                nc.vector.scalar_tensor_tensor(result[u][:, :], sums[u][:, :], 0.0, x1[u][:, :], ALU.max,
                                               ALU.add).then_inc(result_got, 1)

            def body(j, u):
                i, _, _ = step(j, u)
                wait(dve, sum_done, i - 2)
                for t in range(B):
                    last = nc.vector.tensor_scalar(hot[u][:, t, :], iota_row[:, :],
                                                   local_flat[:, bass.ds(i * B + t, 1)],
                                                   weight_flat[:, bass.ds(i * B + t, 1)], ALU.is_equal, ALU.mult)
                last.then_inc(hot_got, 1)
                if not (isinstance(i, int) and i == 0):
                    ip, up, jp = step(j, u, -1)
                    nc.vector.tensor_scalar(onward[u][:, :], iota_row[:, :], low_shift[:, bass.ds(i, 1)], None,
                                            ALU.is_equal).then_inc(onward_got, 1)
                    finish(ip, jp, up)

            rounds(dve, body, BLOCKS, RING)
            finish(BLOCKS - 1, (BLOCKS - 1) // RING, (BLOCKS - 1) % RING)

        @block.scalar
        def _(act):
            def body(j, u):
                i, _, _ = step(j, u)
                act.wait_ge(sum_done, i + 1)
                wait(act, result_got, i - 2)
                nc.scalar.copy(sums[u][:, :], sum_ps[u][:, :]).then_inc(sums_got, 1)

            rounds(act, body, BLOCKS, RING)

        @block.tensor
        def _(pe):
            def body(j, u):
                i, _, _ = step(j, u)
                wait(pe, hot_got, i + 1)
                wait(pe, sums_got, i - 2)
                pe.wait_ge(msg_here[u], 16 * B * (j + 1))
                for t in range(B):
                    last = nc.tensor.matmul(sum_ps[u][:, :], hot[u][:, t, :], msg[u][:, t, :], start=t == 0,
                                            stop=t == B - 1 and isinstance(i, int) and i == 0)
                if not (isinstance(i, int) and i == 0):
                    wait(pe, onward_got, i)
                    wait(pe, sums_got, i)
                    last = nc.tensor.matmul(sum_ps[u][:, :], onward[u][:, :], sums[(u - 1) % RING][:, :], start=False,
                                            stop=True)
                last.then_inc(sum_done, 1)

            rounds(pe, body, BLOCKS, RING)


def group_tiles(sb, tag):
    return {"dst_all": sb("dst_all" + tag, [P, COLUMNS]),
            "ones": sb("ones" + tag, [P, P]), "before": sb("before_it" + tag, [P, P]),
            "spare": sb("spare" + tag, [P, 1]),
            "node": sb("node" + tag, [P, 1]), "diag": sb("diag" + tag, [P, P]),
            "same": sb("same" + tag, [P, P]),
            "real": sb("real" + tag, [P, 1]), "earlier": sb("earlier" + tag, [P, P]), "dup": sb("dup" + tag, [P, 1]),
            "leads": sb("leads" + tag, [P, 1]), "offset": sb("offset" + tag, [P, 1]),
            "row_idx": sb("row_idx" + tag, [P, 1], I32), "node_idx": sb("node_idx" + tag, [P, 1], I32),
            "slot": sb("slot" + tag, [P, 1], I32)}


def group_setup(nc, g, local, base, iota_row, iota_col, ready):
    nc.vector.tensor_tensor(g["dst_all"].rearrange("p (s b) -> p s b", b=B), local[:, :, :],
                            base[:, :].unsqueeze(2).broadcast_to([P, BLOCKS, B]), ALU.add).then_inc(ready, 1)
    nc.vector.memset(g["ones"][:, :], 1.0).then_inc(ready, 1)
    nc.vector.tensor_scalar(g["before"][:, :], iota_row[:, :], iota_col[:, 0:1], None, ALU.is_lt).then_inc(ready, 1)
    nc.vector.tensor_scalar(g["spare"][:, :], iota_col[:, 0:1], float(N), None, ALU.add).then_inc(ready, 1)


def group_column(nc, dve, k, g, grouped, written, put, put_before, puts, idx, ident, spread_ps):
    wait(dve, written, 16 * k)
    dve.nop(nofuse=True)
    nc.vector.tensor_copy(g["node"][:, :], g["dst_all"][:, bass.ds(k, 1)]).then_inc(grouped, 1)
    nc.vector.tensor_copy(g["row_idx"][:, :], idx.rearrange("p s b -> p (s b)")[:, bass.ds(k, 1)]
                          ).then_inc(grouped, 1)
    dve.wait_ge(grouped, GROUP_STEPS * k + 2)
    nc.vector.tensor_scalar(g["diag"][:, :], ident[:, :], g["node"][:, 0:1], None, ALU.mult
                            ).then_inc(grouped, 1)
    nc.vector.tensor_scalar(g["real"][:, :], g["node"][:, :], float(N), None, ALU.is_lt).then_inc(grouped, 1)
    dve.wait_ge(put, put_before + puts * k + 1)
    nc.vector.tensor_scalar(g["same"][:, :], spread_ps[:, :], g["node"][:, 0:1], None, ALU.is_equal
                            ).then_inc(grouped, 1)
    dve.wait_ge(grouped, GROUP_STEPS * k + 5)
    nc.vector.tensor_tensor(g["earlier"][:, :], g["same"][:, :], g["before"][:, :], ALU.mult
                            ).then_inc(grouped, 1)
    dve.wait_ge(grouped, GROUP_STEPS * k + 6)
    nc.vector.tensor_reduce(g["dup"][:, :], g["earlier"][:, :], AX.X, ALU.max).then_inc(grouped, 1)
    dve.wait_ge(grouped, GROUP_STEPS * k + 7)
    nc.vector.scalar_tensor_tensor(g["leads"][:, :], g["dup"][:, :], 0.5, g["real"][:, :], ALU.is_lt, ALU.mult
                                   ).then_inc(grouped, 1)
    dve.wait_ge(grouped, GROUP_STEPS * k + 8)
    nc.vector.scalar_tensor_tensor(g["offset"][:, :], g["node"][:, :], g["spare"][:, 0:1], g["leads"][:, :],
                                   ALU.subtract, ALU.mult).then_inc(grouped, 1)
    dve.wait_ge(grouped, GROUP_STEPS * k + 9)
    nc.vector.tensor_tensor(g["slot"][:, :], g["offset"][:, :], g["spare"][:, :], ALU.add).then_inc(grouped, 1)
    nc.vector.tensor_scalar(g["node_idx"][:, :], g["node"][:, :], float(N), None, ALU.min
                            ).then_inc(grouped, 1)


def columns(eng, body):
    body(0)
    with eng.Fori(1, COLUMNS) as k:
        body(k)


def fill(eng, rows, width, tile, done, fills):
    whole = (N + P) // P
    before = 16 * (whole + 1) * fills
    with eng.Fori(0, whole) as i:
        eng.dma_start(rows[bass.ds(i * P, P), :], tile[:, 0:width]).then_inc(done, 16)
    eng.wait_ge(done, before + 16 * whole)
    eng.dma_start(rows[N:N + P, :], tile[:, 0:width]).then_inc(done, 16)
    eng.wait_ge(done, before + 16 * (whole + 1))


def attend_any(nc, sems, q_rows, kv_rows, agg_rows, max_rows, irregular, ident, iota_row, iota_col, src_idx, local, base):
    with ExitStack() as ctx:
        def sb(name, shape, dt=F32):
            return ctx.enter_context(nc.sbuf_tensor(name, shape, dt))

        def sem(name):
            return sems[name]

        g = group_tiles(sb, "_a")
        kv = sb("kv_a", [P, 2 * D])
        q3 = sb("q3_a", [P, 3 * D], BF16)
        qf = sb("qf_a", [P, D])
        prod = sb("prod_a", [P, D])
        score = sb("score_a", [P, H])
        diag8 = sb("diag8_a", [P, H, P])
        apart = sb("apart_a", [P, P])
        masked = sb("masked_a", [P, H, P])
        group_max = sb("group_max_a", [P, H])
        old_max = sb("old_max_a", [P, H])
        new_max = sb("new_max_a", [P, H])
        args = sb("args_a", [P, 2, H])
        exps = sb("exps_a", [P, 2, H])
        acc = sb("acc_a", [P, AGG])
        vals = sb("vals_a", [P, AGG])
        blank = sb("blank_a", [P, AGG])
        lowest = sb("lowest_a", [P, H])
        spread_ps = ctx.enter_context(nc.psum_tensor("spread_ps_a", [P, P], F32))
        scores_ps = ctx.enter_context(nc.psum_tensor("scores_ps_a", [P, H, P], F32))
        sum_ps = ctx.enter_context(nc.psum_tensor("sum_ps_a", [P, AGG], F32))

        ready, filled, kv_in, q_in, max_in, acc_in = (sem("any_ready"), sem("any_filled"), sem("any_kv_in"),
                                                      sem("any_q_in"), sem("any_max_in"), sem("any_acc_in"))
        max_out, written = sem("any_max_out"), sem("any_written")
        grouped = sem("any_grouped")
        weighed = sem("any_weighed")
        put = sem("any_put")
        exps_got = sem("any_exps_got")
        block = ctx.enter_context(nc.Block())

        @block.gpsimd
        def _(pool):
            with pool.If(pool.value_load(irregular[0:1, 0:1], min_val=0, max_val=1) > 0):
                pool.wait_ge(ready, 6)
                fill(pool, agg_rows, AGG, blank, filled, 0)
                fill(pool, max_rows, H, lowest, filled, 1)

                def body(k):
                    pool.wait_ge(grouped, GROUP_STEPS * (k + 1))
                    pool.nop(nofuse=True)
                    for tile, rows, idx, landed in ((kv, kv_rows, g["row_idx"], kv_in), (q3, q_rows, g["node_idx"], q_in),
                                                    (old_max, max_rows, g["node_idx"], max_in),
                                                    (acc, agg_rows, g["slot"], acc_in)):
                        pool.indirect_dma_start(out=tile[:, :], out_offset=None, in_=rows,
                                                in_offset=bass.IndirectOffsetOnAxis(ap=idx[:, 0:1], axis=0)
                                                ).then_inc(landed, 16)
                    pool.wait_ge(weighed, WEIGH_STEPS * k + 15)
                    pool.nop(nofuse=True)
                    pool.indirect_dma_start(out=max_rows, out_offset=bass.IndirectOffsetOnAxis(ap=g["slot"][:, 0:1],
                                            axis=0), in_=new_max[:, :], in_offset=None).then_inc(max_out, 16)
                    pool.wait_ge(max_out, 16 * k + 16)
                    pool.nop(nofuse=True)
                    pool.indirect_dma_start(out=agg_rows, out_offset=bass.IndirectOffsetOnAxis(ap=g["slot"][:, 0:1],
                                            axis=0), in_=acc[:, :], in_offset=None).then_inc(written, 16)

                columns(pool, body)
                pool.wait_ge(written, 16 * COLUMNS)
            pool.nop(nofuse=True)

        @block.vector
        def _(dve):
            with dve.If(dve.value_load(irregular[0:1, 0:1], min_val=0, max_val=1) > 0):
                group_setup(nc, g, local, base, iota_row, iota_col, ready)
                nc.vector.memset(blank[:, :], 0.0).then_inc(ready, 1)
                nc.vector.memset(lowest[:, :], NEG).then_inc(ready, 1)
                dve.wait_ge(ready, 6)
                wide = [P, H, P]

                def body(k):
                    group_column(nc, dve, k, g, grouped, written, put, 0, 3, src_idx, ident, spread_ps)
                    dve.wait_ge(q_in, 16 * k + 16)
                    nc.vector.tensor_tensor(qf[:, :], q3[:, 0:D], q3[:, D:2 * D], ALU.add).then_inc(weighed, 1)
                    dve.wait_ge(weighed, WEIGH_STEPS * k + 1)
                    nc.vector.tensor_tensor(qf[:, :], qf[:, :], q3[:, 2 * D:3 * D], ALU.add).then_inc(weighed, 1)
                    dve.wait_ge(weighed, WEIGH_STEPS * k + 2)
                    dve.wait_ge(kv_in, 16 * k + 16)
                    nc.vector.tensor_tensor(prod[:, :], qf[:, :], kv[:, 0:D], ALU.mult).then_inc(weighed, 1)
                    dve.wait_ge(weighed, WEIGH_STEPS * k + 3)
                    nc.vector.tensor_reduce(score[:, :], prod[:, :].rearrange("p (d h) -> p h d", h=H), AX.X,
                                            ALU.add).then_inc(weighed, 1)
                    dve.wait_ge(weighed, WEIGH_STEPS * k + 4)
                    nc.vector.tensor_tensor(diag8[:, :, :], ident[:, :].unsqueeze(1).broadcast_to(wide),
                                            score[:, :].unsqueeze(2).broadcast_to(wide), ALU.mult
                                            ).then_inc(weighed, 1)
                    nc.vector.tensor_scalar(apart[:, :], g["same"][:, :], -1.0, -NEG, ALU.add, ALU.mult
                                            ).then_inc(weighed, 1)
                    dve.wait_ge(weighed, WEIGH_STEPS * k + 6)
                    dve.wait_ge(put, 3 * k + 2)
                    nc.vector.tensor_tensor(masked[:, :, :], scores_ps[:, :, :],
                                            apart[:, :].unsqueeze(1).broadcast_to(wide), ALU.add
                                            ).then_inc(weighed, 1)
                    dve.wait_ge(weighed, WEIGH_STEPS * k + 7)
                    nc.vector.tensor_reduce(group_max[:, :], masked[:, :, :], AX.X, ALU.max).then_inc(weighed, 1)
                    dve.wait_ge(weighed, WEIGH_STEPS * k + 8)
                    dve.wait_ge(max_in, 16 * k + 16)
                    nc.vector.tensor_tensor(new_max[:, :], group_max[:, :], old_max[:, :], ALU.max
                                            ).then_inc(weighed, 1)
                    dve.wait_ge(weighed, WEIGH_STEPS * k + 9)
                    nc.vector.tensor_tensor(args[:, 0, :], old_max[:, :], new_max[:, :], ALU.subtract
                                            ).then_inc(weighed, 1)
                    nc.vector.tensor_tensor(args[:, 1, :], score[:, :], new_max[:, :], ALU.subtract
                                            ).then_inc(weighed, 1)
                    dve.wait_ge(exps_got, k + 1)
                    nc.vector.tensor_tensor(vals[:, 0:D].rearrange("p (d h) -> p d h", h=H),
                                            kv[:, D:2 * D].rearrange("p (d h) -> p d h", h=H),
                                            exps[:, 1, :].unsqueeze(1).broadcast_to([P, HD, H]), ALU.mult
                                            ).then_inc(weighed, 1)
                    nc.vector.tensor_copy(vals[:, D:AGG], exps[:, 1, :]).then_inc(weighed, 1)
                    dve.wait_ge(acc_in, 16 * k + 16)
                    nc.vector.tensor_tensor(acc[:, :].rearrange("p (d h) -> p d h", h=H),
                                            acc[:, :].rearrange("p (d h) -> p d h", h=H),
                                            exps[:, 0, :].unsqueeze(1).broadcast_to([P, HD + 1, H]), ALU.mult
                                            ).then_inc(weighed, 1)
                    dve.wait_ge(weighed, WEIGH_STEPS * k + 14)
                    dve.wait_ge(put, 3 * k + 3)
                    nc.vector.tensor_tensor(acc[:, :], acc[:, :], sum_ps[:, :], ALU.add).then_inc(weighed, 1)

                columns(dve, body)
            dve.nop(nofuse=True)

        @block.scalar
        def _(act):
            with act.If(act.value_load(irregular[0:1, 0:1], min_val=0, max_val=1) > 0):
                def body(k):
                    act.wait_ge(weighed, WEIGH_STEPS * k + 11)
                    nc.scalar.activation(exps[:, :, :], args[:, :, :], ACT.Exp).then_inc(exps_got, 1)

                columns(act, body)
            act.nop(nofuse=True)

        @block.tensor
        def _(pe):
            with pe.If(pe.value_load(irregular[0:1, 0:1], min_val=0, max_val=1) > 0):
                pe.wait_ge(ready, 6)

                def body(k):
                    pe.wait_ge(grouped, GROUP_STEPS * k + 3)
                    nc.tensor.matmul(spread_ps[:, :], g["ones"][:, :], g["diag"][:, :], start=True, stop=True
                                     ).then_inc(put, 1)
                    pe.wait_ge(weighed, WEIGH_STEPS * k + 5)
                    for half in range(2):
                        heads = slice(half * H // 2, (half + 1) * H // 2)
                        last = nc.tensor.matmul(scores_ps[:, heads, :], g["ones"][:, :], diag8[:, heads, :],
                                                start=True, stop=True)
                    last.then_inc(put, 1)
                    pe.wait_ge(weighed, WEIGH_STEPS * k + 13)
                    nc.tensor.matmul(sum_ps[:, :], g["same"][:, :], vals[:, :], start=True, stop=True
                                     ).then_inc(put, 1)

                columns(pe, body)
            pe.nop(nofuse=True)


def collect_any(nc, sems, msg_rows, x1_rows, acc_rows, irregular, ident, iota_row, iota_col, msg_idx, weight, local, base,
                out):
    with ExitStack() as ctx:
        def sb(name, shape, dt=F32):
            return ctx.enter_context(nc.sbuf_tensor(name, shape, dt))

        def sem(name):
            return sems[name]

        g = group_tiles(sb, "_c")
        msg = sb("msg_c", [P, D])
        scaled = sb("scaled_c", [P, D])
        acc = sb("acc_c", [P, D])
        x1 = sb("x1_c", [P, D])
        result = sb("result_any", [P, D])
        blank = sb("blank_c", [P, D])
        spread_ps = ctx.enter_context(nc.psum_tensor("spread_ps_c", [P, P], F32))
        sum_ps = ctx.enter_context(nc.psum_tensor("sum_ps_any", [P, D], F32))

        ready, filled = sem("any_ready"), sem("any_filled")
        msg_in, acc_in, written = sem("any_msg_in"), sem("any_total_in"), sem("any_total_out")
        grouped = sem("any_grouped_c")
        added = sem("any_added")
        put = sem("any_put")
        put_before = 3 * COLUMNS
        block = ctx.enter_context(nc.Block())

        @block.gpsimd
        def _(pool):
            with pool.If(pool.value_load(irregular[0:1, 0:1], min_val=0, max_val=1) > 0):
                pool.wait_ge(ready, 6 + 5)
                fill(pool, acc_rows, D, blank, filled, 2)

                def body(k):
                    pool.wait_ge(grouped, GROUP_STEPS * (k + 1))
                    pool.nop(nofuse=True)
                    for tile, rows, idx, landed in ((msg, msg_rows, g["row_idx"], msg_in),
                                                    (acc, acc_rows, g["slot"], acc_in)):
                        pool.indirect_dma_start(out=tile[:, :], out_offset=None, in_=rows,
                                                in_offset=bass.IndirectOffsetOnAxis(ap=idx[:, 0:1], axis=0)
                                                ).then_inc(landed, 16)
                    pool.wait_ge(added, 2 * k + 2)
                    pool.nop(nofuse=True)
                    pool.indirect_dma_start(out=acc_rows, out_offset=bass.IndirectOffsetOnAxis(ap=g["slot"][:, 0:1],
                                            axis=0), in_=acc[:, :], in_offset=None).then_inc(written, 16)

                columns(pool, body)
                pool.wait_ge(written, 16 * COLUMNS)

                def finish(i):
                    wait(pool, written, 16 * (COLUMNS + i))
                    pool.nop(nofuse=True)
                    pool.dma_start(acc[:, :], acc_rows[bass.ds(row0(i), P), :]).then_inc(acc_in, 16)
                    pool.dma_start(x1[:, :], x1_rows[bass.ds(row0(i), P), :]).then_inc(msg_in, 16)
                    pool.wait_ge(added, 2 * COLUMNS + i + 1)
                    pool.nop(nofuse=True)
                    pool.dma_start(out[bass.ds(row0(i), P), :], result[:, :]).then_inc(written, 16)

                finish(0)
                with pool.Fori(1, TILES - 1) as i:
                    finish(i)
                finish(TILES - 1)
                pool.wait_ge(written, 16 * (COLUMNS + TILES))
            pool.nop(nofuse=True)

        @block.vector
        def _(dve):
            with dve.If(dve.value_load(irregular[0:1, 0:1], min_val=0, max_val=1) > 0):
                group_setup(nc, g, local, base, iota_row, iota_col, ready)
                nc.vector.memset(blank[:, :], 0.0).then_inc(ready, 1)
                dve.wait_ge(ready, 6 + 5)
                weight_flat = weight[:, :, :].rearrange("p s b -> p (s b)")

                def body(k):
                    group_column(nc, dve, k, g, grouped, written, put, put_before, 2, msg_idx, ident, spread_ps)
                    dve.wait_ge(msg_in, 16 * k + 16)
                    nc.vector.tensor_scalar(scaled[:, :], msg[:, :], weight_flat[:, bass.ds(k, 1)], None, ALU.mult
                                            ).then_inc(added, 1)
                    dve.wait_ge(acc_in, 16 * k + 16)
                    dve.wait_ge(put, put_before + 2 * k + 2)
                    nc.vector.tensor_tensor(acc[:, :], acc[:, :], sum_ps[:, :], ALU.add).then_inc(added, 1)

                columns(dve, body)

                def finish(i):
                    dve.wait_ge(acc_in, 16 * (COLUMNS + i + 1))
                    dve.wait_ge(msg_in, 16 * (COLUMNS + i + 1))
                    nc.vector.scalar_tensor_tensor(result[:, :], acc[:, :], 0.0, x1[:, :], ALU.max, ALU.add
                                                   ).then_inc(added, 1)

                with dve.Fori(0, TILES) as i:
                    finish(i)
            dve.nop(nofuse=True)

        @block.tensor
        def _(pe):
            with pe.If(pe.value_load(irregular[0:1, 0:1], min_val=0, max_val=1) > 0):
                pe.wait_ge(ready, 6 + 5)

                def body(k):
                    pe.wait_ge(grouped, GROUP_STEPS * k + 3)
                    nc.tensor.matmul(spread_ps[:, :], g["ones"][:, :], g["diag"][:, :], start=True, stop=True
                                     ).then_inc(put, 1)
                    pe.wait_ge(added, 2 * k + 1)
                    nc.tensor.matmul(sum_ps[:, :], g["same"][:, :], scaled[:, :], start=True, stop=True
                                     ).then_inc(put, 1)

                columns(pe, body)
            pe.nop(nofuse=True)


def kernel(**inputs):
    import numpy as np
    import concourse.bacc as bacc
    from concourse.bass_utils import run_bass_kernel_spmd as run

    arrays = {name: np.ascontiguousarray(a) for name, a in inputs.items()}
    arrays["edge_weight1"] = arrays["edge_weight1"].reshape(E)
    arrays["L1_gnn_gate_weight"] = np.ascontiguousarray(arrays["L1_gnn_gate_weight"].reshape(R, D).T)
    names = ["x", "src", "dst", "edge_type_16", "edge_weight1", "L0_gnn_Wq", "L0_gnn_bq", "L0_gnn_Wk", "L0_gnn_bk",
             "L0_gnn_Wv", "L0_gnn_bv", "L0_gnn_Wo", "L0_gnn_bo", "L1_gnn_weight", "L1_gnn_gate_weight"]
    nc = bacc.Bacc("TRN2", target_bir_lowering=False, num_devices=1)
    args = [nc.dram_tensor("in_" + name, arrays[name].shape, mybir.dt.from_np(arrays[name].dtype),
                           kind="ExternalInput").ap() for name in names]
    out = nc.dram_tensor("out_rows", [N, D], F32, kind="ExternalOutput").ap()
    build(nc, *args, out)
    result = run(nc, [{"in_" + name: arrays[name] for name in names}], core_ids=[0])
    return result.results[0]["out_rows"]
```
